# Optimizing a Trainium2 kernel written in Bass

```python
import numpy as np
import jax
import jax.numpy as jnp

def _softmax(x, axis=-1):
    return jax.nn.softmax(x, axis=axis)

def _gelu(x):
    return jax.nn.gelu(x, approximate=True)

def _silu(x):
    return jax.nn.silu(x)

def _sigmoid(x):
    return jax.nn.sigmoid(x)

def _layernorm(x, axis=-1, eps=1e-05):
    m = jnp.mean(x, axis=axis, keepdims=True)
    v = jnp.var(x, axis=axis, keepdims=True)
    return (x - m) / jnp.sqrt(v + eps)

def _scatter_add(tgt, idx, src, axis=0):
    return tgt.at[idx].add(src)

def _segment_sum(src, seg, n):
    return jax.ops.segment_sum(src, seg, n)
kernel_name = 'mk_gps_d2_gnn_r32_f1e17f'

def setup_inputs(seed: int=0):
    np.random.seed(seed)
    _w = jnp.asarray

    def _rec_inputs():
        import jax
        import jax.numpy as jnp
        _gk = jax.random.key(seed)
        x = -8.776e-05 + 1 * jax.random.normal(jax.random.fold_in(_gk, 1), (625, 256), jnp.float32)
        _s = jax.random.randint(jax.random.fold_in(_gk, 2), (5000,), 0, 625, jnp.int32)
        _d = jax.random.randint(jax.random.fold_in(_gk, 3), (5000,), 0, 625, jnp.int32)
        _loop = jnp.arange(625, dtype=jnp.int32)
        src = jnp.concatenate([_s, _d, _loop])
        dst = jnp.concatenate([_d, _s, _loop])
        _o = jnp.argsort(dst, stable=True)
        src = src[_o]
        dst = dst[_o]
        return (x, src, dst)
    x, src, dst = _rec_inputs()

    def _L0_gnn_setup():
        import jax, jax.numpy as jnp
        import numpy as np
        N = 625
        E = 20000
        D = 256
        H = 4
        Dh = 64
        L = 3
        BN_EPS = 1e-05

        def _transformer_conv(x, src, dst, Wq, bq, Wk, bk, Wv, bv, Ws, bs):
            q = (x @ Wq + bq).reshape(N, H, Dh)
            k = (x @ Wk + bk).reshape(N, H, Dh)
            v = (x @ Wv + bv).reshape(N, H, Dh)
            qd = q[dst]
            ks_ = k[src]
            score = jnp.einsum('ehd,ehd->eh', qd, ks_) / np.sqrt(Dh)
            m = jax.ops.segment_max(score, dst, num_segments=N)
            ex = jnp.exp(score - m[dst])
            denom = jax.ops.segment_sum(ex, dst, num_segments=N)
            alpha = ex / denom[dst]
            msg = alpha[:, :, None] * v[src]
            out = jax.ops.segment_sum(msg, dst, num_segments=N)
            out = out.reshape(N, H * Dh)
            return out + x @ Ws + bs

        def _batch_norm(x, gamma, beta):
            mean = jnp.mean(x, axis=0)
            var = jnp.var(x, axis=0)
            return gamma * (x - mean) * jax.lax.rsqrt(var + BN_EPS) + beta
        key = jax.random.key(seed)
        ks = jax.random.split(key, 14)
        s = 1.0 / np.sqrt(D)
        f32 = jnp.float32
        return {'x': jax.random.normal(ks[0], (N, D), f32), 'edge_index': jax.random.randint(ks[1], (2, E), 0, N, dtype=jnp.int32), 'Wq': jax.random.normal(ks[2], (L, D, D), f32) * s, 'bq': jax.random.normal(ks[3], (L, D), f32) * 0.02, 'Wk': jax.random.normal(ks[4], (L, D, D), f32) * s, 'bk': jax.random.normal(ks[5], (L, D), f32) * 0.02, 'Wv': jax.random.normal(ks[6], (L, D, D), f32) * s, 'bv': jax.random.normal(ks[7], (L, D), f32) * 0.02, 'Ws': jax.random.normal(ks[8], (L, D, D), f32) * s, 'bs': jax.random.normal(ks[9], (L, D), f32) * 0.02, 'bn_gamma': 1.0 + 0.1 * jax.random.normal(ks[10], (L - 1, D), f32), 'bn_beta': 0.1 * jax.random.normal(ks[11], (L - 1, D), f32)}
    _L0_gnn_all = _L0_gnn_setup()
    _L0_gnn_in = {k: v for k, v in _L0_gnn_all.items() if k in ('Wq', 'bq', 'Wk', 'bk', 'Wv', 'bv', 'Ws', 'bs', 'bn_gamma', 'bn_beta')}
    del _L0_gnn_all

    def _L0_mix_setup():
        import jax, jax.numpy as jnp
        import numpy as np
        N, F, C, H = (32, 128, 256, 8)
        D = C // H
        EPS_ATTN = 1e-06
        EPS_LN = 1e-05

        def layer_norm(x, g, b):
            mu = jnp.mean(x, axis=-1, keepdims=True)
            var = jnp.var(x, axis=-1, keepdims=True)
            return (x - mu) * jax.lax.rsqrt(var + EPS_LN) * g + b
        key = jax.random.key(seed)
        ks = jax.random.split(key, 8)
        s = 1.0 / np.sqrt(C)
        return {'x': jax.random.normal(ks[0], (N, F, C), jnp.float32), 'Wqkv': jax.random.uniform(ks[1], (3 * C, C), jnp.float32, -s, s), 'ln1_g': jnp.ones((C,), jnp.float32), 'ln1_b': jnp.zeros((C,), jnp.float32), 'W1': jax.random.uniform(ks[2], (C, C), jnp.float32, -s, s), 'b1': jax.random.uniform(ks[3], (C,), jnp.float32, -s, s), 'W2': jax.random.uniform(ks[4], (C, C), jnp.float32, -s, s), 'b2': jax.random.uniform(ks[5], (C,), jnp.float32, -s, s), 'ln2_g': jnp.ones((C,), jnp.float32), 'ln2_b': jnp.zeros((C,), jnp.float32)}
    _L0_mix_all = _L0_mix_setup()
    _L0_mix_in = {k: v for k, v in _L0_mix_all.items() if k in ('Wqkv', 'ln1_g', 'ln1_b', 'W1', 'b1', 'W2', 'b2', 'ln2_g', 'ln2_b')}
    del _L0_mix_all

    def _L0_ffn_setup():
        import jax, jax.numpy as jnp
        import numpy as np
        B, S, H, F, E, K = (8, 128, 256, 512, 16, 2)
        EPS = 1e-05
        key = jax.random.key(seed)
        ks = jax.random.split(key, 9)
        sc = 0.02
        return {'x': jax.random.normal(ks[0], (B, S, H), dtype=jnp.float32), 'gate_w': jax.random.normal(ks[1], (H, E), dtype=jnp.float32) * sc, 'gate_b': jnp.zeros((E,), dtype=jnp.float32), 'w1': jax.random.normal(ks[2], (E, H, F), dtype=jnp.float32) * sc, 'b1': jnp.zeros((E, F), dtype=jnp.float32), 'w2': jax.random.normal(ks[3], (E, F, H), dtype=jnp.float32) * sc, 'b2': jnp.zeros((E, H), dtype=jnp.float32), 'gamma': jnp.ones((H,), dtype=jnp.float32), 'beta': jnp.zeros((H,), dtype=jnp.float32)}
    _L0_ffn_all = _L0_ffn_setup()
    _L0_ffn_in = {k: v for k, v in _L0_ffn_all.items() if k in ('gate_w', 'gate_b', 'w1', 'b1', 'w2', 'b2', 'gamma', 'beta')}
    del _L0_ffn_all

    def _L1_gnn_setup():
        import jax, jax.numpy as jnp
        import numpy as np
        N = 50000
        E = 50000
        D = 256
        H = 256
        EPS = 1e-05

        def _gnn_layer(x, row, col, W, b, g, beta):
            n = x.shape[0]
            neigh = x[col]
            agg = jax.ops.segment_sum(neigh, row, num_segments=n)
            deg = jax.ops.segment_sum(jnp.ones((row.shape[0],), x.dtype), row, num_segments=n)
            deg = jnp.maximum(deg, 1.0)[:, None]
            h = (x + agg / deg) @ W.T + b
            mu = jnp.mean(h, axis=-1, keepdims=True)
            var = jnp.mean(jnp.square(h - mu), axis=-1, keepdims=True)
            hn = (h - mu) * jax.lax.rsqrt(var + EPS) * g + beta
            return jax.nn.silu(hn)
        key = jax.random.key(seed)
        ks = jax.random.split(key, 12)
        x = jax.random.normal(ks[0], (N, D), dtype=jnp.float32)
        edge_index = jax.random.randint(ks[1], (2, E), 0, N, dtype=jnp.int32)
        s0 = 1.0 / np.sqrt(D)
        s1 = 1.0 / np.sqrt(H)
        W0 = jax.random.uniform(ks[2], (H, D), jnp.float32, -s0, s0)
        b0 = jax.random.uniform(ks[3], (H,), jnp.float32, -s0, s0)
        g0 = jnp.ones((H,), jnp.float32)
        beta0 = jnp.zeros((H,), jnp.float32)
        W1 = jax.random.uniform(ks[4], (H, H), jnp.float32, -s1, s1)
        b1 = jax.random.uniform(ks[5], (H,), jnp.float32, -s1, s1)
        g1 = jnp.ones((H,), jnp.float32)
        beta1 = jnp.zeros((H,), jnp.float32)
        return {'x': x, 'edge_index': edge_index, 'W0': W0, 'b0': b0, 'g0': g0, 'beta0': beta0, 'W1': W1, 'b1': b1, 'g1': g1, 'beta1': beta1}
    _L1_gnn_all = _L1_gnn_setup()
    _L1_gnn_in = {k: v for k, v in _L1_gnn_all.items() if k in ('W0', 'b0', 'g0', 'beta0', 'W1', 'b1', 'g1', 'beta1')}
    del _L1_gnn_all

    def _L1_mix_setup():
        import jax, jax.numpy as jnp
        import numpy as np
        DIM = 256
        HEADS = 4
        HEAD_DIM = DIM // HEADS
        MLP_HIDDEN = DIM * 3
        B, N = (8, 128)
        EPS = 1e-05

        def _layernorm(x, g, b):
            mu = jnp.mean(x, axis=-1, keepdims=True)
            var = jnp.mean(jnp.square(x - mu), axis=-1, keepdims=True)
            return (x - mu) * jax.lax.rsqrt(var + EPS) * g + b
        key = jax.random.key(seed)
        ks = jax.random.split(key, 8)
        s = 0.02
        return {'x': jax.random.normal(ks[0], (B, N, DIM), dtype=jnp.float32), 'w_qkv': jax.random.normal(ks[1], (DIM, 3 * DIM), dtype=jnp.float32) * s, 'b_qkv': jnp.zeros((3 * DIM,), dtype=jnp.float32), 'norm_g': jnp.ones((DIM,), dtype=jnp.float32), 'norm_b': jnp.zeros((DIM,), dtype=jnp.float32), 'w_fc1': jax.random.normal(ks[2], (DIM, MLP_HIDDEN), dtype=jnp.float32) * s, 'b_fc1': jnp.zeros((MLP_HIDDEN,), dtype=jnp.float32), 'w_fc2': jax.random.normal(ks[3], (MLP_HIDDEN, DIM), dtype=jnp.float32) * s, 'b_fc2': jnp.zeros((DIM,), dtype=jnp.float32)}
    _L1_mix_all = _L1_mix_setup()
    _L1_mix_in = {k: v for k, v in _L1_mix_all.items() if k in ('w_qkv', 'b_qkv', 'norm_g', 'norm_b', 'w_fc1', 'b_fc1', 'w_fc2', 'b_fc2')}
    del _L1_mix_all

    def _L1_ffn_setup():
        import jax, jax.numpy as jnp
        import numpy as np
        BN_EPS = 0.001

        def _bn(h, g, b, m, v):
            return g * (h - m) * jax.lax.rsqrt(v + BN_EPS) + b
        key = jax.random.key(seed)
        ks = jax.random.split(key, 8)
        B, F, Df = (256, 64, 256)
        E, H, D = (8, 256, 256)
        s1 = 1.0 / np.sqrt(Df)
        s2 = 1.0 / np.sqrt(H)
        return {'x': jax.random.normal(ks[0], (B, F, Df), jnp.float32), 'Wr': jax.random.normal(ks[1], (Df, E), jnp.float32) * s1, 'br': jnp.zeros((E,), jnp.float32), 'W1': jax.random.normal(ks[2], (E, Df, H), jnp.float32) * s1, 'b1': jnp.zeros((E, H), jnp.float32), 'g1': jnp.ones((E, H), jnp.float32), 'be1': jnp.zeros((E, H), jnp.float32), 'm1': jnp.zeros((E, H), jnp.float32), 'v1': jnp.ones((E, H), jnp.float32), 'W2': jax.random.normal(ks[3], (E, H, H), jnp.float32) * s2, 'b2': jnp.zeros((E, H), jnp.float32), 'g2': jnp.ones((E, H), jnp.float32), 'be2': jnp.zeros((E, H), jnp.float32), 'm2': jnp.zeros((E, H), jnp.float32), 'v2': jnp.ones((E, H), jnp.float32), 'Wo': jax.random.normal(ks[4], (E, H, D), jnp.float32) * s2, 'bo': jnp.zeros((E, D), jnp.float32)}
    _L1_ffn_all = _L1_ffn_setup()
    _L1_ffn_in = {k: v for k, v in _L1_ffn_all.items() if k in ('Wr', 'br', 'W1', 'b1', 'g1', 'be1', 'm1', 'v1', 'W2', 'b2', 'g2', 'be2', 'm2', 'v2', 'Wo', 'bo')}
    del _L1_ffn_all
    return {'x': x, 'src': src, 'dst': dst, 'L0_gnn_Wq': _L0_gnn_in['Wq'], 'L0_gnn_bq': _L0_gnn_in['bq'], 'L0_gnn_Wk': _L0_gnn_in['Wk'], 'L0_gnn_bk': _L0_gnn_in['bk'], 'L0_gnn_Wv': _L0_gnn_in['Wv'], 'L0_gnn_bv': _L0_gnn_in['bv'], 'L0_gnn_Ws': _L0_gnn_in['Ws'], 'L0_gnn_bs': _L0_gnn_in['bs'], 'L0_gnn_bn_gamma': _L0_gnn_in['bn_gamma'], 'L0_gnn_bn_beta': _L0_gnn_in['bn_beta'], 'L0_mix_Wqkv': _L0_mix_in['Wqkv'], 'L0_mix_ln1_g': _L0_mix_in['ln1_g'], 'L0_mix_ln1_b': _L0_mix_in['ln1_b'], 'L0_mix_W1': _L0_mix_in['W1'], 'L0_mix_b1': _L0_mix_in['b1'], 'L0_mix_W2': _L0_mix_in['W2'], 'L0_mix_b2': _L0_mix_in['b2'], 'L0_mix_ln2_g': _L0_mix_in['ln2_g'], 'L0_mix_ln2_b': _L0_mix_in['ln2_b'], 'L0_ffn_gate_w': _L0_ffn_in['gate_w'], 'L0_ffn_gate_b': _L0_ffn_in['gate_b'], 'L0_ffn_w1': _L0_ffn_in['w1'], 'L0_ffn_b1': _L0_ffn_in['b1'], 'L0_ffn_w2': _L0_ffn_in['w2'], 'L0_ffn_b2': _L0_ffn_in['b2'], 'L0_ffn_gamma': _L0_ffn_in['gamma'], 'L0_ffn_beta': _L0_ffn_in['beta'], 'L1_gnn_W0': _L1_gnn_in['W0'], 'L1_gnn_b0': _L1_gnn_in['b0'], 'L1_gnn_g0': _L1_gnn_in['g0'], 'L1_gnn_beta0': _L1_gnn_in['beta0'], 'L1_gnn_W1': _L1_gnn_in['W1'], 'L1_gnn_b1': _L1_gnn_in['b1'], 'L1_gnn_g1': _L1_gnn_in['g1'], 'L1_gnn_beta1': _L1_gnn_in['beta1'], 'L1_mix_w_qkv': _L1_mix_in['w_qkv'], 'L1_mix_b_qkv': _L1_mix_in['b_qkv'], 'L1_mix_norm_g': _L1_mix_in['norm_g'], 'L1_mix_norm_b': _L1_mix_in['norm_b'], 'L1_mix_w_fc1': _L1_mix_in['w_fc1'], 'L1_mix_b_fc1': _L1_mix_in['b_fc1'], 'L1_mix_w_fc2': _L1_mix_in['w_fc2'], 'L1_mix_b_fc2': _L1_mix_in['b_fc2'], 'L1_ffn_Wr': _L1_ffn_in['Wr'], 'L1_ffn_br': _L1_ffn_in['br'], 'L1_ffn_W1': _L1_ffn_in['W1'], 'L1_ffn_b1': _L1_ffn_in['b1'], 'L1_ffn_g1': _L1_ffn_in['g1'], 'L1_ffn_be1': _L1_ffn_in['be1'], 'L1_ffn_m1': _L1_ffn_in['m1'], 'L1_ffn_v1': _L1_ffn_in['v1'], 'L1_ffn_W2': _L1_ffn_in['W2'], 'L1_ffn_b2': _L1_ffn_in['b2'], 'L1_ffn_g2': _L1_ffn_in['g2'], 'L1_ffn_be2': _L1_ffn_in['be2'], 'L1_ffn_m2': _L1_ffn_in['m2'], 'L1_ffn_v2': _L1_ffn_in['v2'], 'L1_ffn_Wo': _L1_ffn_in['Wo'], 'L1_ffn_bo': _L1_ffn_in['bo']}

def reference(x, src, dst, L0_gnn_Wq, L0_gnn_bq, L0_gnn_Wk, L0_gnn_bk, L0_gnn_Wv, L0_gnn_bv, L0_gnn_Ws, L0_gnn_bs, L0_gnn_bn_gamma, L0_gnn_bn_beta, L0_mix_Wqkv, L0_mix_ln1_g, L0_mix_ln1_b, L0_mix_W1, L0_mix_b1, L0_mix_W2, L0_mix_b2, L0_mix_ln2_g, L0_mix_ln2_b, L0_ffn_gate_w, L0_ffn_gate_b, L0_ffn_w1, L0_ffn_b1, L0_ffn_w2, L0_ffn_b2, L0_ffn_gamma, L0_ffn_beta, L1_gnn_W0, L1_gnn_b0, L1_gnn_g0, L1_gnn_beta0, L1_gnn_W1, L1_gnn_b1, L1_gnn_g1, L1_gnn_beta1, L1_mix_w_qkv, L1_mix_b_qkv, L1_mix_norm_g, L1_mix_norm_b, L1_mix_w_fc1, L1_mix_b_fc1, L1_mix_w_fc2, L1_mix_b_fc2, L1_ffn_Wr, L1_ffn_br, L1_ffn_W1, L1_ffn_b1, L1_ffn_g1, L1_ffn_be1, L1_ffn_m1, L1_ffn_v1, L1_ffn_W2, L1_ffn_b2, L1_ffn_g2, L1_ffn_be2, L1_ffn_m2, L1_ffn_v2, L1_ffn_Wo, L1_ffn_bo):
    import jax
    import jax.numpy as jnp

    def _L0_gnn_ref(x, edge_index, Wq, bq, Wk, bk, Wv, bv, Ws, bs, bn_gamma, bn_beta):
        import jax, jax.numpy as jnp
        import numpy as np
        N = 625
        E = 20000
        D = 256
        H = 4
        Dh = 64
        L = 3
        BN_EPS = 1e-05

        def _transformer_conv(x, src, dst, Wq, bq, Wk, bk, Wv, bv, Ws, bs):
            q = (x @ Wq + bq).reshape(N, H, Dh)
            k = (x @ Wk + bk).reshape(N, H, Dh)
            v = (x @ Wv + bv).reshape(N, H, Dh)
            qd = q[dst]
            ks_ = k[src]
            score = jnp.einsum('ehd,ehd->eh', qd, ks_) / np.sqrt(Dh)
            m = jax.ops.segment_max(score, dst, num_segments=N)
            ex = jnp.exp(score - m[dst])
            denom = jax.ops.segment_sum(ex, dst, num_segments=N)
            alpha = ex / denom[dst]
            msg = alpha[:, :, None] * v[src]
            out = jax.ops.segment_sum(msg, dst, num_segments=N)
            out = out.reshape(N, H * Dh)
            return out + x @ Ws + bs

        def _batch_norm(x, gamma, beta):
            mean = jnp.mean(x, axis=0)
            var = jnp.var(x, axis=0)
            return gamma * (x - mean) * jax.lax.rsqrt(var + BN_EPS) + beta
        src, dst = (edge_index[0], edge_index[1])
        for i in range(L):
            x = _transformer_conv(x, src, dst, Wq[i], bq[i], Wk[i], bk[i], Wv[i], bv[i], Ws[i], bs[i])
            if i < L - 1:
                x = jax.nn.relu(_batch_norm(x, bn_gamma[i], bn_beta[i]))
        return x

    def _L0_mix_ref(x, Wqkv, ln1_g, ln1_b, W1, b1, W2, b2, ln2_g, ln2_b):
        import jax, jax.numpy as jnp
        import numpy as np
        N, F, C, H = (32, 128, 256, 8)
        D = C // H
        EPS_ATTN = 1e-06
        EPS_LN = 1e-05

        def layer_norm(x, g, b):
            mu = jnp.mean(x, axis=-1, keepdims=True)
            var = jnp.var(x, axis=-1, keepdims=True)
            return (x - mu) * jax.lax.rsqrt(var + EPS_LN) * g + b
        n, f, c = x.shape
        qkv = jnp.einsum('nfc,oc->nfo', x, Wqkv)
        q, k, v = jnp.split(qkv, 3, axis=-1)
        q = q.reshape(n, f, H, D)
        k = k.reshape(n, f, H, D)
        v = v.reshape(n, f, H, D)
        q = jax.nn.elu(q) + 1.0
        k = jax.nn.elu(k) + 1.0
        kv = jnp.einsum('nshd,nshm->nhmd', k, v)
        ksum = jnp.sum(k, axis=1)
        z = 1.0 / (jnp.einsum('nlhd,nhd->nlh', q, ksum) + EPS_ATTN)
        t = jnp.einsum('nlhd,nhmd,nlh->nlhm', q, kv, z)
        t = t.reshape(n, f, c)
        x1 = layer_norm(t + x, ln1_g, ln1_b)
        h = jax.nn.gelu(jnp.einsum('nfc,oc->nfo', x1, W1) + b1, approximate=False)
        y = jnp.einsum('nfc,oc->nfo', h, W2) + b2
        return layer_norm(y + x1, ln2_g, ln2_b)

    def _L0_ffn_ref(x, gate_w, gate_b, w1, b1, w2, b2, gamma, beta):
        import jax, jax.numpy as jnp
        import numpy as np
        B, S, H, F, E, K = (8, 128, 256, 512, 16, 2)
        EPS = 1e-05
        gate_logits = x @ gate_w + gate_b
        topk_vals, topk_idx = jax.lax.top_k(gate_logits, K)
        topk_w = jax.nn.softmax(topk_vals, axis=-1)
        h = jax.nn.relu(jnp.einsum('bsh,ehf->bsef', x, w1) + b1)
        expert_out = jnp.einsum('bsef,efh->bseh', h, w2) + b2
        sel = jnp.take_along_axis(expert_out, topk_idx[:, :, :, None], axis=2)
        moe = jnp.sum(topk_w[..., None] * sel, axis=2)
        y = x + moe
        mu = jnp.mean(y, axis=-1, keepdims=True)
        var = jnp.var(y, axis=-1, keepdims=True)
        return (y - mu) / jnp.sqrt(var + EPS) * gamma + beta

    def _L1_gnn_ref(x, edge_index, W0, b0, g0, beta0, W1, b1, g1, beta1):
        import jax, jax.numpy as jnp
        import numpy as np
        N = 50000
        E = 50000
        D = 256
        H = 256
        EPS = 1e-05

        def _gnn_layer(x, row, col, W, b, g, beta):
            n = x.shape[0]
            neigh = x[col]
            agg = jax.ops.segment_sum(neigh, row, num_segments=n)
            deg = jax.ops.segment_sum(jnp.ones((row.shape[0],), x.dtype), row, num_segments=n)
            deg = jnp.maximum(deg, 1.0)[:, None]
            h = (x + agg / deg) @ W.T + b
            mu = jnp.mean(h, axis=-1, keepdims=True)
            var = jnp.mean(jnp.square(h - mu), axis=-1, keepdims=True)
            hn = (h - mu) * jax.lax.rsqrt(var + EPS) * g + beta
            return jax.nn.silu(hn)
        row, col = (edge_index[0], edge_index[1])
        x = _gnn_layer(x, row, col, W0, b0, g0, beta0)
        x = _gnn_layer(x, row, col, W1, b1, g1, beta1)
        return x

    def _L1_mix_ref(x, w_qkv, b_qkv, norm_g, norm_b, w_fc1, b_fc1, w_fc2, b_fc2):
        import jax, jax.numpy as jnp
        import numpy as np
        DIM = 256
        HEADS = 4
        HEAD_DIM = DIM // HEADS
        MLP_HIDDEN = DIM * 3
        B, N = (8, 128)
        EPS = 1e-05

        def _layernorm(x, g, b):
            mu = jnp.mean(x, axis=-1, keepdims=True)
            var = jnp.mean(jnp.square(x - mu), axis=-1, keepdims=True)
            return (x - mu) * jax.lax.rsqrt(var + EPS) * g + b
        Bx, Nx, C = x.shape
        scale = HEAD_DIM ** (-0.5)
        qkv = (x @ w_qkv + b_qkv).reshape(Bx, Nx, 3, HEADS, HEAD_DIM)
        qkv = jnp.transpose(qkv, (2, 0, 3, 1, 4))
        q, k, v = (qkv[0], qkv[1], qkv[2])
        k = k * scale
        attn = jnp.einsum('bhnd,bhne->bhde', k, v)
        attn = jax.nn.softmax(attn, axis=-1)
        xf = jnp.einsum('bhde,bhne->bhnd', attn, q)
        xf = jnp.transpose(xf, (0, 2, 1, 3)).reshape(Bx, Nx, C)
        x = x + xf
        h = _layernorm(x, norm_g, norm_b)
        h = jax.nn.gelu(h @ w_fc1 + b_fc1, approximate=False) @ w_fc2 + b_fc2
        return x + h

    def _L1_ffn_ref(x, Wr, br, W1, b1, g1, be1, m1, v1, W2, b2, g2, be2, m2, v2, Wo, bo):
        import jax, jax.numpy as jnp
        import numpy as np
        BN_EPS = 0.001

        def _bn(h, g, b, m, v):
            return g * (h - m) * jax.lax.rsqrt(v + BN_EPS) + b
        feat = jnp.mean(x, axis=0)
        w = jax.nn.softmax(feat @ Wr + br, axis=-1)
        h = jnp.einsum('bfd,edh->bfeh', x, W1) + b1
        h = jax.nn.relu(_bn(h, g1, be1, m1, v1))
        h = jnp.einsum('bfeh,ehk->bfek', h, W2) + b2
        h = jax.nn.relu(_bn(h, g2, be2, m2, v2))
        y = jnp.einsum('bfeh,ehd->bfed', h, Wo) + bo
        return jnp.einsum('bfed,fe->bfd', y, w)
    edge_index = jnp.stack([src, dst])
    xn = _layernorm(x, axis=-1)
    x = x + _L0_gnn_ref(xn, edge_index, L0_gnn_Wq, L0_gnn_bq, L0_gnn_Wk, L0_gnn_bk, L0_gnn_Wv, L0_gnn_bv, L0_gnn_Ws, L0_gnn_bs, L0_gnn_bn_gamma, L0_gnn_bn_beta) + _L0_mix_ref(xn[None], L0_mix_Wqkv, L0_mix_ln1_g, L0_mix_ln1_b, L0_mix_W1, L0_mix_b1, L0_mix_W2, L0_mix_b2, L0_mix_ln2_g, L0_mix_ln2_b)[0]
    x = x + _L0_ffn_ref(_layernorm(x, axis=-1)[None], L0_ffn_gate_w, L0_ffn_gate_b, L0_ffn_w1, L0_ffn_b1, L0_ffn_w2, L0_ffn_b2, L0_ffn_gamma, L0_ffn_beta)[0]
    xn = _layernorm(x, axis=-1)
    x = x + _L1_gnn_ref(xn, edge_index, L1_gnn_W0, L1_gnn_b0, L1_gnn_g0, L1_gnn_beta0, L1_gnn_W1, L1_gnn_b1, L1_gnn_g1, L1_gnn_beta1) + _L1_mix_ref(xn[None], L1_mix_w_qkv, L1_mix_b_qkv, L1_mix_norm_g, L1_mix_norm_b, L1_mix_w_fc1, L1_mix_b_fc1, L1_mix_w_fc2, L1_mix_b_fc2)[0]
    x = x + _L1_ffn_ref(_layernorm(x, axis=-1)[None], L1_ffn_Wr, L1_ffn_br, L1_ffn_W1, L1_ffn_b1, L1_ffn_g1, L1_ffn_be1, L1_ffn_m1, L1_ffn_v1, L1_ffn_W2, L1_ffn_b2, L1_ffn_g2, L1_ffn_be2, L1_ffn_m2, L1_ffn_v2, L1_ffn_Wo, L1_ffn_bo)[0]
    return x

_drawn_inputs = setup_inputs


def setup_inputs(seed=0):
    import zlib

    import numpy as np

    out = dict(_drawn_inputs(seed))
    spreads = {'L0_mix_ln1_g': (1.0, 0.2),
     'L0_mix_ln1_b': (0.0, 0.1),
     'L0_mix_ln2_g': (1.0, 0.2),
     'L0_mix_ln2_b': (0.0, 0.1),
     'L0_ffn_gate_b': (0.0, 0.358),
     'L0_ffn_b1': (0.0, 0.8),
     'L0_ffn_b2': (0.0, 0.349),
     'L0_ffn_gamma': (1.0, 0.2),
     'L0_ffn_beta': (0.0, 0.1),
     'L1_gnn_g0': (1.0, 0.2),
     'L1_gnn_beta0': (0.0, 0.472),
     'L1_gnn_g1': (1.0, 0.2),
     'L1_gnn_beta1': (0.0, 0.524),
     'L1_mix_b_qkv': (0.0, 0.357),
     'L1_mix_norm_g': (1.0, 0.6),
     'L1_mix_norm_b': (0.0, 2.0),
     'L1_mix_b_fc1': (0.0, 0.8),
     'L1_mix_b_fc2': (0.0, 0.373),
     'L1_ffn_br': (0.0, 0.8),
     'L1_ffn_b1': (0.0, 0.8),
     'L1_ffn_g1': (1.0, 0.6),
     'L1_ffn_be1': (0.0, 0.8),
     'L1_ffn_m1': (0.0, 0.8),
     'L1_ffn_v1': (1.0, 0.6),
     'L1_ffn_b2': (0.0, 0.8),
     'L1_ffn_g2': (1.0, 0.6),
     'L1_ffn_be2': (0.0, 0.8),
     'L1_ffn_m2': (0.0, 0.8),
     'L1_ffn_v2': (1.0, 0.6),
     'L1_ffn_bo': (0.0, 0.71)}
    factors = {'L0_gnn_bq': 8.0,
     'L0_gnn_bk': 64.0,
     'L0_gnn_bv': 6.07,
     'L0_gnn_bs': 6.596,
     'L0_mix_Wqkv': 4.638,
     'L0_mix_b1': 8.0,
     'L0_mix_b2': 3.248,
     'L0_ffn_w1': 2.962,
     'L1_gnn_b0': 5.646,
     'L1_gnn_b1': 5.825}
    for name, (base, spread) in spreads.items():
        noise = np.random.default_rng([zlib.crc32(name.encode()), seed]).standard_normal(out[name].shape)
        drawn = base * np.exp(spread * noise) if base else spread * noise
        out[name] = jnp.asarray(drawn.astype(out[name].dtype))
    for name, factor in factors.items():
        out[name] = (out[name] * factor).astype(out[name].dtype)
    return out
```

```python
from contextlib import ExitStack

import concourse.bass as bass
from concourse import mybir

ALU = mybir.AluOpType
ACT = mybir.ActivationFunctionType
F32 = mybir.dt.float32
BF16 = mybir.dt.bfloat16
I32 = mybir.dt.int32
I16 = mybir.dt.int16
U32 = mybir.dt.uint32
AX = mybir.AxisListType.X

N = 625
TP = 125
NT = N // TP
D = 256
NC2 = D // 128
HALF = 313
NP = 2 * HALF
EDGES = 10625
ET = EDGES // TP
E0, F0 = 16, 512
E1 = 8
HM = 3 * D
GL = 3
GH = 4
STEPS = GH * NT
MASK = -8.0e30
HAS_EDGE = -1.0e29
FIELD = 4096
CHUNKS = [(0, 32), (32, 64), (64, ET)]

ROWS = ["mix_ln1_g", "mix_ln1_b", "mix_b2", "mix_ln2_g", "mix_ln2_b", "moe_gamma", "moe_beta",
        "g1_b0", "g1_g0", "g1_beta0", "g1_b1", "g1_g1", "g1_beta1",
        "m1_bk", "m1_bv", "m1_norm_g", "m1_norm_b", "m1_bfc2", "gates"]
COLS = [("mix_b1", 2), ("m1_bq", 2), ("m1_bfc1", 6), ("moe_b1", E0 * 4)] + \
       [(k, 2 * E1) for k in ("b1", "g1", "be1", "m1", "v1", "b2", "g2", "be2", "m2", "v2")]
NCOLS = sum(n for _, n in COLS)


NORMS = ["ln0", "ln1", "ln2", "lnm", "lny", "lnx", "gn0", "lnh", "gn1", "lnf"]
TURNS = ["n0", "m1", "xm", "x2", "g1", "y1", "x3"]


class Steps:

    def __init__(self, eng, sem, base=0):
        self.eng, self.sem, self.base, self.n = eng, sem, base, 0

    def step(self, ins):
        ins.then_inc(self.sem, 1)
        self.n += 1

    def settle(self):
        self.eng.wait_ge(self.sem, self.base + self.n)

    def link(self, ins):
        self.step(ins)
        self.settle()


def program(nc, A, out):
    with ExitStack() as ctx:
        def sb(name, shape, dt=F32):
            return ctx.enter_context(nc.sbuf_tensor(name, shape, dt))

        sems = {}

        def S(name):
            if name not in sems:
                sems[name] = ctx.enter_context(nc.semaphore(name))
            return sems[name]

        ps = ctx.enter_context(nc.psum_tensor("ps", [128, 8, 512], F32))

        def pair(b, rows=128):
            return ps[0:rows, b:b + 2, 0:HALF]

        def quads(b, rows=TP):
            return ps[0:rows, b:b + 2, :].rearrange("p b n -> p (b n)")[:, 0:640]\
                .rearrange("p (t n) -> p t n", n=128)[:, :, 0:TP]

        def halves(ap):
            return ap.rearrange("p (b n) -> p b n", b=2)

        ident = sb("ident", [128, 128])
        node_ids = sb("node_ids", [TP, N], I16)
        expert_ids = sb("expert_ids", [TP, 16])
        neg_half = sb("neg_half", [128, 2 * E1 * 2])
        ones = sb("ones", [TP, 128])
        minus_one = sb("minus_one", [TP, 1])
        head_mask = sb("head_mask", [128, 4, 32])
        head_cols = sb("head_cols", [128, 4])

        rows = sb("rows", [TP, len(ROWS), D])
        cols = sb("cols", [128, NCOLS])
        row = {k: rows[:, i, :] for i, k in enumerate(ROWS)}
        col, at = {}, 0
        for k, n in COLS:
            col[k] = (at, n)
            at += n
        gw = sb("gw", [128, 4, NC2, D])
        gbias = sb("gbias", [TP, 2 * D])
        gcols = sb("gcols", [128, GL * 8])
        w_g1 = sb("w_g1", [128, NC2, 2 * D])
        w_m1 = sb("w_m1", [128, NC2, 3 * D + HM])
        w_mix = w_m1[:, :, 0:5 * D]
        gate_w = sb("gate_w", [128, NC2, E0 + E1])
        moe_b2 = sb("moe_b2", [E0, D])
        moe_bo = sb("moe_bo", [E1, D])
        ring = sb("ring", [128, 2, 8 * D])
        w1_moe = [ring[:, u, 0:2 * F0].rearrange("p (c n) -> p c n", c=2) for u in range(2)]
        w2_moe = [ring[:, u, 2 * F0:4 * F0].rearrange("p (c n) -> p c n", c=4) for u in range(2)]
        w3_ffn = [[ring[:, u, k * 2 * D:(k + 1) * 2 * D].rearrange("p (c n) -> p c n", c=2)
                   for k in range(3)] for u in range(2)]

        def R(name):
            return sb(name, [TP, NT, D])

        def T(name):
            return sb(name, [128, NC2, NP])

        x_R, n_R, mix_R, h_R, y_R = [R(k) for k in ("x_R", "n_R", "mix_R", "h_R", "y_R")]
        n_T, q_T, k_T, a_T, b_T, c_T = [T(k) for k in ("n_T", "q_T", "k_T", "a_T", "b_T", "c_T")]
        count = sb("count", [TP, NT, NP])
        logc_all = sb("logc", [128, NT * NP])
        logc = logc_all[0:TP].rearrange("p (t n) -> p t n", t=NT)
        vones = logc_all[0:TP, 0:NT * 258].rearrange("p (t c n) -> p t c n", t=NT, c=2)
        w_fc2 = logc_all[:, 0:HM // 128 * D].rearrange("p (c n) -> p c n", n=D)
        big1 = sb("big1", [128, 4 * NP + 640])
        big2 = sb("big2", [128, 4 * NP + 640])
        idx = sb("idx", [TP, 2, ET], I32)
        idf = sb("idf", [TP, 4, ET])
        oh_dst = sb("oh_dst", [TP, 4, N + 1], BF16)
        oh_src = sb("oh_src", [TP, 4, HALF + 1], BF16)
        vs = sb("vs", [TP, NT, 2 * D])
        stats = {k: (sb(f"st_{k}", [TP, NT, 6]), sb(f"mv_{k}", [TP, NT, 2]),
                     sb(f"ve_{k}", [TP, NT]), sb(f"rs_{k}", [TP, NT]))
                 for k in NORMS}

        cnt_new = big1[0:TP, 0:NT * HALF].bitcast(I32).rearrange("p (t n) -> p t n", t=NT)
        cnt_lo = big1[0:TP, NT * HALF:2 * NT * HALF].bitcast(I32).rearrange("p (t n) -> p t n", t=NT)
        cnt_hi = big2[0:TP, 0:NT * HALF].bitcast(I32).rearrange("p (t n) -> p t n", t=NT)
        cnt_tmp = big2[0:TP, NT * HALF:2 * NT * HALF].bitcast(I32).rearrange("p (t n) -> p t n", t=NT)
        probs = [big1[0:TP, k * NP:(k + 1) * NP] for k in range(3)]
        probs_T = [big2[0:TP, k * 640:k * 640 + N].rearrange("p (s n) -> p s n", s=NT) for k in range(2)]
        hid = [b[:, 0:4 * NP].rearrange("p (m n) -> p m n", m=4) for b in (big1, big2)]

        kv_sb = sb("kv_sb", [128, 2, 132])
        ek = sb("ek", [TP, 2, D])
        eq = sb("eq", [128, 2, HALF])
        zden = sb("zden", [TP, 2, NT, 8])
        gmax = sb("gmax", [TP, STEPS])
        gneg = sb("gneg", [TP, STEPS])
        gden = sb("gden", [TP, STEPS])
        grec = sb("grec", [TP, STEPS])
        att = sb("att", [TP, NT, 64])
        bst = sb("bst", [128, 2, 2, 6])
        bmv = sb("bmv", [128, 2, 2])
        bve = sb("bve", [128, 2])
        brs = sb("brs", [128, 2])
        bsc = sb("bsc", [128, 3, 2])
        lg = sb("lg", [TP, NT, 16])
        top = sb("top", [TP, NT, 8])
        topi = sb("topi", [TP, NT, 8], U32)
        topf = sb("topf", [TP, NT, 2])
        tw = sb("tw", [TP, 4, NT])
        gate = sb("gate", [TP, NT, 16])
        gate2 = sb("gate2", [TP, NT, 16])
        gate_T = eq[0:16].rearrange("p a n -> p (a n)")[:, 0:N]
        inv_deg = sb("inv_deg", [128, NP])
        at_sb = sb("at_sb", [128, 2, 128])
        at_T = sb("at_T", [128, 2, 128])
        at_m = sb("at_m", [128, 4, 4])
        bn_v = sb("bn_v", [128, 4 * E1])
        bn_r = sb("bn_r", [128, 4 * E1])
        bn_s = sb("bn_s", [128, 4 * E1])
        bn_b = sb("bn_b", [128, 4 * E1])
        bn_t = sb("bn_t", [128, 4 * E1])

        def c(name, j=0, n=1):
            return cols[:, col[name][0] + j:col[name][0] + j + n]

        def wide(r):
            return r.unsqueeze(1).broadcast_to([TP, NT, D])

        block = ctx.enter_context(nc.Block())

        @block.sync
        def _(sp):
            sp.dma_start(x_R[:], A["x"].rearrange("(t p) f -> p t f", p=TP)).then_inc(S("x_loaded"), 16)
            sp.dma_start(idx[:, 0, :], A["src"].rearrange("(p j) -> p j", p=TP)).then_inc(S("edges_loaded"), 16)
            sp.dma_start(idx[:, 1, :], A["dst"].rearrange("(p j) -> p j", p=TP)).then_inc(S("edges_loaded"), 16)
            sp.dma_start(w_mix, A["w_mix"].rearrange("(c p) n -> p c n", p=128)).then_inc(S("w_mix_loaded"), 16)
            sp.dma_start(rows[:], A["rows"].unsqueeze(0).broadcast_to([TP, len(ROWS), D])).then_inc(S("rows_loaded"), 16)
            sp.dma_start(cols[:], A["cols"]).then_inc(S("cols_loaded"), 16)

            def attention_weights(i, first):
                if not first:
                    sp.wait_ge(S("g_rows_read"), i * NT)
                sp.dma_start(gw[:], A["gw"][bass.ds(i, 1)].rearrange("a m (c p) n -> p (a m) c n", p=128))\
                    .then_inc(S("gw_loaded"), 16)
                sp.dma_start(gbias[:], A["gbias"][bass.ds(i, 1)].broadcast_to([TP, 2 * D]))\
                    .then_inc(S("gw_loaded"), 16)

            sp.dma_start(gcols[:], A["gcols"]).then_inc(S("gcols_loaded"), 16)
            attention_weights(0, True)
            sp.dma_start(w_g1[:], A["w_g1"].rearrange("(c p) n -> p c n", p=128)).then_inc(S("w_g1_loaded"), 16)
            sp.dma_start(gate_w[:], A["gate_w"].rearrange("(c p) n -> p c n", p=128)).then_inc(S("gates_loaded"), 16)
            sp.dma_start(moe_b2[:], A["moe_b2"]).then_inc(S("gates_loaded"), 16)
            sp.dma_start(moe_bo[:], A["moe_bo"]).then_inc(S("gates_loaded"), 16)
            for e in range(2):
                sp.dma_start(w1_moe[e], A["moe_w1"][e].rearrange("(c p) n -> p c n", p=128)).then_inc(S(f"w1_loaded{e}"), 16)
                sp.dma_start(w2_moe[e], A["moe_w2"][e].rearrange("(c p) n -> p c n", p=128)).then_inc(S(f"w2_loaded{e}"), 16)
            sp.wait_ge(S("my_done"), NT)
            sp.dma_start(w_m1[:], A["w_m1"].rearrange("(c p) n -> p c n", p=128)).then_inc(S("w_m1_loaded"), 16)
            with sp.Fori(1, GL) as i:
                attention_weights(i, False)
            sp.wait_ge(S("g_max"), GL * STEPS)
            sp.dma_start(w_fc2, A["w_fc2"].rearrange("(c p) n -> p c n", p=128)).then_inc(S("w_fc2_loaded"), 16)
            with sp.Fori(1, E0 // 2) as g:
                for u in range(2):
                    sp.wait_ge(S("moe_h_done"), (g * 2 + u - 1) * 4)
                    sp.dma_start(w1_moe[u], A["moe_w1"][bass.ds(g * 2 + u, 1)].rearrange("a (c p) n -> p (a c) n", p=128))\
                        .then_inc(S(f"w1_loaded{u}"), 16)
                    sp.wait_ge(S("moe_y_done"), (g * 2 + u - 1) * 3)
                    sp.dma_start(w2_moe[u], A["moe_w2"][bass.ds(g * 2 + u, 1)].rearrange("a (c p) n -> p (a c) n", p=128))\
                        .then_inc(S(f"w2_loaded{u}"), 16)

            def ffn_weights(e, u):
                sp.dma_start(w3_ffn[u][0], A["ffn_w"][bass.ds(e, 1), 0].rearrange("a (c p) n -> p (a c) n", p=128))\
                    .then_inc(S(f"ffn_loaded{u}"), 16)
                sp.dma_start(w3_ffn[u][1], A["ffn_w"][bass.ds(e, 1), 1].rearrange("a (c p) n -> p (a c) n", p=128))\
                    .then_inc(S(f"ffn_loaded{u}"), 16)
                sp.dma_start(w3_ffn[u][2], A["ffn_w"][bass.ds(e, 1), 2].rearrange("a (c p) n -> p (a c) n", p=128))\
                    .then_inc(S(f"ffn_loaded{u}"), 16)

            for e in range(2):
                sp.wait_ge(S("moe_h_done"), (E0 - 1 + e) * 4)
                sp.wait_ge(S("moe_y_done"), (E0 - 1 + e) * 3)
                ffn_weights(e, e)
            with sp.Fori(1, E1 // 2) as g:
                for u in range(2):
                    sp.wait_ge(S("ffn_y_done"), (g * 2 + u - 1) * 3)
                    ffn_weights(g * 2 + u, u)
            sp.wait_ge(S("ffn_acc"), E1 * NT)
            sp.dma_start(out.rearrange("(t p) f -> p t f", p=TP), x_R[:]).then_inc(S("stored"), 16)
            sp.wait_ge(S("stored"), 16)

        @block.gpsimd
        def _(pool):
            own = Steps(pool, S("pool_steps"))

            def rstd(name):
                st, mv, ve, rs = stats[name]
                pool.wait_ge(S("norm_var"), NORMS.index(name) + 1)
                pool.tensor_tensor(rs[:], ve[:], neg_half[0:TP, 0:NT], ALU.pow).then_inc(S("norm_rstd"), 1)

            own.step(pool.memset(minus_one[:], -1.0))
            own.link(pool.memset(neg_half[:], -0.5))
            rstd("ln0")
            own.step(pool.memset(ident[:], 0.0))
            own.step(pool.memset(head_mask[:], 1.0))
            own.link(pool.memset(head_cols[:], 1.0))
            pool.affine_select(out=ident[:], in_=ident[:], compare_op=ALU.not_equal, fill=1.0, base=0,
                               pattern=[[-1, 128]], channel_multiplier=1).then_inc(S("ident_ready"), 1)
            pool.iota(node_ids[:], pattern=[[1, N]], base=0, channel_multiplier=0).then_inc(S("ids_ready"), 1)
            for t in (n_T, q_T, k_T, a_T, b_T, c_T):
                pool.memset(t[:, :, N:NP], 0.0).then_inc(S("pads_ready"), 1)
            pool.memset(vones[:, :, :, 128:129], 1.0).then_inc(S("vones_ready"), 1)
            own.step(pool.affine_select(out=head_mask[:], in_=head_mask[:], compare_op=ALU.is_ge, fill=0.0, base=0,
                                        pattern=[[-32, 4], [0, 32]], channel_multiplier=1))
            own.link(pool.affine_select(out=head_cols[:], in_=head_cols[:], compare_op=ALU.is_ge, fill=0.0, base=0,
                                        pattern=[[-32, 4]], channel_multiplier=1))
            pool.affine_select(out=head_mask[:], in_=head_mask[:], compare_op=ALU.is_ge, fill=0.0, base=31,
                               pattern=[[32, 4], [0, 32]], channel_multiplier=-1).then_inc(S("masks_ready"), 1)
            pool.affine_select(out=head_cols[:], in_=head_cols[:], compare_op=ALU.is_ge, fill=0.0, base=31,
                               pattern=[[32, 4]], channel_multiplier=-1).then_inc(S("masks_ready"), 1)
            own.link(pool.iota(expert_ids[:].bitcast(I32), pattern=[[1, 16]], base=0, channel_multiplier=0))
            pool.tensor_copy(expert_ids[:], expert_ids[:].bitcast(I32)).then_inc(S("expert_ids_ready"), 1)
            pool.memset(ones[:], 1.0).then_inc(S("ones_ready"), 1)
            pool.memset(at_sb[:], 0.0).then_inc(S("at_zero"), 1)
            rstd("ln1")
            rstd("ln2")

            pool.wait_ge(S("bn_var"), 2)
            pool.tensor_tensor(bn_r[:], bn_v[:], neg_half[:, 0:4 * E1], ALU.pow).then_inc(S("bn_rstd"), 1)

            def attention(i, last):
                for n in range(STEPS):
                    pool.wait_ge(S("g_max"), i * STEPS + n + 1)
                    pool.tensor_tensor(gneg[:, n:n + 1], gmax[:, n:n + 1], minus_one[:], ALU.mult)\
                        .then_inc(S("g_neg"), 1)
                if not last:
                    pool.wait_ge(S("g_var"), i + 1)
                    pool.tensor_tensor(brs[:], bve[:], neg_half[:, 0:2], ALU.pow).then_inc(S("g_rstd"), 1)

            with pool.Fori(0, GL - 1) as i:
                attention(i, False)
            attention(GL - 1, True)
            for name in ("lnm", "lny", "lnx", "gn0", "lnh", "gn1", "lnf"):
                rstd(name)

        @block.scalar
        def _(act):
            def evac_T(name, dst, bank):
                act.wait_ge(S("rows_turned"), 10 * TURNS.index(name) + 10)
                act.activation(dst[:, :, 0:4 * TP], ps[:, bank:bank + 2, 0:4 * TP], ACT.Identity)\
                    .then_inc(S("T_by_act"), 1)

            evac_T("n0", n_T, 5)

            def counts(k):
                act.wait_ge(S("onehot_used"), CHUNKS[k][1])
                if k:
                    act.wait_ge(S("counts_added"), k)
                act.activation(cnt_new, ps[0:TP, 0:NT, 0:HALF], ACT.Copy).then_inc(S("counts_out"), 1)

            counts(0)
            for j in range(4):
                act.wait_ge(S("mq_done"), j + 1)
                if j >= 2:
                    act.wait_ge(S("mq_phi"), j - 1)
                act.activation(eq[:, j % 2, :], ps[:, 5 + j % 3, 0:HALF], ACT.Exp).then_inc(S("mq_exp"), 1)
            for t in range(NT):
                act.wait_ge(S("mkv_done"), t + 1)
                if t >= 2:
                    act.wait_ge(S("mkv_phi"), t - 1)
                act.activation(ek[:, t % 2, :], ps[0:TP, 5 + (4 + t) % 3, 0:D], ACT.Exp)
                act.activation(vones[:, t, :, 0:128],
                               ps[0:TP, 5 + (4 + t) % 3, D:2 * D].rearrange("p (c n) -> p c n", c=2), ACT.Copy)\
                    .then_inc(S("mkv_exp"), 1)
            counts(1)
            evac_T("m1", a_T, 5)
            act.wait_ge(S("cols_loaded"), 16)
            for j in range(4):
                m, h = divmod(j, 2)
                act.wait_ge(S("mh_done"), j + 1)
                act.activation(b_T[:, m, h * HALF:(h + 1) * HALF], ps[:, 5 + (18 + j) % 3, 0:HALF], ACT.Gelu,
                               bias=c("mix_b1", m)).then_inc(S("mh_gelu"), 1)
            counts(2)
            act.wait_ge(S("count_floor"), 1)
            act.activation(logc, logc, ACT.Ln).then_inc(S("count_ln"), 1)

            def attention(i, last):
                for m in range(NC2):
                    act.wait_ge(S("g_q_done"), i * 2 + m + 1)
                    act.activation(q_T[:, m, :].rearrange("p (b n) -> p b n", b=2), pair(2 * m), ACT.Identity,
                                   bias=gcols[:, bass.ds(i * 8 + m, 1)]).then_inc(S("g_q"), 1)
                for n in range(STEPS + 1):
                    if n < STEPS:
                        act.wait_ge(S("g_neg"), i * STEPS + n + 1)
                        act.activation(probs[n % 3], probs[n % 3], ACT.Exp, bias=gneg[:, n:n + 1],
                                       accum_out=gden[:, n:n + 1]).then_inc(S("g_exp"), 1)
                    if n:
                        m = n - 1
                        act.wait_ge(S("g_turned"), i * STEPS + m + 1)
                        if m >= 2:
                            act.wait_ge(S("g_pv"), i * STEPS + m - 1)
                        act.activation(probs_T[m % 2], quads(4), ACT.Copy).then_inc(S("g_probs_T"), 1)
                if not last:
                    act.wait_ge(S("gh_turned"), i * 10 + 10)
                    act.activation(a_T[:, :, 0:4 * TP], ps[:, 0:2, 0:4 * TP], ACT.Identity).then_inc(S("gh_T"), 1)
                    act.wait_ge(S("g_affine"), i + 1)
                    for m in range(NC2):
                        act.activation(n_T[:, m, 0:N], a_T[:, m, 0:N], ACT.Relu, bias=bsc[:, 2, m:m + 1],
                                       scale=bsc[:, 0, m:m + 1]).then_inc(S("g_next"), 1)

            act.wait_ge(S("gcols_loaded"), 16)
            with act.Fori(0, GL - 1) as i:
                attention(i, False)
            attention(GL - 1, True)

            evac_T("xm", c_T, 0)
            act.wait_ge(S("top_diff"), 1)
            act.activation(tw[:, 1, :], tw[:, 0, :], ACT.Exp).then_inc(S("top_exp"), 1)

            def moe_h(e, u, first):
                for m in range(4):
                    act.wait_ge(S("moe_h_done"), e * 4 + m + 1)
                    if m == 0 and not first:
                        act.wait_ge(S("moe_y_done"), (e - 1) * 3)
                    act.activation(halves(hid[u][:, m, :]), pair(2 * (m % 2)), ACT.Relu,
                                   bias=cols[:, bass.ds(e * 4 + (col["moe_b1"][0] + m), 1)]).then_inc(S("moe_relu"), 1)

            moe_h(0, 0, True)
            moe_h(1, 1, True)
            with act.Fori(1, E0 // 2) as g:
                for u in range(2):
                    moe_h(g * 2 + u, u, False)

            evac_T("x2", n_T, 0)
            for m in range(NC2):
                act.wait_ge(S("m1_q_done"), m + 1)
                act.activation(halves(q_T[:, m, :]), pair(4 + 2 * m), ACT.Identity, bias=c("m1_bq", m))\
                    .then_inc(S("m1_q"), 1)
            for k in range(4):
                act.wait_ge(S("m1_neg"), k + 1)
                p, q = 64 * (k % 2), k // 2
                act.activation(at_sb[p:p + 64, q, p:p + 64], ps[p:p + 64, 5, q * 128 + p:q * 128 + p + 64], ACT.Exp,
                               bias=at_m[p:p + 64, k, 1:2], scale=0.125, accum_out=at_m[p:p + 64, k, 2:3])\
                    .then_inc(S("m1_exp"), 1)
            act.wait_ge(S("gn0_normed"), 1)
            act.activation(y_R[:], y_R[:], ACT.Silu).then_inc(S("g1_x"), 1)
            evac_T("g1", k_T, 0)
            evac_T("y1", b_T, 4)
            for m in range(HM // 128):
                act.wait_ge(S("fc1_done"), m + 1)
                act.activation(halves(hid[0][:, m, :] if m < 4 else hid[1][:, m - 4, :]), pair(4 + 2 * (m % 2)),
                               ACT.Gelu, bias=c("m1_bfc1", m)).then_inc(S("fc1_gelu"), 1)
            act.wait_ge(S("gn1_normed"), 1)
            act.activation(y_R[:], y_R[:], ACT.Silu).then_inc(S("g1_x2"), 1)
            evac_T("x3", c_T, 0)
            act.wait_ge(S("gate2_shift"), 1)
            act.activation(gate2[:, :, 0:E1], gate2[:, :, 0:E1], ACT.Exp).then_inc(S("gate2_exp"), 1)

            act.wait_ge(S("bn_affine"), 1)

            def ffn(e, u, first):
                for k in range(2):
                    for m in range(NC2):
                        act.wait_ge(S("ffn_h_done"), e * 4 + 2 * k + m + 1)
                        if k == 0 and m == 0 and not first:
                            act.wait_ge(S("ffn_y_done"), (e - 1) * 3)
                        j = e * 2 + (2 * E1 * k + m)
                        act.activation(halves(hid[u][:, 2 * k + m, :]), pair(2 * m), ACT.Relu,
                                       bias=bn_b[:, bass.ds(j, 1)], scale=bn_s[:, bass.ds(j, 1)])\
                            .then_inc(S("ffn_relu"), 1)

            ffn(0, 0, True)
            ffn(1, 1, True)
            with act.Fori(1, E1 // 2) as g:
                for u in range(2):
                    ffn(g * 2 + u, u, False)

        @block.vector
        def _(dve):
            own = Steps(dve, S("dve_steps"))
            tt, tsc, stt = dve.tensor_tensor, dve.tensor_scalar, dve.scalar_tensor_tensor

            def norm(name, X, Y, eps, gain=None, shift=None):
                st, mv, ve, rs = stats[name]
                for t in range(NT):
                    own.step(dve.bn_stats(st[:, t, :], X[:, t, :]))
                own.settle()
                for t in range(NT):
                    own.step(dve.bn_aggr(mv[:, t, :], st[:, t, :]))
                own.settle()
                tsc(ve[:], mv[:, :, 1], eps, None, ALU.add).then_inc(S("norm_var"), 1)
                dve.wait_ge(S("norm_rstd"), NORMS.index(name) + 1)
                for t in range(NT):
                    last = tsc(Y[:, t, :], X[:, t, :], mv[:, t, 0:1], rs[:, t:t + 1], ALU.subtract, ALU.mult)
                    if t < NT - 1 or gain is not None:
                        own.step(last)
                if gain is not None:
                    own.settle()
                    own.link(tt(Y[:], Y[:], wide(gain), ALU.mult))
                    last = tt(Y[:], Y[:], wide(shift), ALU.add)
                return last

            def evac_T(name, dst, bank):
                dve.wait_ge(S("rows_turned"), 10 * TURNS.index(name) + 10)
                dve.tensor_copy(dst[:, :, 4 * TP:N], ps[:, bank, 0:2 * TP].rearrange("p (c n) -> p c n", c=2))\
                    .then_inc(S("T_by_dve"), 1)

            dve.wait_ge(S("x_loaded"), 16)
            norm("ln0", x_R, n_R, 1e-5).then_inc(S("n0_ready"), 1)
            dve.wait_ge(S("edges_loaded"), 32)
            own.link(dve.tensor_copy(idf[:, 0:2, :], idx[:]))
            own.link(tsc(idf[:, 3, :], idf[:, 0, :], float(HALF), None, ALU.is_ge))
            own.step(stt(out=idf[:, 2, :], in0=idf[:, 3, :], scalar=-float(HALF), in1=idf[:, 0, :],
                         op0=ALU.mult, op1=ALU.add))
            own.link(tsc(idf[:, 3, :], idf[:, 3, :], float(FIELD - 1), 1.0, ALU.mult, ALU.add))
            evac_T("n0", n_T, 7)
            dve.wait_ge(S("ids_ready"), 1)

            def one_hot(j, u, free):
                if free is not None:
                    dve.wait_ge(S("onehot_used"), free)
                tsc(oh_src[:, u, 0:HALF], node_ids[:, 0:HALF], idf[:, 2, bass.ds(j, 1)], idf[:, 3, bass.ds(j, 1)],
                    ALU.is_equal, ALU.mult)
                tsc(oh_dst[:, u, 0:N], node_ids[:], idf[:, 1, bass.ds(j, 1)], None, ALU.is_equal)\
                    .then_inc(S("onehot_ready"), 1)

            def edges(k):
                a, b = CHUNKS[k]
                if a == 0:
                    for u in range(4):
                        one_hot(u, u, None)
                    a = 4
                with dve.Fori(a // 4, b // 4) as g:
                    for u in range(4):
                        one_hot(g * 4 + u, u, g * 4 + (u - 3))
                if b % 4:
                    one_hot(b - 1, 0, b - 4)

            def add_counts(k):
                dve.wait_ge(S("counts_out"), k + 1)
                if k == 0:
                    own.step(tsc(cnt_hi, cnt_new, 12, None, ALU.logical_shift_right))
                    tsc(cnt_lo, cnt_new, FIELD - 1, None, ALU.bitwise_and).then_inc(S("counts_added"), 1)
                    dve.wait_ge(S("counts_added"), 1)
                    return
                lo, hi = (count[:, :, 0:HALF], count[:, :, HALF:NP]) if k == 2 else (cnt_lo, cnt_hi)
                own.link(tsc(cnt_tmp, cnt_new, 12, None, ALU.logical_shift_right))
                own.link(tt(hi, cnt_hi, cnt_tmp, ALU.add))
                own.link(tsc(cnt_tmp, cnt_new, FIELD - 1, None, ALU.bitwise_and))
                tt(lo, cnt_lo, cnt_tmp, ALU.add).then_inc(S("counts_added"), 1)
                dve.wait_ge(S("counts_added"), k + 1)

            edges(0)
            add_counts(0)
            dve.wait_ge(S("pads_ready"), 6)
            for j in range(4):
                m, h = divmod(j, 2)
                dve.wait_ge(S("mq_exp"), j + 1)
                own.link(tsc(eq[:, j % 2, :], eq[:, j % 2, :], 1.0, None, ALU.min))
                stt(out=q_T[:, m, h * HALF:(h + 1) * HALF], in0=ps[:, 5 + j % 3, 0:HALF], scalar=0.0,
                    in1=eq[:, j % 2, :], op0=ALU.max, op1=ALU.add).then_inc(S("mq_phi"), 1)
            for t in range(NT):
                dve.wait_ge(S("mkv_exp"), t + 1)
                own.link(tsc(ek[:, t % 2, :], ek[:, t % 2, :], 1.0, None, ALU.min))
                stt(out=vs[:, t, 0:D], in0=ps[0:TP, 5 + (4 + t) % 3, 0:D], scalar=0.0,
                    in1=ek[:, t % 2, :], op0=ALU.max, op1=ALU.add).then_inc(S("mkv_phi"), 1)
            edges(1)
            dve.wait_ge(S("masks_ready"), 2)
            dve.wait_ge(S("mKV_done"), 2)
            for q in range(2):
                own.step(tt(kv_sb[:, q, 0:128].rearrange("p (h n) -> p h n", h=4),
                            ps[:, 5, q * 129:q * 129 + 128].rearrange("p (h n) -> p h n", h=4), head_mask[:], ALU.mult))
                last = tsc(kv_sb[:, q, 128:132], head_cols[:], ps[:, 5, q * 129 + 128:q * 129 + 129], None, ALU.mult)
                if q == 0:
                    own.step(last)
            last.then_inc(S("mKV_ready"), 1)
            add_counts(1)
            for t in range(NT):
                b = 5 + (1 + t) % 3
                dve.wait_ge(S("mt_done"), t + 1)
                src = ps[0:TP, b, 0:264].rearrange("p (c n) -> p c n", c=2)
                own.link(tsc(zden[:, 0, t, :].rearrange("p (c n) -> p c n", c=2), src[:, :, 128:132], 1e-6, None, ALU.add))
                own.link(dve.reciprocal(zden[:, 1, t, :], zden[:, 0, t, :]))
                for q in range(2):
                    last = tt(mix_R[:, t, q * 128:(q + 1) * 128].rearrange("p (h n) -> p h n", h=4),
                              ps[0:TP, b, q * 132:q * 132 + 128].rearrange("p (h n) -> p h n", h=4),
                              zden[:, 1, t, 4 * q:4 * q + 4].unsqueeze(2).broadcast_to([TP, 4, 32]), ALU.mult)
                    if q == 0:
                        own.step(last)
                last.then_inc(S("mt_out"), 1)
            own.settle()
            dve.wait_ge(S("mt_out"), NT)
            own.link(tt(mix_R[:], mix_R[:], n_R[:], ALU.add))
            dve.wait_ge(S("rows_loaded"), 16)
            norm("ln1", mix_R, h_R, 1e-5, row["mix_ln1_g"], row["mix_ln1_b"]).then_inc(S("m1_ready"), 1)
            dve.wait_ge(S("m1_ready"), 1)
            edges(2)
            evac_T("m1", a_T, 7)
            own.link(tt(h_R[:], h_R[:], wide(row["mix_b2"]), ALU.add))
            for t in range(NT):
                dve.wait_ge(S("my_done"), t + 1)
                tt(mix_R[:, t, :], ps[0:TP, 5 + (22 + t) % 3, 0:D], h_R[:, t, :], ALU.add).then_inc(S("my_out"), 1)
            dve.wait_ge(S("my_out"), NT)
            own.link(norm("ln2", mix_R, mix_R, 1e-5, row["mix_ln2_g"], row["mix_ln2_b"]))
            own.link(tt(x_R[:], x_R[:], mix_R[:], ALU.add))
            add_counts(2)
            own.step(tsc(logc, count[:], 1.0, None, ALU.max))
            dve.wait_ge(S("counts_added"), 3)
            tsc(big2[0:TP, 0:NT * NP].rearrange("p (t n) -> p t n", t=NT), count[:], 0.5, MASK,
                ALU.is_lt, ALU.mult).then_inc(S("count_floor"), 1)
            own.settle()
            dve.wait_ge(S("count_floor"), 1)
            dve.wait_ge(S("count_ln"), 1)
            stt(out=logc, in0=logc, scalar=8.0, in1=big2[0:TP, 0:NT * NP].rearrange("p (t n) -> p t n", t=NT),
                op0=ALU.mult, op1=ALU.add).then_inc(S("logc_ready"), 1)
            dve.wait_ge(S("cols_loaded"), 16)
            for k in range(2):
                tsc(bn_v[:, k * 2 * E1:(k + 1) * 2 * E1], c("v1" if k == 0 else "v2", 0, 2 * E1), 1e-3, None, ALU.add)\
                    .then_inc(S("bn_var"), 1)
            dve.wait_ge(S("bn_rstd"), 1)
            for k in range(2):
                z = slice(k * 2 * E1, (k + 1) * 2 * E1)
                own.step(tt(bn_s[:, z], bn_r[:, z], c("g1" if k == 0 else "g2", 0, 2 * E1), ALU.mult))
                own.link(tt(bn_t[:, z], c("b1" if k == 0 else "b2", 0, 2 * E1), c("m1" if k == 0 else "m2", 0, 2 * E1),
                            ALU.subtract))
                own.link(tt(bn_t[:, z], bn_t[:, z], bn_s[:, z], ALU.mult))
                last = tt(bn_b[:, z], bn_t[:, z], c("be1" if k == 0 else "be2", 0, 2 * E1), ALU.add)
                if k == 0:
                    own.step(last)
            last.then_inc(S("bn_affine"), 1)

            LAYER_STEPS = 2 * GH + 8

            def attention(i, last_layer):
                lay = Steps(dve, S("g_dve_steps"), i * LAYER_STEPS)
                dve.wait_ge(S("logc_ready"), 1)
                dve.wait_ge(S("gcols_loaded"), 16)
                for m in range(NC2):
                    dve.wait_ge(S("g_k_done"), i * 2 + m + 1)
                    tsc(halves(k_T[:, m, :]), pair(4 + 2 * m), gcols[:, bass.ds(i * 8 + (2 + m), 1)], None, ALU.add)\
                        .then_inc(S("g_k"), 1)
                for t in range(NT):
                    dve.wait_ge(S("g_rows_done"), i * NT + t + 1)
                    tt(vs[:, t, :], ps[0:TP, t, :], gbias[:], ALU.add).then_inc(S("g_rows_read"), 1)
                dve.wait_ge(S("g_rows_read"), i * NT + NT)

                def head_out(h):
                    z = slice(h * NT, h * NT + NT)
                    dve.wait_ge(S("g_exp"), i * STEPS + h * NT + NT)
                    lay.link(dve.reciprocal(grec[:, z], gden[:, z]))
                    lay.link(stt(out=grec[:, z], in0=gmax[:, z], scalar=HAS_EDGE, in1=grec[:, z],
                                 op0=ALU.is_gt, op1=ALU.mult))
                    dve.wait_ge(S("g_pv"), i * STEPS + h * NT + NT)
                    tt(att[:], ps[0:TP, 6 + h % 2, 0:NT * 64].rearrange("p (t n) -> p t n", t=NT),
                       grec[:, z].unsqueeze(2).broadcast_to([TP, NT, 64]), ALU.mult).then_inc(S("g_head"), 1)
                    dve.wait_ge(S("g_head"), i * GH + h + 1)
                    tt(h_R[:, :, h * 64:(h + 1) * 64], att[:], vs[:, :, D + h * 64:D + (h + 1) * 64], ALU.add)\
                        .then_inc(S("g_out"), 1)
                    dve.wait_ge(S("g_out"), i * GH + h + 1)

                for n in range(STEPS):
                    dve.wait_ge(S("g_scores"), i * STEPS + n + 1)
                    if n >= 3:
                        dve.wait_ge(S("g_turned"), i * STEPS + n - 2)
                    dve.nop(nofuse=True)
                    dve.tensor_tensor_reduce(out=halves(probs[n % 3]), in0=pair(2 * (n % 2), TP),
                                             in1=halves(logc[:, n % NT, :]), scale=0.125, scalar=-3.0e38,
                                             op0=ALU.add, op1=ALU.max, accum_out=gmax[:, n:n + 1])\
                        .then_inc(S("g_max"), 1)
                    if n % NT == 3 and n > NT:
                        head_out(n // NT - 1)
                head_out(GH - 1)
                if last_layer:
                    return
                dve.wait_ge(S("gh_turned"), i * 10 + 10)
                dve.tensor_copy(a_T[:, :, 4 * TP:N], ps[:, 2, 0:2 * TP].rearrange("p (c n) -> p c n", c=2))\
                    .then_inc(S("gh_T2"), 1)
                dve.wait_ge(S("gh_T"), i + 1)
                dve.wait_ge(S("gh_T2"), i + 1)
                for m in range(NC2):
                    lay.step(dve.bn_stats(bst[:, m, 0, :], a_T[:, m, 0:HALF]))
                    lay.step(dve.bn_stats(bst[:, m, 1, :], a_T[:, m, HALF:N]))
                lay.settle()
                dve.nop(nofuse=True)
                for m in range(NC2):
                    lay.step(dve.bn_aggr(bmv[:, m, :], bst[:, m, :, :]))
                lay.settle()
                tsc(bve[:], bmv[:, :, 1], 1e-5, None, ALU.add).then_inc(S("g_var"), 1)
                dve.wait_ge(S("g_rstd"), i + 1)
                lay.link(tt(bsc[:, 0, :], brs[:], gcols[:, bass.ds(i * 8 + 4, 2)], ALU.mult))
                lay.link(tt(bsc[:, 1, :], bmv[:, :, 0], bsc[:, 0, :], ALU.mult))
                tt(bsc[:, 2, :], gcols[:, bass.ds(i * 8 + 6, 2)], bsc[:, 1, :], ALU.subtract).then_inc(S("g_affine"), 1)
                return lay.n

            with dve.Fori(0, GL - 1) as i:
                LS = attention(i, False)
            assert LS == LAYER_STEPS, LS
            attention(GL - 1, True)

            own.link(tt(x_R[:], x_R[:], h_R[:], ALU.add))
            norm("lnm", x_R, n_R, 1e-5).then_inc(S("xm_ready"), 1)
            evac_T("xm", c_T, 2)
            dve.wait_ge(S("logits_done"), 1)
            own.link(tt(lg[:], ps[0:TP, 7, 0:NT * 16].rearrange("p (t n) -> p t n", t=NT),
                        row["gates"][:, 0:16].unsqueeze(1).broadcast_to([TP, NT, 16]), ALU.add))
            for t in range(NT):
                own.step(dve.max(top[:, t, :], lg[:, t, :]))
            own.settle()
            for t in range(NT):
                own.step(dve.max_index(topi[:, t, :], top[:, t, :], lg[:, t, :]))
            tt(tw[:, 0, :], top[:, :, 1], top[:, :, 0], ALU.subtract).then_inc(S("top_diff"), 1)
            own.settle()
            own.step(dve.tensor_copy(topf[:], topi[:, :, 0:2]))
            dve.wait_ge(S("top_exp"), 1)
            own.link(tsc(tw[:, 2, :], tw[:, 1, :], 1.0, None, ALU.add))
            own.link(dve.reciprocal(tw[:, 2, :], tw[:, 2, :]))
            own.link(tt(tw[:, 3, :], tw[:, 1, :], tw[:, 2, :], ALU.mult))
            dve.wait_ge(S("expert_ids_ready"), 1)
            for t in range(NT):
                own.step(tsc(gate[:, t, :], expert_ids[:], topf[:, t, 0:1], tw[:, 2, t:t + 1], ALU.is_equal, ALU.mult))
                own.step(tsc(lg[:, t, :], expert_ids[:], topf[:, t, 1:2], tw[:, 3, t:t + 1], ALU.is_equal, ALU.mult))
            own.settle()
            tt(gate[:], gate[:], lg[:], ALU.add).then_inc(S("gate_ready"), 1)
            dve.wait_ge(S("gate_turned"), NT)
            dve.tensor_copy(gate_T.rearrange("p (t n) -> p t n", t=NT), quads(4, 16)).then_inc(S("gate_T_ready"), 1)

            def rows_of(name, acc, e, scale, base, n0):
                for t in range(NT):
                    if t % 2 == 0:
                        dve.wait_ge(S(f"{name}_y_done"), e * 3 + t // 2 + 1)
                    src = ps[0:TP, 4 + t // 2, (t % 2) * D:(t % 2 + 1) * D]
                    if n0:
                        dve.wait_ge(S(f"{name}_acc"), e * NT + t - NT + 1)
                    stt(out=acc[:, t, :], in0=src, scalar=scale(t), in1=acc[:, t, :], op0=ALU.mult, op1=ALU.add)\
                        .then_inc(S(f"{name}_acc"), 1)

            def bias_rows(name, acc):
                for t in range(NT):
                    dve.wait_ge(S(f"{name}_b_done"), min(t // 2 * 2 + 2, NT))
                    tt(acc[:, t, :], ps[0:TP, 7 - t // 2, (t % 2) * D:(t % 2 + 1) * D],
                       acc[:, t, :], ALU.add).then_inc(S(f"{name}_bias_in"), 1)
                dve.wait_ge(S(f"{name}_bias_in"), NT)

            bias_rows("moe", n_R)
            rows_of("moe", n_R, 0, lambda t: gate[:, t, 0:1], 0, False)
            gate_flat = gate[:].rearrange("p t n -> p (t n)")
            rows_of("moe", n_R, 1, lambda t: gate[:, t, 1:2], 0, True)
            with dve.Fori(1, E0 // 2) as g:
                for u in range(2):
                    e = g * 2 + u
                    rows_of("moe", n_R, e, lambda t: gate_flat[:, bass.ds(e + 16 * t, 1)], 0, True)
            dve.wait_ge(S("moe_acc"), E0 * NT)
            own.link(norm("lny", n_R, y_R, 1e-5, row["moe_gamma"], row["moe_beta"]))
            own.link(tt(x_R[:], x_R[:], y_R[:], ALU.add))
            norm("lnx", x_R, n_R, 1e-5).then_inc(S("x2_ready"), 1)
            evac_T("x2", n_T, 2)

            dve.wait_ge(S("deg_done"), 1)
            own.link(tsc(halves(inv_deg[:]), pair(0), 1.0, None, ALU.max))
            dve.reciprocal(inv_deg[:], inv_deg[:]).then_inc(S("inv_deg_ready"), 1)
            dve.wait_ge(S("inv_deg_ready"), 1)

            def aggregate(l, src_T):
                for m in range(NC2):
                    dve.wait_ge(S("agg_done"), 2 * l + m + 1)
                    own.link(tt(halves(a_T[:, m, :]), pair(2 * m), halves(inv_deg[:]), ALU.mult))
                    tt(a_T[:, m, :], a_T[:, m, :], src_T[:, m, :], ALU.add).then_inc(S("agg_out"), 1)

            dve.wait_ge(S("T_by_act"), TURNS.index("x2") + 1)
            dve.wait_ge(S("T_by_dve"), TURNS.index("x2") + 1)
            aggregate(0, n_T)
            for t in range(NT):
                dve.wait_ge(S("m1_kv_done"), t + 1)
                tt(vs[:, t, :], ps[0:TP, 4 + t % 4, :],
                   rows[:, ROWS.index("m1_bk"):ROWS.index("m1_bv") + 1, :].rearrange("p a n -> p (a n)"), ALU.add)\
                    .then_inc(S("m1_kv"), 1)

            def graph_rows(l):
                for t in range(NT):
                    dve.wait_ge(S("g1_h_done"), l * NT + t + 1)
                    tt(y_R[:, t, :], ps[0:TP, t % 4, 0:D], row[f"g1_b{l}"], ALU.add).then_inc(S("g1_h"), 1)
                dve.wait_ge(S("g1_h"), l * NT + NT)
                norm(f"gn{l}", y_R, y_R, 1e-5, row[f"g1_g{l}"], row[f"g1_beta{l}"]).then_inc(S(f"gn{l}_normed"), 1)

            dve.wait_ge(S("m1_at_done"), 2)
            for k in range(4):
                p, q = 64 * (k % 2), k // 2
                own.link(dve.reduce_max(at_m[p:p + 64, k, 0:1], ps[p:p + 64, 5, q * 128 + p:q * 128 + p + 64], AX))
            for k in range(4):
                p = 64 * (k % 2)
                tsc(at_m[p:p + 64, k, 1:2], at_m[p:p + 64, k, 0:1], -0.125, None, ALU.mult).then_inc(S("m1_neg"), 1)
            graph_rows(0)
            for k in range(4):
                p, q = 64 * (k % 2), k // 2
                dve.wait_ge(S("m1_exp"), k + 1)
                own.link(dve.reciprocal(at_m[p:p + 64, k, 2:3], at_m[p:p + 64, k, 2:3]))
                tsc(at_sb[p:p + 64, q, p:p + 64], at_sb[p:p + 64, q, p:p + 64], at_m[p:p + 64, k, 2:3], None, ALU.mult)\
                    .then_inc(S("m1_attn"), 1)
            dve.wait_ge(S("at_turned"), 2)
            dve.tensor_copy(at_T[:], ps[:, 6, 0:256].rearrange("p (c n) -> p c n", c=2)).then_inc(S("at_T_ready"), 1)
            for t in range(NT):
                dve.wait_ge(S("m1_xf_done"), t + 1)
                tt(mix_R[:, t, :], ps[0:TP, 4 + t % 4, 0:D], n_R[:, t, :], ALU.add).then_inc(S("m1_xf"), 1)
            dve.wait_ge(S("m1_xf"), NT)
            norm("lnh", mix_R, h_R, 1e-5, row["m1_norm_g"], row["m1_norm_b"]).then_inc(S("y1_ready"), 1)
            evac_T("g1", k_T, 2)
            evac_T("y1", b_T, 6)
            dve.wait_ge(S("T_by_act"), TURNS.index("g1") + 1)
            dve.wait_ge(S("T_by_dve"), TURNS.index("g1") + 1)
            aggregate(1, k_T)
            own.step(tt(x_R[:], x_R[:], mix_R[:], ALU.add))
            own.settle()
            own.link(tt(x_R[:], x_R[:], wide(row["m1_bfc2"]), ALU.add))
            graph_rows(1)
            for t in range(NT):
                dve.wait_ge(S("fc2_done"), t + 1)
                tt(x_R[:, t, :], ps[0:TP, 4 + t % 4, 0:D], x_R[:, t, :], ALU.add).then_inc(S("fc2_out"), 1)
            dve.wait_ge(S("fc2_out"), NT)
            dve.wait_ge(S("g1_x2"), 1)
            own.link(tt(x_R[:], x_R[:], y_R[:], ALU.add))
            norm("lnf", x_R, n_R, 1e-5).then_inc(S("x3_ready"), 1)
            evac_T("x3", c_T, 2)

            dve.wait_ge(S("logits2_done"), 1)
            own.link(tt(gate2[:, :, 0:E1], ps[0:TP, 7, 0:NT * E1].rearrange("p (t n) -> p t n", t=NT),
                        row["gates"][:, 16:16 + E1].unsqueeze(1).broadcast_to([TP, NT, E1]), ALU.add))
            own.link(dve.tensor_reduce(tw[:, 0, :], gate2[:, :, 0:E1], AX, ALU.max))
            tt(gate2[:, :, 0:E1], gate2[:, :, 0:E1], tw[:, 0, :].unsqueeze(2).broadcast_to([TP, NT, E1]), ALU.subtract)\
                .then_inc(S("gate2_shift"), 1)
            dve.wait_ge(S("gate2_exp"), 1)
            own.link(dve.tensor_reduce(tw[:, 1, :], gate2[:, :, 0:E1], AX, ALU.add))
            own.link(dve.reciprocal(tw[:, 1, :], tw[:, 1, :]))
            tt(gate2[:, :, 0:E1], gate2[:, :, 0:E1], tw[:, 1, :].unsqueeze(2).broadcast_to([TP, NT, E1]), ALU.mult)\
                .then_inc(S("gate2_ready"), 1)
            dve.wait_ge(S("gate2_turned"), NT)
            dve.tensor_copy(gate_T[0:E1, :].rearrange("p (t n) -> p t n", t=NT), quads(4, E1)).then_inc(S("gate2_T_ready"), 1)
            bias_rows("ffn", x_R)
            gate2_flat = gate2[:].rearrange("p t n -> p (t n)")
            rows_of("ffn", x_R, 0, lambda t: gate2[:, t, 0:1], 0, False)
            rows_of("ffn", x_R, 1, lambda t: gate2[:, t, 1:2], 0, True)
            with dve.Fori(1, E1 // 2) as g:
                for u in range(2):
                    e = g * 2 + u
                    rows_of("ffn", x_R, e, lambda t: gate2_flat[:, bass.ds(e + 16 * t, 1)], 0, True)

        @block.tensor
        def _(pe):
            mm = pe.matmul

            def turn(name, src, bank):
                pe.wait_ge(S(f"{name}_ready"), 1)
                for t in range(NT):
                    for q in range(NC2):
                        dst = ps[:, bank + q, t * TP:(t + 1) * TP] if t < 4 else ps[:, bank + 2, q * TP:(q + 1) * TP]
                        pe.transpose(dst, src[:, t, q * 128:(q + 1) * 128], ident[0:TP, 0:TP])\
                            .then_inc(S("rows_turned"), 1)

            def turned(name):
                pe.wait_ge(S("T_by_act"), TURNS.index(name) + 1)
                pe.wait_ge(S("T_by_dve"), TURNS.index(name) + 1)

            def to_T(b, w, src_T, m0, K=NC2):
                for h in range(2):
                    for k in range(K):
                        last = mm(ps[:, b + h, 0:HALF], w[:, k, m0:m0 + 128], src_T[:, k, h * HALF:(h + 1) * HALF],
                                  start=(k == 0), stop=(k == K - 1))
                return last

            def to_R(dst, src, t, w, K=NC2):
                for k in range(K):
                    last = mm(dst, src(k)[:, t * TP:(t + 1) * TP], w(k), start=(k == 0), stop=(k == K - 1))
                return last

            pe.wait_ge(S("ident_ready"), 1)
            turn("n0", n_R, 5)

            def count_tile(u, j, first, last):
                pe.wait_ge(S("onehot_ready"), j + 1)
                for t in range(NT):
                    ins = mm(ps[0:TP, t, 0:HALF], oh_dst[:, u, t * TP:(t + 1) * TP], oh_src[:, u, 0:HALF],
                             start=first, stop=last, skip_group_check=not (first or last))
                ins.then_inc(S("onehot_used"), 1)
                return ins

            def edges(k):
                a, b = CHUNKS[k]
                if k:
                    pe.wait_ge(S("counts_out"), k)
                for u in range(4):
                    count_tile(u, a + u, u == 0, False)
                rest = 1 if b % 4 else 0
                with pe.Fori(a // 4 + 1, b // 4 - (1 - rest)) as g:
                    for u in range(4):
                        count_tile(u, g * 4 + u, False, False)
                if rest:
                    count_tile(0, b - 1, False, True)
                else:
                    for u in range(4):
                        count_tile(u, b - 4 + u, False, u == 3)

            edges(0)
            pe.wait_ge(S("w_mix_loaded"), 16)
            turned("n0")
            pe.wait_ge(S("pads_ready"), 6)
            for j in range(4):
                m, h = divmod(j, 2)
                if j == 3:
                    pe.wait_ge(S("mq_phi"), 1)
                for k in range(NC2):
                    last = mm(ps[:, 5 + j % 3, 0:HALF], w_mix[:, k, m * 128:(m + 1) * 128],
                              n_T[:, k, h * HALF:(h + 1) * HALF], start=(k == 0), stop=(k == 1))
                last.then_inc(S("mq_done"), 1)
            for t in range(NT):
                pe.wait_ge(S("mq_phi"), min(t + 2, 4))
                if t >= 3:
                    pe.wait_ge(S("mkv_phi"), t - 2)
                to_R(ps[0:TP, 5 + (4 + t) % 3, :], lambda k: n_T[:, k, :], t, lambda k: w_mix[:, k, D:3 * D])\
                    .then_inc(S("mkv_done"), 1)
            edges(1)
            pe.wait_ge(S("mkv_phi"), NT)
            pe.wait_ge(S("vones_ready"), 1)
            for q in range(2):
                for t in range(NT):
                    last = mm(ps[:, 5, q * 129:(q + 1) * 129], vs[:, t, q * 128:(q + 1) * 128], vones[:, t, q, :],
                              start=(t == 0), stop=(t == NT - 1))
                last.then_inc(S("mKV_done"), 1)
            pe.wait_ge(S("mKV_ready"), 1)
            for t in range(NT):
                if t >= 3:
                    pe.wait_ge(S("mt_out"), t - 2)
                for q in range(2):
                    last = mm(ps[0:TP, 5 + (1 + t) % 3, q * 132:(q + 1) * 132], q_T[:, q, t * TP:(t + 1) * TP],
                              kv_sb[:, q, :], start=True, stop=True)
                last.then_inc(S("mt_done"), 1)
            edges(2)
            turn("m1", h_R, 5)
            turned("m1")
            for j in range(4):
                m, h = divmod(j, 2)
                if j == 3:
                    pe.wait_ge(S("mh_gelu"), 1)
                for k in range(NC2):
                    last = mm(ps[:, 5 + (18 + j) % 3, 0:HALF], w_mix[:, k, 3 * D + m * 128:3 * D + (m + 1) * 128],
                              a_T[:, k, h * HALF:(h + 1) * HALF], start=(k == 0), stop=(k == 1))
                last.then_inc(S("mh_done"), 1)
            pe.wait_ge(S("mh_gelu"), 4)
            for t in range(NT):
                if t >= 3:
                    pe.wait_ge(S("my_out"), t - 2)
                to_R(ps[0:TP, 5 + (22 + t) % 3, 0:D], lambda k: b_T[:, k, :], t, lambda k: w_mix[:, k, 4 * D:5 * D])\
                    .then_inc(S("my_done"), 1)
            pe.wait_ge(S("counts_out"), 3)
            pe.wait_ge(S("my_out"), NT)

            def attention(i, first, last_layer):
                if not first:
                    pe.wait_ge(S("g_next"), i * 2)
                pe.wait_ge(S("gw_loaded"), i * 32 + 32)
                for m in range(NC2):
                    to_T(2 * m, gw[:, 0], n_T, m * 128).then_inc(S("g_q_done"), 1)
                for m in range(NC2):
                    to_T(4 + 2 * m, gw[:, 1], n_T, m * 128).then_inc(S("g_k_done"), 1)
                for t in range(NT):
                    if t == 0:
                        pe.wait_ge(S("g_q"), i * 2 + 1)
                    if t == 2:
                        pe.wait_ge(S("g_q"), i * 2 + 2)
                    if t == 4:
                        pe.wait_ge(S("g_k"), i * 2 + 1)
                    for k in range(NC2):
                        last = mm(ps[0:TP, t, :], n_T[:, k, t * TP:(t + 1) * TP],
                                  gw[:, 2:4, k, :], start=(k == 0), stop=(k == 1))
                    last.then_inc(S("g_rows_done"), 1)
                pe.wait_ge(S("g_k"), i * 2 + 2)

                def scores(n):
                    h, t = divmod(n, NT)
                    if n < 2:
                        pe.wait_ge(S("g_rows_read"), i * NT + 2 * n + 2)
                    else:
                        pe.wait_ge(S("g_max"), i * STEPS + n - 1)
                    p = 64 * (h % 2)
                    for b in range(2):
                        last = mm(ps[0:TP, 2 * (n % 2) + b, 0:HALF], q_T[p:p + 64, h // 2, t * TP:(t + 1) * TP],
                                  k_T[p:p + 64, h // 2, b * HALF:(b + 1) * HALF], start=True, stop=True)
                    last.then_inc(S("g_scores"), 1)

                def turn_probs(n):
                    pe.wait_ge(S("g_exp"), i * STEPS + n + 1)
                    if n:
                        pe.wait_ge(S("g_probs_T"), i * STEPS + n)
                    else:
                        pe.wait_ge(S("g_rows_read"), i * NT + NT)
                    for s in range(NT):
                        last = pe.transpose(quads(4)[:, s, :], probs[n % 3][:, s * TP:(s + 1) * TP], ident[0:TP, 0:TP])
                    last.then_inc(S("g_turned"), 1)

                def weigh(n):
                    h, t = divmod(n, NT)
                    if t == 0 and h >= 2:
                        pe.wait_ge(S("g_head"), i * GH + h - 1)
                    pe.wait_ge(S("g_probs_T"), i * STEPS + n + 1)
                    for s in range(NT):
                        last = mm(ps[0:TP, 6 + h % 2, t * 64:(t + 1) * 64], probs_T[n % 2][:, s, :],
                                  vs[:, s, h * 64:(h + 1) * 64], start=(s == 0), stop=(s == NT - 1))
                    last.then_inc(S("g_pv"), 1)

                scores(0)
                scores(1)
                for n in range(STEPS + 1):
                    if n < STEPS:
                        turn_probs(n)
                    if n + 2 < STEPS:
                        scores(n + 2)
                    if n:
                        weigh(n - 1)
                if last_layer:
                    return
                pe.wait_ge(S("g_out"), i * GH + GH)
                for t in range(NT):
                    for q in range(NC2):
                        dst = ps[:, q, t * TP:(t + 1) * TP] if t < 4 else ps[:, 2, q * TP:(q + 1) * TP]
                        pe.transpose(dst, h_R[:, t, q * 128:(q + 1) * 128], ident[0:TP, 0:TP])\
                            .then_inc(S("gh_turned"), 1)

            attention(0, True, False)
            with pe.Fori(1, GL - 1) as i:
                attention(i, False, False)
            attention(GL - 1, False, True)

            turn("xm", n_R, 0)
            turned("xm")
            pe.wait_ge(S("gates_loaded"), 48)
            for t in range(NT):
                last = to_R(ps[0:TP, 7, t * 16:(t + 1) * 16], lambda k: c_T[:, k, :], t, lambda k: gate_w[:, k, 0:16])
            last.then_inc(S("logits_done"), 1)

            def bias_rows(name, biases, n):
                for t in range(NT):
                    mm(ps[0:TP, 7 - t // 2, (t % 2) * D:(t % 2 + 1) * D],
                       gate_T[0:n, t * TP:(t + 1) * TP], biases[:], start=True, stop=True).then_inc(S(f"{name}_b_done"), 1)

            def moe_h(e, u, load, first):
                pe.wait_ge(S(f"w1_loaded{u}"), load)
                for m in range(4):
                    if not (first and m < 2):
                        pe.wait_ge(S("moe_relu"), e * 4 + m - 1)
                    to_T(2 * (m % 2), w1_moe[u], c_T, m * 128).then_inc(S("moe_h_done"), 1)

            def expert_y(name, hidden, e, w, first, K):
                for t in range(NT):
                    if t % 2 == 0 and not first:
                        pe.wait_ge(S(f"{name}_acc"), e * NT + min(t + 2, NT) - NT)
                    last = to_R(ps[0:TP, 4 + t // 2, (t % 2) * D:(t % 2 + 1) * D], hidden, t, w, K)
                    if t % 2 or t == NT - 1:
                        last.then_inc(S(f"{name}_y_done"), 1)

            def moe_y(e, u, load, first):
                pe.wait_ge(S(f"w2_loaded{u}"), load)
                pe.wait_ge(S("moe_relu"), e * 4 + 4)
                expert_y("moe", lambda k: hid[u][:, k, :], e, lambda k: w2_moe[u][:, k, :], first, 4)

            moe_h(0, 0, 16, True)
            pe.wait_ge(S("gate_ready"), 1)
            for t in range(NT):
                pe.transpose(quads(4, 16)[:, t, :], gate[:, t, :], ident[0:TP, 0:TP]).then_inc(S("gate_turned"), 1)
            pe.wait_ge(S("gate_T_ready"), 1)
            bias_rows("moe", moe_b2, E0)
            moe_h(1, 1, 16, False)
            pe.wait_ge(S("moe_bias_in"), NT)
            moe_y(0, 0, 16, True)
            with pe.Fori(1, E0 // 2) as g:
                moe_h(g * 2, 0, g * 16 + 16, False)
                moe_y(g * 2 - 1, 1, g * 16, False)
                moe_h(g * 2 + 1, 1, g * 16 + 16, False)
                moe_y(g * 2, 0, g * 16 + 16, False)
            moe_y(E0 - 1, 1, 8 * 16, False)

            turn("x2", n_R, 0)
            turned("x2")
            pe.wait_ge(S("w_m1_loaded"), 16)
            for m in range(NC2):
                to_T(4 + 2 * m, w_m1, n_T, m * 128).then_inc(S("m1_q_done"), 1)
            pe.wait_ge(S("ones_ready"), 1)
            for h in range(2):
                for s in range(NT):
                    last = mm(ps[:, h, 0:HALF], ones[:], count[:, s, h * HALF:(h + 1) * HALF],
                              start=(s == 0), stop=(s == NT - 1))
            last.then_inc(S("deg_done"), 1)

            def aggregate(l, src_R):
                for m in range(NC2):
                    for h in range(2):
                        for s in range(NT):
                            last = mm(ps[:, 2 * m + h, 0:HALF], src_R[:, s, m * 128:(m + 1) * 128],
                                      count[:, s, h * HALF:(h + 1) * HALF], start=(s == 0), stop=(s == NT - 1))
                    last.then_inc(S("agg_done"), 1)

            pe.wait_ge(S("inv_deg_ready"), 1)
            aggregate(0, n_R)
            for t in range(NT):
                if t == 0:
                    pe.wait_ge(S("m1_q"), 1)
                if t == 2:
                    pe.wait_ge(S("m1_q"), 2)
                if t == 4:
                    pe.wait_ge(S("m1_kv"), 1)
                to_R(ps[0:TP, 4 + t % 4, :], lambda k: n_T[:, k, :], t, lambda k: w_m1[:, k, D:3 * D])\
                    .then_inc(S("m1_kv_done"), 1)

            def graph_rows(l):
                pe.wait_ge(S("agg_out"), 2 * l + 2)
                for t in range(NT):
                    if t == 4:
                        pe.wait_ge(S("g1_h"), l * NT + 1)
                    to_R(ps[0:TP, t % 4, 0:D], lambda k: a_T[:, k, :], t, lambda k: w_g1[:, k, l * D:(l + 1) * D])\
                        .then_inc(S("g1_h_done"), 1)

            pe.wait_ge(S("m1_kv"), NT)
            for q in range(2):
                for t in range(NT):
                    last = mm(ps[:, 5, q * 128:(q + 1) * 128], vs[:, t, q * 128:(q + 1) * 128],
                              vs[:, t, D + q * 128:D + (q + 1) * 128], start=(t == 0), stop=(t == NT - 1))
                last.then_inc(S("m1_at_done"), 1)
            pe.wait_ge(S("w_g1_loaded"), 16)
            graph_rows(0)
            pe.wait_ge(S("m1_attn"), 4)
            for q in range(2):
                pe.transpose(ps[:, 6, q * 128:(q + 1) * 128], at_sb[:, q, :], ident[:]).then_inc(S("at_turned"), 1)
            pe.wait_ge(S("at_T_ready"), 1)
            for t in range(NT):
                if t == 4:
                    pe.wait_ge(S("m1_xf"), 1)
                for q in range(2):
                    last = mm(ps[0:TP, 4 + t % 4, q * 128:(q + 1) * 128], q_T[:, q, t * TP:(t + 1) * TP],
                              at_T[:, q, :], start=True, stop=True)
                last.then_inc(S("m1_xf_done"), 1)
            pe.wait_ge(S("g1_x"), 1)
            for t in range(NT):
                for q in range(NC2):
                    dst = ps[:, q, t * TP:(t + 1) * TP] if t < 4 else ps[:, 2, q * TP:(q + 1) * TP]
                    pe.transpose(dst, y_R[:, t, q * 128:(q + 1) * 128], ident[0:TP, 0:TP]).then_inc(S("rows_turned"), 1)
            turn("y1", h_R, 4)
            turned("g1")
            aggregate(1, y_R)
            turned("y1")
            for m in range(HM // 128):
                if m >= 2:
                    pe.wait_ge(S("fc1_gelu"), m - 1)
                to_T(4 + 2 * (m % 2), w_m1, b_T, 3 * D + m * 128).then_inc(S("fc1_done"), 1)
            graph_rows(1)
            pe.wait_ge(S("w_fc2_loaded"), 16)
            pe.wait_ge(S("fc1_gelu"), HM // 128)
            for t in range(NT):
                if t == 4:
                    pe.wait_ge(S("fc2_out"), 1)
                to_R(ps[0:TP, 4 + t % 4, 0:D], lambda k: (hid[0][:, k, :] if k < 4 else hid[1][:, k - 4, :]), t,
                     lambda k: w_fc2[:, k, :], HM // 128).then_inc(S("fc2_done"), 1)

            turn("x3", n_R, 0)
            turned("x3")
            for t in range(NT):
                last = to_R(ps[0:TP, 7, t * E1:(t + 1) * E1], lambda k: c_T[:, k, :], t, lambda k: gate_w[:, k, 16:16 + E1])
            last.then_inc(S("logits2_done"), 1)

            def ffn_h(e, u, k, first):
                for m in range(NC2):
                    if k == 1:
                        if m == 0:
                            pe.wait_ge(S("ffn_relu"), e * 4 + 2)
                    elif not first:
                        pe.wait_ge(S("ffn_relu"), e * 4 + m - 1)
                    src = c_T if k == 0 else hid[u]
                    to_T(2 * m, w3_ffn[u][k], src, m * 128).then_inc(S("ffn_h_done"), 1)

            def ffn_y(e, u, first):
                pe.wait_ge(S("ffn_relu"), e * 4 + 4)
                expert_y("ffn", lambda k: hid[u][:, 2 + k, :], e, lambda k: w3_ffn[u][2][:, k, :], first, 2)

            pe.wait_ge(S("ffn_loaded0"), 48)
            ffn_h(0, 0, 0, True)
            pe.wait_ge(S("gate2_ready"), 1)
            for t in range(NT):
                pe.transpose(quads(4, E1)[:, t, :], gate2[:, t, 0:E1], ident[0:TP, 0:TP]).then_inc(S("gate2_turned"), 1)
            pe.wait_ge(S("gate2_T_ready"), 1)
            bias_rows("ffn", moe_bo, E1)
            ffn_h(0, 0, 1, True)
            pe.wait_ge(S("ffn_loaded1"), 48)
            ffn_h(1, 1, 0, False)
            pe.wait_ge(S("ffn_bias_in"), NT)
            ffn_y(0, 0, True)
            ffn_h(1, 1, 1, False)
            with pe.Fori(1, E1 // 2) as g:
                pe.wait_ge(S("ffn_loaded0"), g * 48 + 48)
                ffn_h(g * 2, 0, 0, False)
                ffn_y(g * 2 - 1, 1, False)
                ffn_h(g * 2, 0, 1, False)
                pe.wait_ge(S("ffn_loaded1"), g * 48 + 48)
                ffn_h(g * 2 + 1, 1, 0, False)
                ffn_y(g * 2, 0, False)
                ffn_h(g * 2 + 1, 1, 1, False)
            ffn_y(E1 - 1, 1, False)


def kernel(**inputs):
    import numpy as np
    import concourse.bacc as bacc
    from concourse import mybir as mb
    from concourse.bass_utils import run_bass_kernel_spmd

    a = {k: np.asarray(v) for k, v in inputs.items()}

    def columns(v):
        return np.reshape(v, (-1, 128)).T

    gates = np.zeros((D,), np.float32)
    gates[0:E0] = a["L0_ffn_gate_b"]
    gates[E0:E0 + E1] = a["L1_ffn_br"]
    b_qkv = a["L1_mix_b_qkv"]
    by_name = {
        "mix_ln1_g": a["L0_mix_ln1_g"], "mix_ln1_b": a["L0_mix_ln1_b"], "mix_b2": a["L0_mix_b2"],
        "mix_ln2_g": a["L0_mix_ln2_g"], "mix_ln2_b": a["L0_mix_ln2_b"],
        "moe_gamma": a["L0_ffn_gamma"], "moe_beta": a["L0_ffn_beta"],
        "g1_b0": a["L1_gnn_b0"], "g1_g0": a["L1_gnn_g0"], "g1_beta0": a["L1_gnn_beta0"],
        "g1_b1": a["L1_gnn_b1"], "g1_g1": a["L1_gnn_g1"], "g1_beta1": a["L1_gnn_beta1"],
        "m1_bk": b_qkv[D:2 * D], "m1_bv": b_qkv[2 * D:3 * D],
        "m1_norm_g": a["L1_mix_norm_g"], "m1_norm_b": a["L1_mix_norm_b"], "m1_bfc2": a["L1_mix_b_fc2"],
        "gates": gates,
        "mix_b1": a["L0_mix_b1"], "m1_bq": b_qkv[0:D], "m1_bfc1": a["L1_mix_b_fc1"], "moe_b1": a["L0_ffn_b1"],
        **{k: a[f"L1_ffn_{k}"] for k in ("b1", "g1", "be1", "m1", "v1", "b2", "g2", "be2", "m2", "v2")},
    }
    nothing = np.zeros((1, D), np.float32)
    bn_g = np.concatenate([a["L0_gnn_bn_gamma"], nothing])
    bn_b = np.concatenate([a["L0_gnn_bn_beta"], nothing])
    arrays = {
        "x": a["x"], "src": a["src"], "dst": a["dst"],
        "rows": np.stack([by_name[k] for k in ROWS]),
        "cols": np.concatenate([columns(by_name[k]) for k, _ in COLS], 1),
        "gw": np.stack([a["L0_gnn_Wq"], a["L0_gnn_Wk"], a["L0_gnn_Wv"], a["L0_gnn_Ws"]], 1),
        "gbias": np.concatenate([a["L0_gnn_bv"], a["L0_gnn_bs"]], 1),
        "gcols": np.concatenate([columns(v[i]) for i in range(GL)
                                 for v in (a["L0_gnn_bq"], a["L0_gnn_bk"], bn_g, bn_b)], 1),
        "w_mix": np.concatenate([a["L0_mix_Wqkv"].T, a["L0_mix_W1"].T, a["L0_mix_W2"].T], 1),
        "w_g1": np.concatenate([a["L1_gnn_W0"].T, a["L1_gnn_W1"].T], 1),
        "w_m1": np.concatenate([a["L1_mix_w_qkv"], a["L1_mix_w_fc1"]], 1),
        "w_fc2": a["L1_mix_w_fc2"],
        "gate_w": np.concatenate([a["L0_ffn_gate_w"], a["L1_ffn_Wr"]], 1),
        "moe_w1": a["L0_ffn_w1"], "moe_w2": a["L0_ffn_w2"], "moe_b2": a["L0_ffn_b2"],
        "ffn_w": np.stack([a["L1_ffn_W1"], a["L1_ffn_W2"], a["L1_ffn_Wo"]], 1), "moe_bo": a["L1_ffn_bo"],
    }
    arrays = {f"in_{k}": np.ascontiguousarray(v) for k, v in arrays.items()}
    nc = bacc.Bacc("TRN2", target_bir_lowering=False, num_devices=1)
    A = {k[3:]: nc.dram_tensor(k, v.shape, mb.dt.from_np(v.dtype), kind="ExternalInput").ap() for k, v in arrays.items()}
    out = nc.dram_tensor("out_x", (N, D), mb.dt.float32, kind="ExternalOutput").ap()
    program(nc, A, out)
    r = run_bass_kernel_spmd(nc, [arrays], core_ids=[0])
    return r.results[0]["out_x"]
```

```python
from contextlib import ExitStack

import concourse.bass as bass
from concourse import mybir

ALU = mybir.AluOpType
ACT = mybir.ActivationFunctionType
F32 = mybir.dt.float32
F16 = mybir.dt.float16
F32R = mybir.dt.float32r
BF16 = mybir.dt.bfloat16
I32 = mybir.dt.int32
I16 = mybir.dt.int16
U32 = mybir.dt.uint32
AX = mybir.AxisListType.X

N = 625
TP = 125
NT = N // TP
D = 256
NC2 = D // 128
HALF = 314
NP = 2 * HALF
EDGES = 10625
ET = EDGES // TP
E0, F0 = 16, 512
SLOT = 128
MT = 2 * N // SLOT + E0
TB = 4
E1 = 8
HM = 3 * D
GL = 3
GH = 4
STEPS = GH * NT
ROWS_BANK = [2, 3, 4, 5, 7]
MASK = -8.0e30
HAS_EDGE = -1.0e29
FIELD = 4096
CHUNKS = [(0, 32), (32, 64), (64, ET)]

ROWS = ["mix_ln1_g", "mix_ln1_b", "mix_b2", "mix_ln2_g", "mix_ln2_b", "moe_gamma", "moe_beta",
        "g1_b0", "g1_g0", "g1_beta0", "g1_b1", "g1_g1", "g1_beta1",
        "m1_bk", "m1_bv", "m1_norm_g", "m1_norm_b", "m1_bfc2", "gates"]
COLS = [("mix_b1", 2), ("m1_bq", 2), ("m1_bfc1", 6)] + \
       [(k, 2 * E1) for k in ("b1", "g1", "be1", "m1", "v1", "b2", "g2", "be2", "m2", "v2")]
NCOLS = sum(n for _, n in COLS)


NORMS = ["ln0", "ln1", "ln2", "lnm", "lny", "lnx", "gn0", "lnh", "gn1", "lnf"]
TURNS = ["n0", "m1", "xm", "x2", "g1", "y1", "x3"]


class Steps:

    def __init__(self, eng, sem, base=0):
        self.eng, self.sem, self.base, self.n = eng, sem, base, 0

    def step(self, ins):
        ins.then_inc(self.sem, 1)
        self.n += 1

    def settle(self):
        self.eng.wait_ge(self.sem, self.base + self.n)

    def link(self, ins):
        self.step(ins)
        self.settle()


def program(nc, A, out):
    with ExitStack() as ctx:
        def sb(name, shape, dt=F32):
            return ctx.enter_context(nc.sbuf_tensor(name, shape, dt))

        sems = {}

        def S(name):
            if name not in sems:
                sems[name] = ctx.enter_context(nc.semaphore(name))
            return sems[name]

        ps = ctx.enter_context(nc.psum_tensor("ps", [128, 8, 512], F32))

        def pair(b, rows=128):
            return ps[0:rows, b:b + 2, 0:HALF]

        def quads(b, rows=TP):
            return ps[0:rows, b:b + 2, :].rearrange("p b n -> p (b n)")[:, 0:640]\
                .rearrange("p (t n) -> p t n", n=128)[:, :, 0:TP]

        def halves(ap):
            return ap.rearrange("p (b n) -> p b n", b=2)

        ident = sb("ident", [128, 128])
        node_ids = sb("node_ids", [TP, N], I16)
        expert_ids = sb("expert_ids", [TP, 16])
        neg_half = sb("neg_half", [128, 2 * E1 * 2])
        ones = sb("ones", [TP, 128])
        minus_one = sb("minus_one", [TP, 1])
        head_mask = sb("head_mask", [128, 4, 32])
        head_cols = sb("head_cols", [128, 4])

        rows = sb("rows", [TP, len(ROWS), D])
        cols = sb("cols", [128, NCOLS])
        row = {k: rows[:, i, :] for i, k in enumerate(ROWS)}
        col, at = {}, 0
        for k, n in COLS:
            col[k] = (at, n)
            at += n
        gw = sb("gw", [128, 4, NC2, D])
        gbias = sb("gbias", [TP, 2 * D])
        gcols = sb("gcols", [128, GL * 8])
        w_g1 = sb("w_g1", [128, NC2, 2 * D])
        w_m1 = sb("w_m1", [128, NC2, 3 * D + HM])
        w_mix = w_m1[:, :, 0:5 * D]
        gate_w = sb("gate_w", [128, NC2, E0 + E1])
        moe_b2 = sb("moe_b2", [E0, D])
        moe_bo = sb("moe_bo", [E1, D])
        ring = sb("ring", [128, 2, 8 * D])
        w3_ffn = [[ring[:, u, k * 2 * D:(k + 1) * 2 * D].rearrange("p (c n) -> p c n", c=2)
                   for k in range(3)] for u in range(2)]

        def R(name):
            return sb(name, [TP, NT, D])

        def T(name):
            return sb(name, [128, NC2, NP])

        x_R, n_R, mix_R, h_R, y_R = [R(k) for k in ("x_R", "n_R", "mix_R", "h_R", "y_R")]
        with nc.sbuf_tensor("parts", [128, 2 * GH + 2, NP], F32R) as parts:
            q_parts = [parts[:, h, :] for h in range(GH)]
            k_parts = [parts[:, GH + h, :] for h in range(GH)]
            k_lo = [parts[:, 2 * GH + k, :] for k in range(2)]
        q_T, k_T, b_T, c_T = [T(k) for k in ("q_T", "k_T", "b_T", "c_T")]
        big1 = sb("big1", [128, 5 * NP])
        n_T, a_T = T("n_T"), T("a_T")
        count = sb("count", [TP, NT, NP])
        logc_all = sb("logc", [128, NT * NP])
        logc = logc_all[0:TP].rearrange("p (t n) -> p t n", t=NT)
        vones = logc_all[0:TP, 0:NT * 258].rearrange("p (t c n) -> p t c n", t=NT, c=2)
        w_fc2 = logc_all[:, 0:HM // 128 * D].rearrange("p (c n) -> p c n", n=D)
        big2 = sb("big2", [128, 4 * NP + 640])
        idx = sb("idx", [TP, 2, ET], I32)
        idf = sb("idf", [TP, 4, ET])
        oh_dst_all = sb("oh_dst", [128, 4, N + 1], BF16)
        oh_dst = oh_dst_all[0:TP]
        small = oh_dst_all.rearrange("p a n -> p (a n)").bitcast(F32)
        oh_src = sb("oh_src", [TP, 4, HALF], BF16)
        vs = sb("vs", [TP, NT, 2 * D])
        stats = {k: (sb(f"st_{k}", [TP, NT, 6]), sb(f"mv_{k}", [TP, NT, 2]),
                     sb(f"ve_{k}", [TP, NT]), sb(f"rs_{k}", [TP, NT]))
                 for k in NORMS}

        cnt_new = big1[0:TP, 0:NT * HALF].bitcast(I32).rearrange("p (t n) -> p t n", t=NT)
        cnt_lo = big1[0:TP, NT * HALF:2 * NT * HALF].bitcast(I32).rearrange("p (t n) -> p t n", t=NT)
        cnt_hi = big2[0:TP, 0:NT * HALF].bitcast(I32).rearrange("p (t n) -> p t n", t=NT)
        cnt_tmp = big2[0:TP, NT * HALF:2 * NT * HALF].bitcast(I32).rearrange("p (t n) -> p t n", t=NT)
        probs = [big1[0:TP, k * NP:(k + 1) * NP] for k in range(2, 5)]
        probs_T = [big2[0:TP, k * 640:k * 640 + N].rearrange("p (s n) -> p s n", s=NT) for k in range(2)]
        tile_x = [big1[:, k * D:(k + 1) * D] for k in range(TB)]
        tile_xT = [big1[:, (TB + k) * D:(TB + k + 1) * D].rearrange("p (c n) -> p c n", c=2) for k in range(2)]
        tile_y = [big1[:, (TB + 2 + k) * D:(TB + 3 + k) * D] for k in range(2)]
        tile_h = [big2[:, k * 512:(k + 1) * 512].rearrange("p (m n) -> p m n", m=4) for k in range(2)]
        gw_flat = gw[:].rearrange("p m c n -> p (m c n)")
        W = 2 * F0
        w1_moe = [b.rearrange("p (c n) -> p c n", c=2) for b in
                  (ring[:, 0, 0:W], ring[:, 1, 0:W], gw_flat[:, 0:W], logc_all[:, HM // 128 * D:HM // 128 * D + W])]
        w2_moe = [b.rearrange("p (c n) -> p c n", c=4) for b in
                  (ring[:, 0, W:2 * W], ring[:, 1, W:2 * W], gw_flat[:, W:2 * W], big2[:, 1856:1856 + W])]
        hid = [b[:, 0:4 * NP].rearrange("p (m n) -> p m n", m=4) for b in (big1, big2)]

        kv_sb = sb("kv_sb", [128, 2, 132])
        ek = sb("ek", [TP, 2, D])
        eq = sb("eq", [128, 2, HALF])
        zden = sb("zden", [TP, 2, NT, 8])
        gmax = sb("gmax", [TP, STEPS])
        gneg = sb("gneg", [TP, STEPS])
        gden = sb("gden", [TP, STEPS])
        grec = sb("grec", [TP, STEPS])
        att = sb("att", [TP, NT, 64])
        bst = sb("bst", [128, 2, 2, 6])
        bmv = sb("bmv", [128, 2, 2])
        bve = sb("bve", [128, 2])
        brs = sb("brs", [128, 2])
        bsc = sb("bsc", [128, 3, 2])
        lg = sb("lg", [TP, NT, 16])
        top = sb("top", [TP, NT, 8])
        topi = sb("topi", [TP, NT, 8], U32)
        topf = sb("topf", [TP, NT, 2])
        tw = sb("tw", [TP, 4, NT])
        pick = big2[0:TP, 1536:1696].rearrange("p (k t e) -> p k t e", k=2, t=NT)
        picked = sb("picked", [TP, NT, 16], BF16)
        before = sb("before", [TP, TP], BF16)
        ones_b = sb("ones_b", [TP, 128], BF16)
        tiles = sb("tiles", [TP, 3, 32])
        tiles_i = sb("tiles_i", [TP, 16], I32)
        place = big2[0:TP, 1696:1856].rearrange("p (k t e) -> p k t e", k=2, t=NT)
        slot = sb("slot", [TP, 3, 2 * NT])
        slot_i = sb("slot_i", [TP, 3, 2 * NT], I32)
        row_hot = big2[0:TP, 0:NT * SLOT].bitcast(F16).rearrange("p (k n) -> p k n", k=2 * NT)
        tile_hot = big2[0:TP, NT * SLOT:NT * (SLOT + MT)].bitcast(F16).rearrange("p (k n) -> p k n", k=2 * NT)
        ids_i = sb("ids_i", [128, SLOT], I32)
        row_ids = sb("row_ids", [TP, SLOT])
        tile_ids = sb("tile_ids", [TP, MT])
        choice_ids = sb("choice_ids", [TP, 2 * NT])
        spare_ids = sb("spare_ids", [128, MT])
        own_tile = big2[0:1, 1024:1024 + MT * 16].rearrange("p (j e) -> p j e", j=MT)
        tile_e = sb("tile_e", [1, MT])
        tile_expert = sb("tile_expert", [1, MT], I32)
        slot_m = sb("slot_m", [128, 2, MT])
        from_row = sb("from_row", [128, MT], I32)
        to_row = sb("to_row", [128, MT], I32)
        row_at = sb("row_at", [128, TB + 2], I32)
        b1_moe = sb("b1_moe", [128, TB, 4])
        gate = sb("gate", [TP, NT, 16])
        gate2 = sb("gate2", [TP, NT, 16])
        gate_T = eq[0:16].rearrange("p a n -> p (a n)")[:, 0:N]
        inv_deg = sb("inv_deg", [128, NP])
        at_sb, at_T = [small[:, k * 256:(k + 1) * 256].rearrange("p (c n) -> p c n", c=2) for k in range(2)]
        bn_v, bn_r, bn_s, bn_b, bn_t = [small[:, 512 + k * 4 * E1:512 + (k + 1) * 4 * E1] for k in range(5)]
        at_m = small[:, 704:720].rearrange("p (k n) -> p k n", k=4)

        def c(name, j=0, n=1):
            return cols[:, col[name][0] + j:col[name][0] + j + n]

        def wide(r):
            return r.unsqueeze(1).broadcast_to([TP, NT, D])

        moe_in = nc.dram_tensor("moe_in", (N, D), F32, kind="Internal").ap()
        moe_out = nc.dram_tensor("moe_out", (1 + 2 * N + MT * SLOT, D), F32, kind="Internal").ap()

        block = ctx.enter_context(nc.Block())

        @block.sync
        def _(sp):
            sp.dma_start(x_R[:], A["x"].rearrange("(t p) f -> p t f", p=TP)).then_inc(S("x_loaded"), 16)
            sp.dma_start(idx[:, 0, :], A["src"].rearrange("(p j) -> p j", p=TP)).then_inc(S("edges_loaded"), 16)
            sp.dma_start(idx[:, 1, :], A["dst"].rearrange("(p j) -> p j", p=TP)).then_inc(S("edges_loaded"), 16)
            sp.dma_start(w_mix, A["w_mix"].rearrange("(c p) n -> p c n", p=128)).then_inc(S("w_mix_loaded"), 16)
            sp.dma_start(rows[:], A["rows"].unsqueeze(0).broadcast_to([TP, len(ROWS), D])).then_inc(S("rows_loaded"), 16)
            sp.dma_start(cols[:], A["cols"]).then_inc(S("cols_loaded"), 16)

            def attention_weights(i, first):
                if not first:
                    sp.wait_ge(S("g_rows_read"), i * NT)
                sp.dma_start(gw[:], A["gw"][bass.ds(i, 1)].rearrange("a m (c p) n -> p (a m) c n", p=128))\
                    .then_inc(S("gw_loaded"), 16)
                sp.dma_start(gbias[:], A["gbias"][bass.ds(i, 1)].broadcast_to([TP, 2 * D]))\
                    .then_inc(S("gw_loaded"), 16)

            sp.dma_start(gcols[:], A["gcols"]).then_inc(S("gcols_loaded"), 16)
            attention_weights(0, True)
            sp.dma_start(w_g1[:], A["w_g1"].rearrange("(c p) n -> p c n", p=128)).then_inc(S("w_g1_loaded"), 16)
            sp.dma_start(gate_w[:], A["gate_w"].rearrange("(c p) n -> p c n", p=128)).then_inc(S("gates_loaded"), 16)
            sp.dma_start(moe_b2[:], A["moe_b2"]).then_inc(S("gates_loaded"), 16)
            sp.dma_start(moe_bo[:], A["moe_bo"]).then_inc(S("gates_loaded"), 16)
            sp.wait_ge(S("my_done"), NT)
            sp.dma_start(w_m1[:], A["w_m1"].rearrange("(c p) n -> p c n", p=128)).then_inc(S("w_m1_loaded"), 16)
            with sp.Fori(1, GL) as i:
                attention_weights(i, False)
            sp.wait_ge(S("g_max"), GL * STEPS)
            sp.dma_start(w_fc2, A["w_fc2"].rearrange("(c p) n -> p c n", p=128)).then_inc(S("w_fc2_loaded"), 16)
            sp.wait_ge(S("xm_ready"), 1)
            sp.dma_start(moe_in.rearrange("(t p) f -> p t f", p=TP), n_R[:]).then_inc(S("moe_in_stored"), 16)
            sp.wait_ge(S("tile_expert_ready"), 1)

            def tile_weights(j, u, first):
                e = sp.value_load(tile_expert[0:1, bass.ds(j, 1)], min_val=0, max_val=E0 - 1)
                if not first:
                    sp.wait_ge(S("moe_y_done"), j - (TB - 1))
                sp.dma_start(w1_moe[u], A["moe_w1"][bass.ds(e, 1)].rearrange("a (c p) n -> p (a c) n", p=128))\
                    .then_inc(S(f"w_loaded{u}"), 16)
                sp.dma_start(w2_moe[u], A["moe_w2"][bass.ds(e, 1)].rearrange("a (c p) n -> p (a c) n", p=128))\
                    .then_inc(S(f"w_loaded{u}"), 16)
                sp.dma_start(b1_moe[:, u, :], A["moe_b1"][bass.ds(e, 1)].rearrange("a p m -> (a p) m"))\
                    .then_inc(S(f"w_loaded{u}"), 16)

            for j in range(TB):
                tile_weights(j, j, True)
            with sp.Fori(1, MT // TB) as g:
                for u in range(TB):
                    tile_weights(g * TB + u, u, False)
            tile_weights(MT - 1, 0, False)
            sp.wait_ge(S("moe_scattered0"), 16 * (MT - MT // 2))
            sp.wait_ge(S("moe_scattered1"), 16 * (MT // 2))
            sp.dma_start(vs[:].rearrange("p t (a f) -> p (t a) f", a=2),
                         moe_out[1:1 + 2 * N].rearrange("(k p) f -> p k f", p=TP)).then_inc(S("choices_loaded"), 16)

            def ffn_weights(e, u):
                sp.dma_start(w3_ffn[u][0], A["ffn_w"][bass.ds(e, 1), 0].rearrange("a (c p) n -> p (a c) n", p=128))\
                    .then_inc(S(f"ffn_loaded{u}"), 16)
                sp.dma_start(w3_ffn[u][1], A["ffn_w"][bass.ds(e, 1), 1].rearrange("a (c p) n -> p (a c) n", p=128))\
                    .then_inc(S(f"ffn_loaded{u}"), 16)
                sp.dma_start(w3_ffn[u][2], A["ffn_w"][bass.ds(e, 1), 2].rearrange("a (c p) n -> p (a c) n", p=128))\
                    .then_inc(S(f"ffn_loaded{u}"), 16)

            sp.wait_ge(S("moe_y_done"), MT)
            for e in range(2):
                ffn_weights(e, e)
            with sp.Fori(1, E1 // 2) as g:
                for u in range(2):
                    sp.wait_ge(S("ffn_y_done"), (g * 2 + u - 1) * 3)
                    ffn_weights(g * 2 + u, u)
            sp.wait_ge(S("ffn_acc"), E1 * NT)
            sp.dma_start(out.rearrange("(t p) f -> p t f", p=TP), x_R[:]).then_inc(S("stored"), 16)
            sp.wait_ge(S("stored"), 16)

        @block.gpsimd
        def _(pool):
            own = Steps(pool, S("pool_steps"))

            def rstd(name):
                st, mv, ve, rs = stats[name]
                pool.wait_ge(S("norm_var"), NORMS.index(name) + 1)
                pool.tensor_tensor(rs[:], ve[:], neg_half[0:TP, 0:NT], ALU.pow).then_inc(S("norm_rstd"), 1)

            own.step(pool.memset(minus_one[:], -1.0))
            own.link(pool.memset(neg_half[:], -0.5))
            rstd("ln0")
            own.step(pool.memset(ident[:], 0.0))
            own.step(pool.memset(head_mask[:], 1.0))
            own.link(pool.memset(head_cols[:], 1.0))
            pool.affine_select(out=ident[:], in_=ident[:], compare_op=ALU.not_equal, fill=1.0, base=0,
                               pattern=[[-1, 128]], channel_multiplier=1).then_inc(S("ident_ready"), 1)
            pool.iota(node_ids[:], pattern=[[1, N]], base=0, channel_multiplier=0).then_inc(S("ids_ready"), 1)
            for t in (n_T, a_T):
                pool.memset(t[:, :, N:NP], 0.0).then_inc(S("pads_ready"), 1)
            pool.memset(vones[:, :, :, 128:129], 1.0).then_inc(S("vones_ready"), 1)
            own.step(pool.affine_select(out=head_mask[:], in_=head_mask[:], compare_op=ALU.is_ge, fill=0.0, base=0,
                                        pattern=[[-32, 4], [0, 32]], channel_multiplier=1))
            own.link(pool.affine_select(out=head_cols[:], in_=head_cols[:], compare_op=ALU.is_ge, fill=0.0, base=0,
                                        pattern=[[-32, 4]], channel_multiplier=1))
            pool.affine_select(out=head_mask[:], in_=head_mask[:], compare_op=ALU.is_ge, fill=0.0, base=31,
                               pattern=[[32, 4], [0, 32]], channel_multiplier=-1).then_inc(S("masks_ready"), 1)
            pool.affine_select(out=head_cols[:], in_=head_cols[:], compare_op=ALU.is_ge, fill=0.0, base=31,
                               pattern=[[32, 4]], channel_multiplier=-1).then_inc(S("masks_ready"), 1)
            for ids, pattern, base, down in ((expert_ids, [[1, 16]], 0, 0), (row_ids, [[1, SLOT]], 0, 0),
                                             (tile_ids, [[1, MT]], 0, 0), (choice_ids, [[TP, 2 * NT]], 1, 1),
                                             (spare_ids, [[SLOT, MT]], 1 + 2 * N, 1)):
                p, n = ids.shape
                own.link(pool.iota(ids_i[0:p, 0:n], pattern=pattern, base=base, channel_multiplier=down))
                own.link(pool.tensor_copy(ids[:], ids_i[0:p, 0:n]))
            own.step(pool.memset(ones_b[:], 1.0))
            own.step(pool.memset(tiles[:], 0.0))
            own.link(pool.memset(before[:], 0.0))
            pool.affine_select(out=before[:], in_=before[:], compare_op=ALU.is_ge, fill=1.0, base=0,
                               pattern=[[-1, TP]], channel_multiplier=1).then_inc(S("routing_ids_ready"), 1)
            pool.memset(ones[:], 1.0).then_inc(S("ones_ready"), 1)
            rstd("ln1")
            pool.wait_ge(S("counts_out"), 3)
            pool.memset(at_sb[:], 0.0).then_inc(S("at_zero"), 1)

            pool.wait_ge(S("bn_var"), 2)
            pool.tensor_tensor(bn_r[:], bn_v[:], neg_half[:, 0:4 * E1], ALU.pow).then_inc(S("bn_rstd"), 1)

            def attention(i, last):
                for n in range(STEPS):
                    pool.wait_ge(S("g_max"), i * STEPS + n + 1)
                    pool.tensor_tensor(gneg[:, n:n + 1], gmax[:, n:n + 1], minus_one[:], ALU.mult)\
                        .then_inc(S("g_neg"), 1)
                    if last and n == 6:
                        rstd("ln2")
                if not last:
                    pool.wait_ge(S("g_var"), i + 1)
                    pool.tensor_tensor(brs[:], bve[:], neg_half[:, 0:2], ALU.pow).then_inc(S("g_rstd"), 1)

            with pool.Fori(0, GL - 1) as i:
                attention(i, False)
            attention(GL - 1, True)
            rstd("lnm")
            for t in (k_T, b_T, c_T):
                pool.memset(t[:, :, N:NP], 0.0).then_inc(S("pads_ready"), 1)
            pool.wait_ge(S("rows_placed"), 2)
            pool.wait_ge(S("moe_in_stored"), 16)

            def gather(j, u):
                pool.tensor_copy(row_at[:, u:u + 1], from_row[:, bass.ds(j, 1)]).then_inc(S("gather_at"), 1)
                pool.wait_ge(S("gather_at"), j + 1)
                pool.nop(nofuse=True)
                pool.indirect_dma_start(tile_x[u], None, moe_in,
                                        bass.IndirectOffsetOnAxis(ap=row_at[:, u:u + 1].bitcast(U32), axis=0))\
                    .then_inc(S(f"moe_gathered{u}"), 16)

            def scatter(j, u):
                pool.wait_ge(S("moe_y_out"), j + 1)
                pool.nop(nofuse=True)
                pool.tensor_copy(row_at[:, TB + u:TB + 1 + u], to_row[:, bass.ds(j, 1)]).then_inc(S("scatter_at"), 1)
                pool.wait_ge(S("scatter_at"), j + 1)
                pool.nop(nofuse=True)
                pool.indirect_dma_start(moe_out, bass.IndirectOffsetOnAxis(ap=row_at[:, TB + u:TB + 1 + u].bitcast(U32), axis=0),
                                        tile_y[u], None).then_inc(S(f"moe_scattered{u}"), 16)

            for j in range(TB):
                gather(j, j)
            with pool.Fori(0, MT // TB - 1) as g:
                for u in range(TB):
                    scatter(g * TB + u, u % 2)
                    gather(g * TB + (u + TB), u)
            scatter(MT - 1 - TB, 0)
            gather(MT - 1, 0)
            for j in range(MT - TB, MT):
                scatter(j, j % 2)
            for name in ("lny", "lnx", "gn0", "lnh", "gn1", "lnf"):
                rstd(name)

        @block.scalar
        def _(act):
            def evac_T(name, dst, bank):
                act.wait_ge(S("rows_turned"), 10 * TURNS.index(name) + 10)
                act.activation(dst[:, :, 0:4 * TP], ps[:, bank:bank + 2, 0:4 * TP], ACT.Identity)\
                    .then_inc(S("T_by_act"), 1)

            evac_T("n0", n_T, 5)

            def counts(k):
                act.wait_ge(S("onehot_used"), CHUNKS[k][1])
                if k:
                    act.wait_ge(S("counts_added"), k)
                act.activation(cnt_new, ps[0:TP, 0:NT, 0:HALF], ACT.Copy).then_inc(S("counts_out"), 1)

            counts(0)
            for j in range(4):
                act.wait_ge(S("mq_done"), j + 1)
                if j >= 2:
                    act.wait_ge(S("mq_phi"), j - 1)
                act.activation(eq[:, j % 2, :], ps[:, 5 + j % 3, 0:HALF], ACT.Exp).then_inc(S("mq_exp"), 1)
            for t in range(NT):
                act.wait_ge(S("mkv_done"), t + 1)
                if t >= 2:
                    act.wait_ge(S("mkv_phi"), t - 1)
                act.activation(ek[:, t % 2, :], ps[0:TP, 5 + (4 + t) % 3, 0:D], ACT.Exp)
                act.activation(vones[:, t, :, 0:128],
                               ps[0:TP, 5 + (4 + t) % 3, D:2 * D].rearrange("p (c n) -> p c n", c=2), ACT.Copy)\
                    .then_inc(S("mkv_exp"), 1)
            counts(1)
            evac_T("m1", a_T, 5)
            counts(2)
            act.wait_ge(S("cols_loaded"), 16)
            for j in range(4):
                m, h = divmod(j, 2)
                act.wait_ge(S("mh_done"), j + 1)
                act.activation(b_T[:, m, h * HALF:(h + 1) * HALF], ps[:, 5 + (18 + j) % 3, 0:HALF], ACT.Gelu,
                               bias=c("mix_b1", m)).then_inc(S("mh_gelu"), 1)
            act.wait_ge(S("count_floor"), 1)
            act.activation(logc, logc, ACT.Ln).then_inc(S("count_ln"), 1)

            def project(i):
                for m in range(NC2):
                    act.wait_ge(S("g_q_done"), i * 2 + m + 1)
                    for h, z in ((2 * m, slice(0, 64)), (2 * m + 1, slice(64, 128))):
                        act.activation(halves(q_parts[h][z]), pair(2 * m)[z], ACT.Identity,
                                       bias=gcols[z, bass.ds(i * 8 + m, 1)]).then_inc(S("g_q"), 1)
                for m in range(NC2):
                    act.wait_ge(S("g_k_done"), i * 2 + m + 1)
                    for h, z in ((2 * m, slice(0, 64)), (2 * m + 1, slice(64, 128))):
                        act.activation(halves(k_parts[h][z]), pair(4 + 2 * m)[z], ACT.Identity,
                                       bias=gcols[z, bass.ds(i * 8 + (2 + m), 1)]).then_inc(S("g_k"), 1)
                    for h, z, other in ((2 * m, slice(0, 64), slice(64, 128)), (2 * m + 1, slice(64, 128), slice(0, 64))):
                        act.wait_ge(S("g_k"), i * 4 + h + 1)
                        act.activation(k_parts[h][other], k_parts[h][z], ACT.Copy).then_inc(S("g_k_twice"), 1)

            def attention(i, last):
                for n in range(STEPS + 1):
                    if n < STEPS:
                        act.wait_ge(S("g_neg"), i * STEPS + n + 1)
                        act.activation(probs[n % 3], probs[n % 3], ACT.Exp, bias=gneg[:, n:n + 1],
                                       accum_out=gden[:, n:n + 1]).then_inc(S("g_exp"), 1)
                    if n:
                        m = n - 1
                        act.wait_ge(S("g_turned"), i * STEPS + m + 1)
                        if m >= 2:
                            act.wait_ge(S("g_pv"), i * STEPS + m - 1)
                        act.activation(probs_T[m % 2], quads(4), ACT.Copy).then_inc(S("g_probs_T"), 1)
                if not last:
                    act.wait_ge(S("gh_turned"), i * 10 + 10)
                    act.activation(a_T[:, :, 0:4 * TP], ps[:, 0:2, 0:4 * TP], ACT.Identity).then_inc(S("gh_T"), 1)
                    act.wait_ge(S("g_affine"), i + 1)
                    for m in range(NC2):
                        act.activation(n_T[:, m, 0:N], a_T[:, m, 0:N], ACT.Relu, bias=bsc[:, 2, m:m + 1],
                                       scale=bsc[:, 0, m:m + 1]).then_inc(S("g_next"), 1)
                    project(i + 1)

            act.wait_ge(S("gcols_loaded"), 16)
            project(0)
            with act.Fori(0, GL - 1) as i:
                attention(i, False)
            attention(GL - 1, True)

            evac_T("xm", c_T, 0)
            act.wait_ge(S("top_diff"), 1)
            act.activation(tw[:, 1, :], tw[:, 0, :], ACT.Exp).then_inc(S("top_exp"), 1)

            act.wait_ge(S("gate_turned"), NT)
            act.activation(gate_T.rearrange("p (t n) -> p t n", t=NT), quads(2, 16), ACT.Copy).then_inc(S("gate_T_ready"), 1)

            def moe_h(j, u, first):
                act.wait_ge(S("moe_h_done"), j + 1)
                if not first:
                    act.wait_ge(S("moe_y_done"), j - 1)
                for m in range(4):
                    last = act.activation(tile_h[u % 2][:, m, :], ps[:, 2 + u % 2, m * SLOT:(m + 1) * SLOT], ACT.Relu,
                                          bias=b1_moe[:, u, m:m + 1])
                last.then_inc(S("moe_relu"), 1)

            for j in range(TB):
                moe_h(j, j, j < 2)
            with act.Fori(1, MT // TB) as g:
                for u in range(TB):
                    moe_h(g * TB + u, u, False)
            moe_h(MT - 1, 0, False)

            evac_T("x2", n_T, 0)
            for m in range(NC2):
                act.wait_ge(S("m1_q_done"), m + 1)
                act.activation(halves(q_T[:, m, :]), pair(4 + 2 * m), ACT.Identity, bias=c("m1_bq", m))\
                    .then_inc(S("m1_q"), 1)
            for k in range(4):
                act.wait_ge(S("m1_neg"), k + 1)
                p, q = 64 * (k % 2), k // 2
                act.activation(at_sb[p:p + 64, q, p:p + 64], ps[p:p + 64, 5, q * 128 + p:q * 128 + p + 64], ACT.Exp,
                               bias=at_m[p:p + 64, k, 1:2], scale=0.125, accum_out=at_m[p:p + 64, k, 2:3])\
                    .then_inc(S("m1_exp"), 1)
            act.wait_ge(S("gn0_normed"), 1)
            act.activation(y_R[:], y_R[:], ACT.Silu).then_inc(S("g1_x"), 1)
            evac_T("g1", k_T, 0)
            evac_T("y1", b_T, 4)
            for m in range(HM // 128):
                act.wait_ge(S("fc1_done"), m + 1)
                act.activation(halves(hid[0][:, m, :] if m < 4 else hid[1][:, m - 4, :]), pair(4 + 2 * (m % 2)),
                               ACT.Gelu, bias=c("m1_bfc1", m)).then_inc(S("fc1_gelu"), 1)
            act.wait_ge(S("gn1_normed"), 1)
            act.activation(y_R[:], y_R[:], ACT.Silu).then_inc(S("g1_x2"), 1)
            evac_T("x3", c_T, 0)
            act.wait_ge(S("gate2_shift"), 1)
            act.activation(gate2[:, :, 0:E1], gate2[:, :, 0:E1], ACT.Exp).then_inc(S("gate2_exp"), 1)

            act.wait_ge(S("bn_affine"), 1)

            def ffn(e, u, first):
                for k in range(2):
                    for m in range(NC2):
                        act.wait_ge(S("ffn_h_done"), e * 4 + 2 * k + m + 1)
                        if k == 0 and m == 0 and not first:
                            act.wait_ge(S("ffn_y_done"), (e - 1) * 3)
                        j = e * 2 + (2 * E1 * k + m)
                        act.activation(halves(hid[u][:, 2 * k + m, :]), pair(2 * m), ACT.Relu,
                                       bias=bn_b[:, bass.ds(j, 1)], scale=bn_s[:, bass.ds(j, 1)])\
                            .then_inc(S("ffn_relu"), 1)

            ffn(0, 0, True)
            ffn(1, 1, True)
            with act.Fori(1, E1 // 2) as g:
                for u in range(2):
                    ffn(g * 2 + u, u, False)

        @block.vector
        def _(dve):
            own = Steps(dve, S("dve_steps"))
            tt, tsc, stt = dve.tensor_tensor, dve.tensor_scalar, dve.scalar_tensor_tensor

            def norm_pieces(name, X, Y, eps, gain=None, shift=None):
                st, mv, ve, rs = stats[name]

                def sums():
                    for t in range(NT):
                        own.step(dve.bn_stats(st[:, t, :], X[:, t, :]))

                def moments():
                    own.settle()
                    for t in range(NT):
                        own.step(dve.bn_aggr(mv[:, t, :], st[:, t, :]))
                    own.settle()
                    tsc(ve[:], mv[:, :, 1], eps, None, ALU.add).then_inc(S("norm_var"), 1)

                def apply():
                    dve.wait_ge(S("norm_rstd"), NORMS.index(name) + 1)
                    for t in range(NT):
                        last = tsc(Y[:, t, :], X[:, t, :], mv[:, t, 0:1], rs[:, t:t + 1], ALU.subtract, ALU.mult)
                        if t < NT - 1 or gain is not None:
                            own.step(last)
                    return last

                def gained():
                    own.settle()
                    own.step(tt(Y[:], Y[:], wide(gain), ALU.mult))

                def shifted():
                    own.settle()
                    return tt(Y[:], Y[:], wide(shift), ALU.add)

                return [sums, moments, apply] + ([gained, lambda: own.step(shifted())] if name == "ln2" else
                                           [gained, shifted] if gain is not None else [])

            def norm(name, X, Y, eps, gain=None, shift=None):
                for piece in norm_pieces(name, X, Y, eps, gain, shift):
                    last = piece()
                return last

            def evac_T(name, dst, bank):
                dve.wait_ge(S("rows_turned"), 10 * TURNS.index(name) + 10)
                dve.tensor_copy(dst[:, :, 4 * TP:N], ps[:, bank, 0:2 * TP].rearrange("p (c n) -> p c n", c=2))\
                    .then_inc(S("T_by_dve"), 1)

            dve.wait_ge(S("x_loaded"), 16)
            norm("ln0", x_R, n_R, 1e-5).then_inc(S("n0_ready"), 1)
            dve.wait_ge(S("edges_loaded"), 32)
            own.link(dve.tensor_copy(idf[:, 0:2, :], idx[:]))
            own.link(tsc(idf[:, 3, :], idf[:, 0, :], float(HALF), None, ALU.is_ge))
            own.step(stt(out=idf[:, 2, :], in0=idf[:, 3, :], scalar=-float(HALF), in1=idf[:, 0, :],
                         op0=ALU.mult, op1=ALU.add))
            own.link(tsc(idf[:, 3, :], idf[:, 3, :], float(FIELD - 1), 1.0, ALU.mult, ALU.add))
            evac_T("n0", n_T, 7)
            dve.wait_ge(S("ids_ready"), 1)

            def one_hot(j, u, free):
                if free is not None:
                    dve.wait_ge(S("onehot_used"), free)
                tsc(oh_src[:, u, 0:HALF], node_ids[:, 0:HALF], idf[:, 2, bass.ds(j, 1)], idf[:, 3, bass.ds(j, 1)],
                    ALU.is_equal, ALU.mult)
                tsc(oh_dst[:, u, 0:N], node_ids[:], idf[:, 1, bass.ds(j, 1)], None, ALU.is_equal)\
                    .then_inc(S("onehot_ready"), 1)

            def edges(k):
                a, b = CHUNKS[k]
                if a == 0:
                    for u in range(4):
                        one_hot(u, u, None)
                    a = 4
                with dve.Fori(a // 4, b // 4) as g:
                    for u in range(4):
                        one_hot(g * 4 + u, u, g * 4 + (u - 3))
                if b % 4:
                    one_hot(b - 1, 0, b - 4)

            def add_counts(k):
                dve.wait_ge(S("counts_out"), k + 1)
                if k == 0:
                    own.step(tsc(cnt_hi, cnt_new, 12, None, ALU.logical_shift_right))
                    tsc(cnt_lo, cnt_new, FIELD - 1, None, ALU.bitwise_and).then_inc(S("counts_added"), 1)
                    dve.wait_ge(S("counts_added"), 1)
                    return
                lo, hi = (count[:, :, 0:HALF], count[:, :, HALF:NP]) if k == 2 else (cnt_lo, cnt_hi)
                own.link(tsc(cnt_tmp, cnt_new, 12, None, ALU.logical_shift_right))
                own.link(tt(hi, cnt_hi, cnt_tmp, ALU.add))
                own.link(tsc(cnt_tmp, cnt_new, FIELD - 1, None, ALU.bitwise_and))
                tt(lo, cnt_lo, cnt_tmp, ALU.add).then_inc(S("counts_added"), 1)
                dve.wait_ge(S("counts_added"), k + 1)

            edges(0)
            add_counts(0)
            dve.wait_ge(S("pads_ready"), 2)
            for j in range(4):
                m, h = divmod(j, 2)
                dve.wait_ge(S("mq_exp"), j + 1)
                own.link(tsc(eq[:, j % 2, :], eq[:, j % 2, :], 1.0, None, ALU.min))
                stt(out=q_T[:, m, h * HALF:(h + 1) * HALF], in0=ps[:, 5 + j % 3, 0:HALF], scalar=0.0,
                    in1=eq[:, j % 2, :], op0=ALU.max, op1=ALU.add).then_inc(S("mq_phi"), 1)
            for t in range(NT):
                dve.wait_ge(S("mkv_exp"), t + 1)
                own.link(tsc(ek[:, t % 2, :], ek[:, t % 2, :], 1.0, None, ALU.min))
                stt(out=vs[:, t, 0:D], in0=ps[0:TP, 5 + (4 + t) % 3, 0:D], scalar=0.0,
                    in1=ek[:, t % 2, :], op0=ALU.max, op1=ALU.add).then_inc(S("mkv_phi"), 1)
            edges(1)
            dve.wait_ge(S("masks_ready"), 2)
            dve.wait_ge(S("mKV_done"), 2)
            for q in range(2):
                own.step(tt(kv_sb[:, q, 0:128].rearrange("p (h n) -> p h n", h=4),
                            ps[:, 5, q * 129:q * 129 + 128].rearrange("p (h n) -> p h n", h=4), head_mask[:], ALU.mult))
                last = tsc(kv_sb[:, q, 128:132], head_cols[:], ps[:, 5, q * 129 + 128:q * 129 + 129], None, ALU.mult)
                if q == 0:
                    own.step(last)
            last.then_inc(S("mKV_ready"), 1)
            add_counts(1)
            for t in range(NT):
                b = 5 + (1 + t) % 3
                dve.wait_ge(S("mt_done"), t + 1)
                src = ps[0:TP, b, 0:264].rearrange("p (c n) -> p c n", c=2)
                own.link(tsc(zden[:, 0, t, :].rearrange("p (c n) -> p c n", c=2), src[:, :, 128:132], 1e-6, None, ALU.add))
                own.link(dve.reciprocal(zden[:, 1, t, :], zden[:, 0, t, :]))
                for q in range(2):
                    last = tt(mix_R[:, t, q * 128:(q + 1) * 128].rearrange("p (h n) -> p h n", h=4),
                              ps[0:TP, b, q * 132:q * 132 + 128].rearrange("p (h n) -> p h n", h=4),
                              zden[:, 1, t, 4 * q:4 * q + 4].unsqueeze(2).broadcast_to([TP, 4, 32]), ALU.mult)
                    if q == 0:
                        own.step(last)
                last.then_inc(S("mt_out"), 1)
            own.settle()
            dve.wait_ge(S("mt_out"), NT)
            own.link(tt(mix_R[:], mix_R[:], n_R[:], ALU.add))
            dve.wait_ge(S("rows_loaded"), 16)
            norm("ln1", mix_R, h_R, 1e-5, row["mix_ln1_g"], row["mix_ln1_b"]).then_inc(S("m1_ready"), 1)
            dve.wait_ge(S("m1_ready"), 1)
            edges(2)
            evac_T("m1", a_T, 7)
            own.link(tt(h_R[:], h_R[:], wide(row["mix_b2"]), ALU.add))
            add_counts(2)
            own.link(tsc(logc, count[:], 1.0, None, ALU.max))
            tsc(big2[0:TP, 0:NT * NP].rearrange("p (t n) -> p t n", t=NT), count[:], 0.5, MASK,
                ALU.is_lt, ALU.mult).then_inc(S("count_floor"), 1)
            for t in range(NT):
                dve.wait_ge(S("my_done"), t + 1)
                tt(mix_R[:, t, :], ps[0:TP, 5 + (22 + t) % 3, 0:D], h_R[:, t, :], ALU.add).then_inc(S("my_out"), 1)
            dve.wait_ge(S("count_floor"), 1)
            dve.wait_ge(S("count_ln"), 1)
            stt(out=logc, in0=logc, scalar=8.0, in1=big2[0:TP, 0:NT * NP].rearrange("p (t n) -> p t n", t=NT),
                op0=ALU.mult, op1=ALU.add).then_inc(S("logc_ready"), 1)
            dve.wait_ge(S("logc_ready"), 1)
            dve.wait_ge(S("cols_loaded"), 16)
            for k in range(2):
                tsc(bn_v[:, k * 2 * E1:(k + 1) * 2 * E1], c("v1" if k == 0 else "v2", 0, 2 * E1), 1e-3, None, ALU.add)\
                    .then_inc(S("bn_var"), 1)

            def bn_affine():
                dve.wait_ge(S("bn_rstd"), 1)
                for k in range(2):
                    z = slice(k * 2 * E1, (k + 1) * 2 * E1)
                    own.step(tt(bn_s[:, z], bn_r[:, z], c("g1" if k == 0 else "g2", 0, 2 * E1), ALU.mult))
                    own.link(tt(bn_t[:, z], c("b1" if k == 0 else "b2", 0, 2 * E1), c("m1" if k == 0 else "m2", 0, 2 * E1),
                                ALU.subtract))
                    own.link(tt(bn_t[:, z], bn_t[:, z], bn_s[:, z], ALU.mult))
                    last = tt(bn_b[:, z], bn_t[:, z], c("be1" if k == 0 else "be2", 0, 2 * E1), ALU.add)
                    if k == 0:
                        own.step(last)
                last.then_inc(S("bn_affine"), 1)

            norm2 = norm_pieces("ln2", mix_R, mix_R, 1e-5, row["mix_ln2_g"], row["mix_ln2_b"])
            fillers = {5: norm2[0], 6: norm2[1], 9: norm2[2], 10: norm2[3], 12: norm2[4], 14: bn_affine,
                       16: lambda: own.link(tt(x_R[:], x_R[:], mix_R[:], ALU.add))}

            LAYER_STEPS = 2 * GH + 8

            def project(i):
                for m in range(NC2):
                    for h, z, other in ((2 * m, slice(0, 64), slice(64, 128)), (2 * m + 1, slice(64, 128), slice(0, 64))):
                        dve.wait_ge(S("g_q"), i * 4 + h + 1)
                        stt(out=halves(q_parts[h][other]), in0=pair(2 * m)[z], scalar=gcols[z, bass.ds(i * 8 + m, 1)],
                            in1=halves(q_parts[h][z]).bitcast(F32), op0=ALU.add, op1=ALU.subtract).then_inc(S("g_q_lo"), 1)
                for m in range(NC2):
                    for h, z in ((2 * m, slice(0, 64)), (2 * m + 1, slice(64, 128))):
                        dve.wait_ge(S("g_k"), i * 4 + h + 1)
                        stt(out=halves(k_lo[m][z]), in0=pair(4 + 2 * m)[z], scalar=gcols[z, bass.ds(i * 8 + (2 + m), 1)],
                            in1=halves(k_parts[h][z]).bitcast(F32), op0=ALU.add, op1=ALU.subtract).then_inc(S("g_k_lo"), 1)
                for t in range(3):
                    rows_in(i, t)

            def rows_in(i, t):
                dve.wait_ge(S("g_rows_done"), i * NT + t + 1)
                tt(vs[:, t, :], ps[0:TP, ROWS_BANK[t], :], gbias[:], ALU.add).then_inc(S("g_rows_read"), 1)

            def attention(i, last_layer):
                lay = Steps(dve, S("g_dve_steps"), i * LAYER_STEPS)

                def head_out(h):
                    z = slice(h * NT, h * NT + NT)
                    dve.wait_ge(S("g_exp"), i * STEPS + h * NT + NT)
                    lay.link(dve.reciprocal(grec[:, z], gden[:, z]))
                    lay.link(stt(out=grec[:, z], in0=gmax[:, z], scalar=HAS_EDGE, in1=grec[:, z],
                                 op0=ALU.is_gt, op1=ALU.mult))
                    dve.wait_ge(S("g_pv"), i * STEPS + h * NT + NT)
                    tt(att[:], ps[0:TP, 6 + h % 2, 0:NT * 64].rearrange("p (t n) -> p t n", t=NT),
                       grec[:, z].unsqueeze(2).broadcast_to([TP, NT, 64]), ALU.mult).then_inc(S("g_head"), 1)
                    dve.wait_ge(S("g_head"), i * GH + h + 1)
                    tt(h_R[:, :, h * 64:(h + 1) * 64], att[:], vs[:, :, D + h * 64:D + (h + 1) * 64], ALU.add)\
                        .then_inc(S("g_out"), 1)
                    dve.wait_ge(S("g_out"), i * GH + h + 1)

                for n in range(STEPS):
                    dve.wait_ge(S("g_scores"), i * STEPS + n + 1)
                    if n >= 3:
                        dve.wait_ge(S("g_turned"), i * STEPS + n - 2)
                    dve.nop(nofuse=True)
                    dve.tensor_tensor_reduce(out=halves(probs[n % 3]), in0=pair(2 * (n % 2), TP),
                                             in1=halves(logc[:, n % NT, :]), scale=0.125, scalar=-3.0e38,
                                             op0=ALU.add, op1=ALU.max, accum_out=gmax[:, n:n + 1])\
                        .then_inc(S("g_max"), 1)
                    if n < 2:
                        rows_in(i, 3 + n)
                    if n == 1:
                        dve.wait_ge(S("g_rows_read"), i * NT + NT)
                    if n % NT == 3 and n > NT:
                        head_out(n // NT - 1)
                    if last_layer and n in fillers:
                        fillers[n]()
                head_out(GH - 1)
                if last_layer:
                    return
                dve.wait_ge(S("gh_turned"), i * 10 + 10)
                dve.tensor_copy(a_T[:, :, 4 * TP:N], ps[:, 2, 0:2 * TP].rearrange("p (c n) -> p c n", c=2))\
                    .then_inc(S("gh_T2"), 1)
                dve.wait_ge(S("gh_T"), i + 1)
                dve.wait_ge(S("gh_T2"), i + 1)
                for m in range(NC2):
                    lay.step(dve.bn_stats(bst[:, m, 0, :], a_T[:, m, 0:HALF]))
                    lay.step(dve.bn_stats(bst[:, m, 1, :], a_T[:, m, HALF:N]))
                lay.settle()
                dve.nop(nofuse=True)
                for m in range(NC2):
                    lay.step(dve.bn_aggr(bmv[:, m, :], bst[:, m, :, :]))
                lay.settle()
                tsc(bve[:], bmv[:, :, 1], 1e-5, None, ALU.add).then_inc(S("g_var"), 1)
                dve.wait_ge(S("g_rstd"), i + 1)
                lay.link(tt(bsc[:, 0, :], brs[:], gcols[:, bass.ds(i * 8 + 4, 2)], ALU.mult))
                lay.link(tt(bsc[:, 1, :], bmv[:, :, 0], bsc[:, 0, :], ALU.mult))
                tt(bsc[:, 2, :], gcols[:, bass.ds(i * 8 + 6, 2)], bsc[:, 1, :], ALU.subtract).then_inc(S("g_affine"), 1)
                project(i + 1)
                return lay.n

            dve.wait_ge(S("gcols_loaded"), 16)
            project(0)

            with dve.Fori(0, GL - 1) as i:
                LS = attention(i, False)
            assert LS == LAYER_STEPS, LS
            attention(GL - 1, True)

            own.link(tt(x_R[:], x_R[:], h_R[:], ALU.add))
            norm("lnm", x_R, n_R, 1e-5).then_inc(S("xm_ready"), 1)
            evac_T("xm", c_T, 2)
            dve.wait_ge(S("logits_done"), 1)
            own.link(tt(lg[:], ps[0:TP, 7, 0:NT * 16].rearrange("p (t n) -> p t n", t=NT),
                        row["gates"][:, 0:16].unsqueeze(1).broadcast_to([TP, NT, 16]), ALU.add))
            for t in range(NT):
                own.step(dve.max(top[:, t, :], lg[:, t, :]))
            own.settle()
            for t in range(NT):
                own.step(dve.max_index(topi[:, t, :], top[:, t, :], lg[:, t, :]))
            tt(tw[:, 0, :], top[:, :, 1], top[:, :, 0], ALU.subtract).then_inc(S("top_diff"), 1)
            own.settle()
            own.link(dve.tensor_copy(topf[:], topi[:, :, 0:2]))
            dve.wait_ge(S("routing_ids_ready"), 1)
            for k in range(2):
                own.step(tt(pick[:, k], expert_ids[:].unsqueeze(1).broadcast_to([TP, NT, 16]),
                            topf[:, :, k].unsqueeze(2).broadcast_to([TP, NT, 16]), ALU.is_equal))
            own.settle()
            tt(picked[:], pick[:, 0], pick[:, 1], ALU.add).then_inc(S("picked_ready"), 1)
            dve.wait_ge(S("top_exp"), 1)
            own.link(tsc(tw[:, 2, :], tw[:, 1, :], 1.0, None, ALU.add))
            own.link(dve.reciprocal(tw[:, 2, :], tw[:, 2, :]))
            own.link(tt(tw[:, 3, :], tw[:, 1, :], tw[:, 2, :], ALU.mult))
            for k in range(2):
                own.step(tt(place[:, k], pick[:, k], tw[:, 2 + k, :].unsqueeze(2).broadcast_to([TP, NT, 16]), ALU.mult))
            own.settle()
            tt(gate[:], place[:, 0], place[:, 1], ALU.add).then_inc(S("gate_ready"), 1)
            dve.wait_ge(S("gate_ready"), 1)
            dve.wait_ge(S("ranked"), 1)
            own.link(tsc(tiles_i[:], ps[0:TP, 6, 128:144], float(SLOT - 1), None, ALU.add))
            own.link(tsc(tiles_i[:], tiles_i[:], 7, None, ALU.logical_shift_right))
            own.link(dve.tensor_copy(tiles[:, 0, 16:32], tiles_i[:]))
            own.link(dve.tensor_copy(tiles[:, 2, 16:32], tiles[:, 0, 16:32]))
            for k, shift in enumerate((1, 2, 4, 8)):
                src, dst = tiles[:, k % 2, :], tiles[:, (k + 1) % 2, :]
                own.link(tt(dst[:, 16:32], src[:, 16:32], src[:, 16 - shift:32 - shift], ALU.add))
            upto = tiles[:, 0, 16:32]
            own.link(tt(tiles[:, 2, 16:32], upto, tiles[:, 2, 16:32], ALU.subtract))
            own.link(stt(out=place[:, 0], in0=tiles[:, 2, 16:32].unsqueeze(1).broadcast_to([TP, NT, 16]),
                         scalar=float(SLOT), in1=ps[0:TP, 6, 0:NT * 16].rearrange("p (t n) -> p t n", t=NT),
                         op0=ALU.mult, op1=ALU.add))
            own.link(tt(own_tile, tile_ids[0:1].unsqueeze(2).broadcast_to([1, MT, 16]),
                        upto[0:1].unsqueeze(1).broadcast_to([1, MT, 16]), ALU.is_ge))
            own.link(dve.tensor_reduce(tile_e[:], own_tile, AX, ALU.add))
            tsc(tile_expert[:], tile_e[:], float(E0 - 1), None, ALU.min).then_inc(S("tile_expert_ready"), 1)
            own.link(tt(place[:, 1], place[:, 0], pick[:, 1], ALU.mult))
            own.link(tt(place[:, 0], place[:, 0], pick[:, 0], ALU.mult))
            own.link(dve.tensor_reduce(slot[:, 0, :].rearrange("p (k t) -> p k t", k=2), place, AX, ALU.add))
            own.link(dve.tensor_copy(slot_i[:, 0, :], slot[:, 0, :]))
            own.step(tsc(slot_i[:, 1, :], slot_i[:, 0, :], 7, None, ALU.logical_shift_right))
            own.link(tsc(slot_i[:, 2, :], slot_i[:, 0, :], SLOT - 1, None, ALU.bitwise_and))
            own.link(dve.tensor_copy(slot[:, 1:3, :], slot_i[:, 1:3, :]))
            for k in range(2 * NT):
                tsc(tile_hot[:, k, :], tile_ids[:], slot[:, 1, k:k + 1], choice_ids[:, k:k + 1], ALU.is_equal, ALU.mult)
                tsc(row_hot[:, k, :], row_ids[:], slot[:, 2, k:k + 1], None, ALU.is_equal).then_inc(S("hot_ready"), 1)
            dve.wait_ge(S("hot_ready"), 2 * NT)
            dve.wait_ge(S("inverted"), 1)
            src = ps[:, 7, 0:MT]
            own.step(tsc(slot_m[:, 0, :], src, float(N) + 0.5, -float(N), ALU.is_gt, ALU.mult))
            own.link(tsc(slot_m[:, 1, :], src, 0.5, None, ALU.is_lt))
            own.step(tt(slot_m[:, 0, :], src, slot_m[:, 0, :], ALU.add))
            own.link(tt(slot_m[:, 1, :], slot_m[:, 1, :], spare_ids[:], ALU.mult))
            own.step(tsc(slot_m[:, 0, :], slot_m[:, 0, :], -1.0, 0.0, ALU.add, ALU.max))
            own.settle()
            dve.tensor_copy(from_row[:], slot_m[:, 0, :]).then_inc(S("rows_placed"), 1)
            tt(to_row[:], src, slot_m[:, 1, :], ALU.add).then_inc(S("rows_placed"), 1)
            dve.wait_ge(S("deg_done"), 1)
            tsc(halves(inv_deg[:]), pair(4), 1.0, None, ALU.max).then_inc(S("deg_read"), 1)
            dve.wait_ge(S("deg_read"), 1)
            own.link(dve.reciprocal(inv_deg[:], inv_deg[:]))

            def rows_of(name, acc, e, scale, base, n0):
                for t in range(NT):
                    if t % 2 == 0:
                        dve.wait_ge(S(f"{name}_y_done"), e * 3 + t // 2 + 1)
                    src = ps[0:TP, 4 + t // 2, (t % 2) * D:(t % 2 + 1) * D]
                    if n0:
                        dve.wait_ge(S(f"{name}_acc"), e * NT + t - NT + 1)
                    stt(out=acc[:, t, :], in0=src, scalar=scale(t), in1=acc[:, t, :], op0=ALU.mult, op1=ALU.add)\
                        .then_inc(S(f"{name}_acc"), 1)

            def bias_rows(name, acc):
                for t in range(NT):
                    dve.wait_ge(S(f"{name}_b_done"), min(t // 2 * 2 + 2, NT))
                    tt(acc[:, t, :], ps[0:TP, 7 - t // 2, (t % 2) * D:(t % 2 + 1) * D],
                       acc[:, t, :], ALU.add).then_inc(S(f"{name}_bias_in"), 1)
                dve.wait_ge(S(f"{name}_bias_in"), NT)

            def moe_tile_T(j, u, first):
                dve.wait_ge(S("moe_turned"), j * 2 + 2)
                if not first:
                    dve.wait_ge(S("moe_h_done"), j - 1)
                dve.tensor_copy(tile_xT[u], ps[:, u, 0:D].rearrange("p (c n) -> p c n", c=2)).then_inc(S("moe_T"), 1)

            def moe_tile_y(j, u, k):
                dve.wait_ge(S("moe_y_done"), j + 1)
                if k is not None:
                    dve.wait_ge(S(f"moe_scattered{u}"), k * 16)
                dve.tensor_copy(tile_y[u], ps[:, 4 + u, 0:D]).then_inc(S("moe_y_out"), 1)

            moe_tile_T(0, 0, True)
            bias_rows("moe", n_R)
            moe_tile_T(1, 1, True)
            moe_tile_T(2, 0, False)
            moe_tile_y(0, 0, None)
            moe_tile_T(3, 1, False)
            moe_tile_y(1, 1, None)
            with dve.Fori(2, MT // 2) as g:
                for u in range(2):
                    moe_tile_T(g * 2 + u, u, False)
                    moe_tile_y(g * 2 + (u - 2), u, g - 1)
            moe_tile_T(MT - 1, 0, False)
            moe_tile_y(MT - 3, 0, (MT - 3) // 2)
            moe_tile_y(MT - 2, 1, (MT - 3) // 2)
            moe_tile_y(MT - 1, 0, (MT - 1) // 2)
            dve.wait_ge(S("choices_loaded"), 16)
            for k in range(2):
                for t in range(NT):
                    j = k * NT + t
                    own.step(stt(out=n_R[:, t, :], in0=vs[:, j // 2, (j % 2) * D:(j % 2 + 1) * D],
                                 scalar=tw[:, 2 + k, t:t + 1], in1=n_R[:, t, :], op0=ALU.mult, op1=ALU.add))
                own.settle()
            own.link(norm("lny", n_R, y_R, 1e-5, row["moe_gamma"], row["moe_beta"]))
            own.link(tt(x_R[:], x_R[:], y_R[:], ALU.add))
            norm("lnx", x_R, n_R, 1e-5).then_inc(S("x2_ready"), 1)
            evac_T("x2", n_T, 2)

            def aggregate(l, src_T):
                for m in range(NC2):
                    dve.wait_ge(S("agg_done"), 2 * l + m + 1)
                    own.link(tt(halves(a_T[:, m, :]), pair(2 * m), halves(inv_deg[:]), ALU.mult))
                    tt(a_T[:, m, :], a_T[:, m, :], src_T[:, m, :], ALU.add).then_inc(S("agg_out"), 1)

            dve.wait_ge(S("T_by_act"), TURNS.index("x2") + 1)
            dve.wait_ge(S("T_by_dve"), TURNS.index("x2") + 1)
            aggregate(0, n_T)
            for t in range(NT):
                dve.wait_ge(S("m1_kv_done"), t + 1)
                tt(vs[:, t, :], ps[0:TP, 4 + t % 4, :],
                   rows[:, ROWS.index("m1_bk"):ROWS.index("m1_bv") + 1, :].rearrange("p a n -> p (a n)"), ALU.add)\
                    .then_inc(S("m1_kv"), 1)

            def graph_rows(l):
                for t in range(NT):
                    dve.wait_ge(S("g1_h_done"), l * NT + t + 1)
                    tt(y_R[:, t, :], ps[0:TP, t % 4, 0:D], row[f"g1_b{l}"], ALU.add).then_inc(S("g1_h"), 1)
                dve.wait_ge(S("g1_h"), l * NT + NT)
                norm(f"gn{l}", y_R, y_R, 1e-5, row[f"g1_g{l}"], row[f"g1_beta{l}"]).then_inc(S(f"gn{l}_normed"), 1)

            dve.wait_ge(S("m1_at_done"), 2)
            for k in range(4):
                p, q = 64 * (k % 2), k // 2
                own.link(dve.reduce_max(at_m[p:p + 64, k, 0:1], ps[p:p + 64, 5, q * 128 + p:q * 128 + p + 64], AX))
            for k in range(4):
                p = 64 * (k % 2)
                tsc(at_m[p:p + 64, k, 1:2], at_m[p:p + 64, k, 0:1], -0.125, None, ALU.mult).then_inc(S("m1_neg"), 1)
            graph_rows(0)
            for k in range(4):
                p, q = 64 * (k % 2), k // 2
                dve.wait_ge(S("m1_exp"), k + 1)
                own.link(dve.reciprocal(at_m[p:p + 64, k, 2:3], at_m[p:p + 64, k, 2:3]))
                tsc(at_sb[p:p + 64, q, p:p + 64], at_sb[p:p + 64, q, p:p + 64], at_m[p:p + 64, k, 2:3], None, ALU.mult)\
                    .then_inc(S("m1_attn"), 1)
            dve.wait_ge(S("at_turned"), 2)
            dve.tensor_copy(at_T[:], ps[:, 6, 0:256].rearrange("p (c n) -> p c n", c=2)).then_inc(S("at_T_ready"), 1)
            for t in range(NT):
                dve.wait_ge(S("m1_xf_done"), t + 1)
                tt(mix_R[:, t, :], ps[0:TP, 4 + t % 4, 0:D], n_R[:, t, :], ALU.add).then_inc(S("m1_xf"), 1)
            dve.wait_ge(S("m1_xf"), NT)
            norm("lnh", mix_R, h_R, 1e-5, row["m1_norm_g"], row["m1_norm_b"]).then_inc(S("y1_ready"), 1)
            evac_T("g1", k_T, 2)
            evac_T("y1", b_T, 6)
            dve.wait_ge(S("T_by_act"), TURNS.index("g1") + 1)
            dve.wait_ge(S("T_by_dve"), TURNS.index("g1") + 1)
            aggregate(1, k_T)
            own.step(tt(x_R[:], x_R[:], mix_R[:], ALU.add))
            own.settle()
            own.link(tt(x_R[:], x_R[:], wide(row["m1_bfc2"]), ALU.add))
            graph_rows(1)
            for t in range(NT):
                dve.wait_ge(S("fc2_done"), t + 1)
                tt(x_R[:, t, :], ps[0:TP, 4 + t % 4, 0:D], x_R[:, t, :], ALU.add).then_inc(S("fc2_out"), 1)
            dve.wait_ge(S("fc2_out"), NT)
            dve.wait_ge(S("g1_x2"), 1)
            own.link(tt(x_R[:], x_R[:], y_R[:], ALU.add))
            norm("lnf", x_R, n_R, 1e-5).then_inc(S("x3_ready"), 1)
            evac_T("x3", c_T, 2)

            dve.wait_ge(S("logits2_done"), 1)
            own.link(tt(gate2[:, :, 0:E1], ps[0:TP, 7, 0:NT * E1].rearrange("p (t n) -> p t n", t=NT),
                        row["gates"][:, 16:16 + E1].unsqueeze(1).broadcast_to([TP, NT, E1]), ALU.add))
            own.link(dve.tensor_reduce(tw[:, 0, :], gate2[:, :, 0:E1], AX, ALU.max))
            tt(gate2[:, :, 0:E1], gate2[:, :, 0:E1], tw[:, 0, :].unsqueeze(2).broadcast_to([TP, NT, E1]), ALU.subtract)\
                .then_inc(S("gate2_shift"), 1)
            dve.wait_ge(S("gate2_exp"), 1)
            own.link(dve.tensor_reduce(tw[:, 1, :], gate2[:, :, 0:E1], AX, ALU.add))
            own.link(dve.reciprocal(tw[:, 1, :], tw[:, 1, :]))
            tt(gate2[:, :, 0:E1], gate2[:, :, 0:E1], tw[:, 1, :].unsqueeze(2).broadcast_to([TP, NT, E1]), ALU.mult)\
                .then_inc(S("gate2_ready"), 1)
            dve.wait_ge(S("gate2_turned"), NT)
            dve.tensor_copy(gate_T[0:E1, :].rearrange("p (t n) -> p t n", t=NT), quads(4, E1)).then_inc(S("gate2_T_ready"), 1)
            bias_rows("ffn", x_R)
            gate2_flat = gate2[:].rearrange("p t n -> p (t n)")
            rows_of("ffn", x_R, 0, lambda t: gate2[:, t, 0:1], 0, False)
            rows_of("ffn", x_R, 1, lambda t: gate2[:, t, 1:2], 0, True)
            with dve.Fori(1, E1 // 2) as g:
                for u in range(2):
                    e = g * 2 + u
                    rows_of("ffn", x_R, e, lambda t: gate2_flat[:, bass.ds(e + 16 * t, 1)], 0, True)

        @block.tensor
        def _(pe):
            mm = pe.matmul

            def turn(name, src, bank):
                pe.wait_ge(S(f"{name}_ready"), 1)
                for t in range(NT):
                    for q in range(NC2):
                        dst = ps[:, bank + q, t * TP:(t + 1) * TP] if t < 4 else ps[:, bank + 2, q * TP:(q + 1) * TP]
                        pe.transpose(dst, src[:, t, q * 128:(q + 1) * 128], ident[0:TP, 0:TP])\
                            .then_inc(S("rows_turned"), 1)

            def turned(name):
                pe.wait_ge(S("T_by_act"), TURNS.index(name) + 1)
                pe.wait_ge(S("T_by_dve"), TURNS.index(name) + 1)

            def to_T(b, w, src_T, m0, K=NC2):
                for h in range(2):
                    for k in range(K):
                        last = mm(ps[:, b + h, 0:HALF], w[:, k, m0:m0 + 128], src_T[:, k, h * HALF:(h + 1) * HALF],
                                  start=(k == 0), stop=(k == K - 1))
                return last

            def to_R(dst, src, t, w, K=NC2):
                for k in range(K):
                    last = mm(dst, src(k)[:, t * TP:(t + 1) * TP], w(k), start=(k == 0), stop=(k == K - 1))
                return last

            pe.wait_ge(S("ident_ready"), 1)
            turn("n0", n_R, 5)

            def count_tile(u, j, first, last):
                pe.wait_ge(S("onehot_ready"), j + 1)
                for t in range(NT):
                    ins = mm(ps[0:TP, t, 0:HALF], oh_dst[:, u, t * TP:(t + 1) * TP], oh_src[:, u, 0:HALF],
                             start=first, stop=last, skip_group_check=not (first or last))
                ins.then_inc(S("onehot_used"), 1)
                return ins

            def edges(k):
                a, b = CHUNKS[k]
                if k:
                    pe.wait_ge(S("counts_out"), k)
                for u in range(4):
                    count_tile(u, a + u, u == 0, False)
                rest = 1 if b % 4 else 0
                with pe.Fori(a // 4 + 1, b // 4 - (1 - rest)) as g:
                    for u in range(4):
                        count_tile(u, g * 4 + u, False, False)
                if rest:
                    count_tile(0, b - 1, False, True)
                else:
                    for u in range(4):
                        count_tile(u, b - 4 + u, False, u == 3)

            edges(0)
            pe.wait_ge(S("w_mix_loaded"), 16)
            turned("n0")
            pe.wait_ge(S("pads_ready"), 2)
            for j in range(4):
                m, h = divmod(j, 2)
                if j == 3:
                    pe.wait_ge(S("mq_phi"), 1)
                for k in range(NC2):
                    last = mm(ps[:, 5 + j % 3, 0:HALF], w_mix[:, k, m * 128:(m + 1) * 128],
                              n_T[:, k, h * HALF:(h + 1) * HALF], start=(k == 0), stop=(k == 1))
                last.then_inc(S("mq_done"), 1)
            for t in range(NT):
                pe.wait_ge(S("mq_phi"), min(t + 2, 4))
                if t >= 3:
                    pe.wait_ge(S("mkv_phi"), t - 2)
                to_R(ps[0:TP, 5 + (4 + t) % 3, :], lambda k: n_T[:, k, :], t, lambda k: w_mix[:, k, D:3 * D])\
                    .then_inc(S("mkv_done"), 1)
            edges(1)
            pe.wait_ge(S("mkv_phi"), NT)
            pe.wait_ge(S("vones_ready"), 1)
            for q in range(2):
                for t in range(NT):
                    last = mm(ps[:, 5, q * 129:(q + 1) * 129], vs[:, t, q * 128:(q + 1) * 128], vones[:, t, q, :],
                              start=(t == 0), stop=(t == NT - 1))
                last.then_inc(S("mKV_done"), 1)
            pe.wait_ge(S("mKV_ready"), 1)
            for t in range(NT):
                if t >= 3:
                    pe.wait_ge(S("mt_out"), t - 2)
                for q in range(2):
                    last = mm(ps[0:TP, 5 + (1 + t) % 3, q * 132:(q + 1) * 132], q_T[:, q, t * TP:(t + 1) * TP],
                              kv_sb[:, q, :], start=True, stop=True)
                last.then_inc(S("mt_done"), 1)
            edges(2)
            turn("m1", h_R, 5)
            turned("m1")
            for j in range(4):
                m, h = divmod(j, 2)
                if j == 3:
                    pe.wait_ge(S("mh_gelu"), 1)
                for k in range(NC2):
                    last = mm(ps[:, 5 + (18 + j) % 3, 0:HALF], w_mix[:, k, 3 * D + m * 128:3 * D + (m + 1) * 128],
                              a_T[:, k, h * HALF:(h + 1) * HALF], start=(k == 0), stop=(k == 1))
                last.then_inc(S("mh_done"), 1)
            pe.wait_ge(S("mh_gelu"), 4)
            for t in range(NT):
                if t >= 3:
                    pe.wait_ge(S("my_out"), t - 2)
                to_R(ps[0:TP, 5 + (22 + t) % 3, 0:D], lambda k: b_T[:, k, :], t, lambda k: w_mix[:, k, 4 * D:5 * D])\
                    .then_inc(S("my_done"), 1)
            pe.wait_ge(S("counts_out"), 3)

            def project(i, first):
                if not first:
                    pe.wait_ge(S("g_next"), i * 2)
                pe.wait_ge(S("gw_loaded"), i * 32 + 32)
                for m in range(NC2):
                    to_T(2 * m, gw[:, 0], n_T, m * 128).then_inc(S("g_q_done"), 1)
                if first:
                    pe.wait_ge(S("my_out"), NT)
                for m in range(NC2):
                    to_T(4 + 2 * m, gw[:, 1], n_T, m * 128).then_inc(S("g_k_done"), 1)
                pe.wait_ge(S("g_q_lo"), i * 4 + 4)
                for t in range(3):
                    if t == 2:
                        pe.wait_ge(S("g_k_lo"), i * 4 + 2)
                    rows_out(i, t)

            def rows_out(i, t):
                for k in range(NC2):
                    last = mm(ps[0:TP, ROWS_BANK[t], :], n_T[:, k, t * TP:(t + 1) * TP], gw[:, 2:4, k, :],
                              start=(k == 0), stop=(k == 1))
                last.then_inc(S("g_rows_done"), 1)

            def attention(i, last_layer):
                def scores(n):
                    h, t = divmod(n, NT)
                    if t == 0:
                        pe.wait_ge(S("g_k_twice"), i * 4 + h + 1)
                        pe.wait_ge(S("g_k_lo"), i * 4 + h + 1)
                    if n == 1:
                        pe.wait_ge(S("g_rows_read"), i * NT + 2)
                    if n >= 2:
                        pe.wait_ge(S("g_max"), i * STEPS + n - 1)
                    z = slice(64 * (h % 2), 64 * (h % 2) + 64)
                    rows_t = slice(t * TP, (t + 1) * TP)
                    for b in range(2):
                        cols_b = slice(b * HALF, (b + 1) * HALF)
                        dst = ps[0:TP, 2 * (n % 2) + b, 0:HALF]
                        mm(dst, q_parts[h][:, rows_t], k_parts[h][:, cols_b], start=True, stop=False)
                        last = mm(dst, q_parts[h][z, rows_t], k_lo[h // 2][z, cols_b], start=False, stop=True)
                    last.then_inc(S("g_scores"), 1)

                def turn_probs(n):
                    pe.wait_ge(S("g_exp"), i * STEPS + n + 1)
                    if n:
                        pe.wait_ge(S("g_probs_T"), i * STEPS + n)
                    else:
                        pe.wait_ge(S("g_rows_read"), i * NT + 4)
                    for s in range(NT):
                        last = pe.transpose(quads(4)[:, s, :], probs[n % 3][:, s * TP:(s + 1) * TP], ident[0:TP, 0:TP])
                    last.then_inc(S("g_turned"), 1)

                def weigh(n):
                    h, t = divmod(n, NT)
                    if t == 0 and h >= 2:
                        pe.wait_ge(S("g_head"), i * GH + h - 1)
                    if n == 0:
                        pe.wait_ge(S("g_rows_read"), i * NT + NT)
                    pe.wait_ge(S("g_probs_T"), i * STEPS + n + 1)
                    for s in range(NT):
                        last = mm(ps[0:TP, 6 + h % 2, t * 64:(t + 1) * 64], probs_T[n % 2][:, s, :],
                                  vs[:, s, h * 64:(h + 1) * 64], start=(s == 0), stop=(s == NT - 1))
                    last.then_inc(S("g_pv"), 1)

                scores(0)
                rows_out(i, 3)
                scores(1)
                pe.wait_ge(S("g_k_lo"), i * 4 + 4)
                rows_out(i, 4)
                for n in range(STEPS + 1):
                    if n < STEPS:
                        turn_probs(n)
                    if n + 2 < STEPS:
                        scores(n + 2)
                    if n:
                        weigh(n - 1)
                if last_layer:
                    return
                pe.wait_ge(S("g_out"), i * GH + GH)
                for t in range(NT):
                    for q in range(NC2):
                        dst = ps[:, q, t * TP:(t + 1) * TP] if t < 4 else ps[:, 2, q * TP:(q + 1) * TP]
                        pe.transpose(dst, h_R[:, t, q * 128:(q + 1) * 128], ident[0:TP, 0:TP])\
                            .then_inc(S("gh_turned"), 1)
                project(i + 1, False)

            project(0, True)
            with pe.Fori(0, GL - 1) as i:
                attention(i, False)
            attention(GL - 1, True)

            turn("xm", n_R, 0)
            turned("xm")
            pe.wait_ge(S("gates_loaded"), 48)
            for t in range(NT):
                last = to_R(ps[0:TP, 7, t * 16:(t + 1) * 16], lambda k: c_T[:, k, :], t, lambda k: gate_w[:, k, 0:16])
            last.then_inc(S("logits_done"), 1)

            def bias_rows(name, biases, n):
                for t in range(NT):
                    mm(ps[0:TP, 7 - t // 2, (t % 2) * D:(t % 2 + 1) * D],
                       gate_T[0:n, t * TP:(t + 1) * TP], biases[:], start=True, stop=True).then_inc(S(f"{name}_b_done"), 1)

            def expert_y(name, hidden, e, w, first, K):
                for t in range(NT):
                    if t % 2 == 0 and not first:
                        pe.wait_ge(S(f"{name}_acc"), e * NT + min(t + 2, NT) - NT)
                    last = to_R(ps[0:TP, 4 + t // 2, (t % 2) * D:(t % 2 + 1) * D], hidden, t, w, K)
                    if t % 2 or t == NT - 1:
                        last.then_inc(S(f"{name}_y_done"), 1)

            pe.wait_ge(S("picked_ready"), 1)
            for t in range(NT):
                for s in range(t + 1):
                    mm(ps[0:TP, 6, t * 16:(t + 1) * 16], (before if s == t else ones_b)[:, 0:TP], picked[:, s, :],
                       start=(s == 0), stop=(s == t))
            for s in range(NT):
                last = mm(ps[0:TP, 6, 128:144], ones_b[:, 0:TP], picked[:, s, :], start=(s == 0), stop=(s == NT - 1))
            last.then_inc(S("ranked"), 1)
            pe.wait_ge(S("ones_ready"), 1)
            for h in range(2):
                for s in range(NT):
                    last = mm(ps[:, 4 + h, 0:HALF], ones[:], count[:, s, h * HALF:(h + 1) * HALF],
                              start=(s == 0), stop=(s == NT - 1))
            last.then_inc(S("deg_done"), 1)
            pe.wait_ge(S("gate_ready"), 1)
            for t in range(NT):
                pe.transpose(quads(2, 16)[:, t, :], gate[:, t, :], ident[0:TP, 0:TP]).then_inc(S("gate_turned"), 1)
            for k in range(2 * NT):
                pe.wait_ge(S("hot_ready"), k + 1)
                last = mm(ps[:, 7, 0:MT], row_hot[:, k, :], tile_hot[:, k, :], start=(k == 0), stop=(k == 2 * NT - 1))
            last.then_inc(S("inverted"), 1)

            def moe_turn(j, u, k, first=False):
                pe.wait_ge(S(f"moe_gathered{u}"), k * 16)
                if not first:
                    pe.wait_ge(S("moe_T"), j - 1)
                for q in range(NC2):
                    pe.transpose(ps[:, u % 2, q * 128:(q + 1) * 128], tile_x[u][:, q * 128:(q + 1) * 128], ident[:])\
                        .then_inc(S("moe_turned"), 1)

            def moe_h(j, u, k, first=False):
                pe.wait_ge(S(f"w_loaded{u}"), k * 48)
                pe.wait_ge(S("moe_T"), j + 1)
                if not first:
                    pe.wait_ge(S("moe_relu"), j - 1)
                for m in range(4):
                    for q in range(NC2):
                        last = mm(ps[:, 2 + u % 2, m * SLOT:(m + 1) * SLOT], w1_moe[u][:, q, m * 128:(m + 1) * 128],
                                  tile_xT[u % 2][:, q, :], start=(q == 0), stop=(q == 1))
                last.then_inc(S("moe_h_done"), 1)

            def moe_y(j, u, first=False):
                pe.wait_ge(S("moe_relu"), j + 1)
                if not first:
                    pe.wait_ge(S("moe_y_out"), j - 1)
                for m in range(4):
                    last = mm(ps[:, 4 + u % 2, 0:D], tile_h[u % 2][:, m, :], w2_moe[u][:, m, :],
                              start=(m == 0), stop=(m == 3))
                last.then_inc(S("moe_y_done"), 1)

            moe_turn(0, 0, 1, True)
            pe.wait_ge(S("gate_T_ready"), 1)
            pe.wait_ge(S("deg_read"), 1)
            bias_rows("moe", moe_b2, E0)
            moe_turn(1, 1, 1, True)
            moe_h(0, 0, 1, True)
            moe_turn(2, 2, 1)
            moe_h(1, 1, 1, True)
            pe.wait_ge(S("moe_bias_in"), NT)
            moe_y(0, 0, True)
            moe_turn(3, 3, 1)
            moe_h(2, 2, 1)
            moe_y(1, 1, True)
            moe_turn(4, 0, 2)
            moe_h(3, 3, 1)
            moe_y(2, 2)
            with pe.Fori(1, MT // TB) as g:
                for u in range(TB):
                    after = (u + 1) % TB
                    moe_turn(g * TB + (u + 1), after, g + (1 if after else 2))
                    moe_h(g * TB + u, u, g + 1)
                    moe_y(g * TB + (u - 1), (u - 1) % TB)
            moe_h(MT - 1, 0, MT // TB + 1)
            moe_y(MT - 2, TB - 1)
            moe_y(MT - 1, 0)

            turn("x2", n_R, 0)
            turned("x2")
            pe.wait_ge(S("w_m1_loaded"), 16)
            for m in range(NC2):
                to_T(4 + 2 * m, w_m1, n_T, m * 128).then_inc(S("m1_q_done"), 1)
            def aggregate(l, src_R):
                for m in range(NC2):
                    for h in range(2):
                        for s in range(NT):
                            last = mm(ps[:, 2 * m + h, 0:HALF], src_R[:, s, m * 128:(m + 1) * 128],
                                      count[:, s, h * HALF:(h + 1) * HALF], start=(s == 0), stop=(s == NT - 1))
                    last.then_inc(S("agg_done"), 1)

            aggregate(0, n_R)
            for t in range(NT):
                if t == 0:
                    pe.wait_ge(S("m1_q"), 1)
                if t == 2:
                    pe.wait_ge(S("m1_q"), 2)
                if t == 4:
                    pe.wait_ge(S("m1_kv"), 1)
                to_R(ps[0:TP, 4 + t % 4, :], lambda k: n_T[:, k, :], t, lambda k: w_m1[:, k, D:3 * D])\
                    .then_inc(S("m1_kv_done"), 1)

            def graph_rows(l):
                pe.wait_ge(S("agg_out"), 2 * l + 2)
                for t in range(NT):
                    if t == 4:
                        pe.wait_ge(S("g1_h"), l * NT + 1)
                    to_R(ps[0:TP, t % 4, 0:D], lambda k: a_T[:, k, :], t, lambda k: w_g1[:, k, l * D:(l + 1) * D])\
                        .then_inc(S("g1_h_done"), 1)

            pe.wait_ge(S("m1_kv"), NT)
            for q in range(2):
                for t in range(NT):
                    last = mm(ps[:, 5, q * 128:(q + 1) * 128], vs[:, t, q * 128:(q + 1) * 128],
                              vs[:, t, D + q * 128:D + (q + 1) * 128], start=(t == 0), stop=(t == NT - 1))
                last.then_inc(S("m1_at_done"), 1)
            pe.wait_ge(S("w_g1_loaded"), 16)
            graph_rows(0)
            pe.wait_ge(S("m1_attn"), 4)
            for q in range(2):
                pe.transpose(ps[:, 6, q * 128:(q + 1) * 128], at_sb[:, q, :], ident[:]).then_inc(S("at_turned"), 1)
            pe.wait_ge(S("at_T_ready"), 1)
            for t in range(NT):
                if t == 4:
                    pe.wait_ge(S("m1_xf"), 1)
                for q in range(2):
                    last = mm(ps[0:TP, 4 + t % 4, q * 128:(q + 1) * 128], q_T[:, q, t * TP:(t + 1) * TP],
                              at_T[:, q, :], start=True, stop=True)
                last.then_inc(S("m1_xf_done"), 1)
            pe.wait_ge(S("g1_x"), 1)
            for t in range(NT):
                for q in range(NC2):
                    dst = ps[:, q, t * TP:(t + 1) * TP] if t < 4 else ps[:, 2, q * TP:(q + 1) * TP]
                    pe.transpose(dst, y_R[:, t, q * 128:(q + 1) * 128], ident[0:TP, 0:TP]).then_inc(S("rows_turned"), 1)
            turn("y1", h_R, 4)
            turned("g1")
            aggregate(1, y_R)
            turned("y1")
            for m in range(HM // 128):
                if m >= 2:
                    pe.wait_ge(S("fc1_gelu"), m - 1)
                to_T(4 + 2 * (m % 2), w_m1, b_T, 3 * D + m * 128).then_inc(S("fc1_done"), 1)
            graph_rows(1)
            pe.wait_ge(S("w_fc2_loaded"), 16)
            pe.wait_ge(S("fc1_gelu"), HM // 128)
            for t in range(NT):
                if t == 4:
                    pe.wait_ge(S("fc2_out"), 1)
                to_R(ps[0:TP, 4 + t % 4, 0:D], lambda k: (hid[0][:, k, :] if k < 4 else hid[1][:, k - 4, :]), t,
                     lambda k: w_fc2[:, k, :], HM // 128).then_inc(S("fc2_done"), 1)

            turn("x3", n_R, 0)
            turned("x3")
            for t in range(NT):
                last = to_R(ps[0:TP, 7, t * E1:(t + 1) * E1], lambda k: c_T[:, k, :], t, lambda k: gate_w[:, k, 16:16 + E1])
            last.then_inc(S("logits2_done"), 1)

            def ffn_h(e, u, k, first):
                for m in range(NC2):
                    if k == 1:
                        if m == 0:
                            pe.wait_ge(S("ffn_relu"), e * 4 + 2)
                    elif not first:
                        pe.wait_ge(S("ffn_relu"), e * 4 + m - 1)
                    src = c_T if k == 0 else hid[u]
                    to_T(2 * m, w3_ffn[u][k], src, m * 128).then_inc(S("ffn_h_done"), 1)

            def ffn_y(e, u, first):
                pe.wait_ge(S("ffn_relu"), e * 4 + 4)
                expert_y("ffn", lambda k: hid[u][:, 2 + k, :], e, lambda k: w3_ffn[u][2][:, k, :], first, 2)

            pe.wait_ge(S("ffn_loaded0"), 48)
            ffn_h(0, 0, 0, True)
            pe.wait_ge(S("gate2_ready"), 1)
            for t in range(NT):
                pe.transpose(quads(4, E1)[:, t, :], gate2[:, t, 0:E1], ident[0:TP, 0:TP]).then_inc(S("gate2_turned"), 1)
            pe.wait_ge(S("gate2_T_ready"), 1)
            bias_rows("ffn", moe_bo, E1)
            ffn_h(0, 0, 1, True)
            pe.wait_ge(S("ffn_loaded1"), 48)
            ffn_h(1, 1, 0, False)
            pe.wait_ge(S("ffn_bias_in"), NT)
            ffn_y(0, 0, True)
            ffn_h(1, 1, 1, False)
            with pe.Fori(1, E1 // 2) as g:
                pe.wait_ge(S("ffn_loaded0"), g * 48 + 48)
                ffn_h(g * 2, 0, 0, False)
                ffn_y(g * 2 - 1, 1, False)
                ffn_h(g * 2, 0, 1, False)
                pe.wait_ge(S("ffn_loaded1"), g * 48 + 48)
                ffn_h(g * 2 + 1, 1, 0, False)
                ffn_y(g * 2, 0, False)
                ffn_h(g * 2 + 1, 1, 1, False)
            ffn_y(E1 - 1, 1, False)


def kernel(**inputs):
    import numpy as np
    import concourse.bacc as bacc
    from concourse import mybir as mb
    from concourse.bass_utils import run_bass_kernel_spmd

    a = {k: np.asarray(v) for k, v in inputs.items()}

    def columns(v):
        return np.reshape(v, (-1, 128)).T

    gates = np.zeros((D,), np.float32)
    gates[0:E0] = a["L0_ffn_gate_b"]
    gates[E0:E0 + E1] = a["L1_ffn_br"]
    b_qkv = a["L1_mix_b_qkv"]
    by_name = {
        "mix_ln1_g": a["L0_mix_ln1_g"], "mix_ln1_b": a["L0_mix_ln1_b"], "mix_b2": a["L0_mix_b2"],
        "mix_ln2_g": a["L0_mix_ln2_g"], "mix_ln2_b": a["L0_mix_ln2_b"],
        "moe_gamma": a["L0_ffn_gamma"], "moe_beta": a["L0_ffn_beta"],
        "g1_b0": a["L1_gnn_b0"], "g1_g0": a["L1_gnn_g0"], "g1_beta0": a["L1_gnn_beta0"],
        "g1_b1": a["L1_gnn_b1"], "g1_g1": a["L1_gnn_g1"], "g1_beta1": a["L1_gnn_beta1"],
        "m1_bk": b_qkv[D:2 * D], "m1_bv": b_qkv[2 * D:3 * D],
        "m1_norm_g": a["L1_mix_norm_g"], "m1_norm_b": a["L1_mix_norm_b"], "m1_bfc2": a["L1_mix_b_fc2"],
        "gates": gates,
        "mix_b1": a["L0_mix_b1"], "m1_bq": b_qkv[0:D], "m1_bfc1": a["L1_mix_b_fc1"],
        **{k: a[f"L1_ffn_{k}"] for k in ("b1", "g1", "be1", "m1", "v1", "b2", "g2", "be2", "m2", "v2")},
    }
    nothing = np.zeros((1, D), np.float32)
    bn_g = np.concatenate([a["L0_gnn_bn_gamma"], nothing])
    bn_b = np.concatenate([a["L0_gnn_bn_beta"], nothing])
    arrays = {
        "x": a["x"], "src": a["src"], "dst": a["dst"],
        "rows": np.stack([by_name[k] for k in ROWS]),
        "cols": np.concatenate([columns(by_name[k]) for k, _ in COLS], 1),
        "gw": np.stack([a["L0_gnn_Wq"], a["L0_gnn_Wk"], a["L0_gnn_Wv"], a["L0_gnn_Ws"]], 1),
        "gbias": np.concatenate([a["L0_gnn_bv"], a["L0_gnn_bs"]], 1),
        "gcols": np.concatenate([columns(v[i]) for i in range(GL)
                                 for v in (a["L0_gnn_bq"], a["L0_gnn_bk"], bn_g, bn_b)], 1),
        "w_mix": np.concatenate([a["L0_mix_Wqkv"].T, a["L0_mix_W1"].T, a["L0_mix_W2"].T], 1),
        "w_g1": np.concatenate([a["L1_gnn_W0"].T, a["L1_gnn_W1"].T], 1),
        "w_m1": np.concatenate([a["L1_mix_w_qkv"], a["L1_mix_w_fc1"]], 1),
        "w_fc2": a["L1_mix_w_fc2"],
        "gate_w": np.concatenate([a["L0_ffn_gate_w"], a["L1_ffn_Wr"]], 1),
        "moe_b1": np.transpose(np.reshape(a["L0_ffn_b1"], (E0, F0 // 128, 128)), (0, 2, 1)),
        "moe_w1": a["L0_ffn_w1"], "moe_w2": a["L0_ffn_w2"], "moe_b2": a["L0_ffn_b2"],
        "ffn_w": np.stack([a["L1_ffn_W1"], a["L1_ffn_W2"], a["L1_ffn_Wo"]], 1), "moe_bo": a["L1_ffn_bo"],
    }
    arrays = {f"in_{k}": np.ascontiguousarray(v) for k, v in arrays.items()}
    nc = bacc.Bacc("TRN2", target_bir_lowering=False, num_devices=1)
    A = {k[3:]: nc.dram_tensor(k, v.shape, mb.dt.from_np(v.dtype), kind="ExternalInput").ap() for k, v in arrays.items()}
    out = nc.dram_tensor("out_x", (N, D), mb.dt.float32, kind="ExternalOutput").ap()
    program(nc, A, out)
    r = run_bass_kernel_spmd(nc, [arrays], core_ids=[0])
    return r.results[0]["out_x"]
```

```python
from contextlib import ExitStack

import concourse.bass as bass
from concourse import mybir

ALU = mybir.AluOpType
ACT = mybir.ActivationFunctionType
F32 = mybir.dt.float32
F16 = mybir.dt.float16
F32R = mybir.dt.float32r
BF16 = mybir.dt.bfloat16
I32 = mybir.dt.int32
I16 = mybir.dt.int16
U32 = mybir.dt.uint32
AX = mybir.AxisListType.X

N = 625
TP = 125
NT = N // TP
D = 256
NC2 = D // 128
HALF = 314
NP = 2 * HALF
EDGES = 10625
ET = EDGES // TP
E0, F0 = 16, 512
SLOT = 128
MT = E0 + 2 * N // SLOT
TB = 6
E1 = 8
HM = 3 * D
GL = 3
GH = 4
STEPS = GH * NT
ROWS_BANK = [2, 3, 4, 5, 7]
MASK = -8.0e30
HAS_EDGE = -1.0e29
FIELD = 4096
CHUNKS = [(0, 32), (32, 64), (64, ET)]

ROWS = ["mix_ln1_g", "mix_ln1_b", "mix_b2", "mix_ln2_g", "mix_ln2_b", "moe_gamma", "moe_beta",
        "g1_b0", "g1_g0", "g1_beta0", "g1_b1", "g1_g1", "g1_beta1",
        "m1_bk", "m1_bv", "m1_norm_g", "m1_norm_b", "m1_bfc2", "gates"]
COLS = [("mix_b1", 2), ("m1_bq", 2), ("m1_bfc1", 6)] + \
       [(k, 2 * E1) for k in ("b1", "g1", "be1", "m1", "v1", "b2", "g2", "be2", "m2", "v2")]
NCOLS = sum(n for _, n in COLS)


NORMS = ["ln0", "ln1", "ln2", "lnm", "lny", "lnx", "lnh", "gn0", "gn1", "lnf"]
TURNS = ["n0", "m1", "xm", "x2", "y1", "g1", "x3"]

GROUPS = [(0, 3), (3, NT)]
READY = ["n0", "m1", "xm", "x2", "y1", "x3"]


class Steps:

    def __init__(self, eng, sem, base=0):
        self.eng, self.sem, self.base, self.n = eng, sem, base, 0

    def step(self, ins):
        ins.then_inc(self.sem, 1)
        self.n += 1

    def settle(self):
        self.eng.wait_ge(self.sem, self.base + self.n)

    def link(self, ins):
        self.step(ins)
        self.settle()


def program(nc, A, out):
    with ExitStack() as ctx:
        def sb(name, shape, dt=F32):
            return ctx.enter_context(nc.sbuf_tensor(name, shape, dt))

        sems = {}

        def S(name):
            if name not in sems:
                sems[name] = ctx.enter_context(nc.semaphore(name))
            return sems[name]

        ps = ctx.enter_context(nc.psum_tensor("ps", [128, 8, 512], F32))

        def pair(b, rows=128):
            return ps[0:rows, b:b + 2, 0:HALF]

        def quads(b, rows=TP):
            return ps[0:rows, b:b + 2, :].rearrange("p b n -> p (b n)")[:, 0:640]\
                .rearrange("p (t n) -> p t n", n=128)[:, :, 0:TP]

        def halves(ap):
            return ap.rearrange("p (b n) -> p b n", b=2)

        ident = sb("ident", [128, 128])
        node_ids = sb("node_ids", [TP, N], I16)
        expert_ids = sb("expert_ids", [TP, 16])
        neg_half = sb("neg_half", [128, 2 * E1 * 2])
        ones = sb("ones", [TP, 128])
        to_floor = sb("to_floor", [TP, 1])
        minus_one = sb("minus_one", [TP, 1])
        head_mask = sb("head_mask", [128, 4, 32])
        head_cols = sb("head_cols", [128, 4])

        rows = sb("rows", [TP, len(ROWS), D])
        cols = sb("cols", [128, NCOLS])
        row = {k: rows[:, i, :] for i, k in enumerate(ROWS)}
        col, at = {}, 0
        for k, n in COLS:
            col[k] = (at, n)
            at += n
        gw = sb("gw", [128, 4, NC2, D])
        gbias = sb("gbias", [TP, 2 * D])
        gcols = sb("gcols", [128, GL * 8])
        w_g1 = sb("w_g1", [128, NC2, 2 * D])
        w_m1 = sb("w_m1", [128, NC2, 3 * D + HM])
        w_mix = w_m1[:, :, 0:5 * D]
        gate_w = sb("gate_w", [128, NC2, E0 + E1])
        moe_b2 = sb("moe_b2", [E0, D])
        moe_bo = sb("moe_bo", [E1, D])
        ring = sb("ring", [128, 2, 8 * D])
        w3_ffn = [[ring[:, u, k * 2 * D:(k + 1) * 2 * D] for k in range(3)] for u in range(2)]

        def R(name):
            return sb(name, [TP, NT, D])

        def T(name):
            return sb(name, [128, NC2, NP])

        x_R, n_R, mix_R, h_R, y_R = [R(k) for k in ("x_R", "n_R", "mix_R", "h_R", "y_R")]
        with nc.sbuf_tensor("parts", [128, 2 * GH + 2, NP], F32R) as parts:
            q_parts = [parts[:, h, :] for h in range(GH)]
            k_parts = [parts[:, GH + h, :] for h in range(GH)]
            k_lo = [parts[:, 2 * GH + k, :] for k in range(2)]
        with nc.sbuf_tensor("spare0", [128, 4 * F0], F32) as spare0:
            pass
        q_T, k_T, b_T, c_T = [T(k) for k in ("q_T", "k_T", "b_T", "c_T")]
        with nc.sbuf_tensor("hid2_parts", [128, 2, NC2, NP], F32R) as hid2_parts:
            pass
        big1 = sb("big1", [128, 5 * NP])
        with nc.sbuf_tensor("spare1", [128, 4 * F0], F32) as spare1:
            spare = [spare0, spare1]
        with nc.sbuf_tensor("x_parts", [128, 2, NC2, NP], F32R) as x_parts:
            pass
        n_T, a_T = T("n_T"), T("a_T")
        with nc.sbuf_tensor("w_parts0", [128, 2, 6 * D], F32R) as w_parts0:
            pass
        count = sb("count", [TP, NT, NP])
        with nc.sbuf_tensor("w_parts1", [128, 2, 6 * D], F32R) as w_parts1:
            w_parts = [w_parts0, w_parts1]
        logc_all = sb("logc", [128, NT * NP])
        logc = logc_all[0:TP].rearrange("p (t n) -> p t n", t=NT)
        vones = logc_all[0:TP, 0:NT * 258].rearrange("p (t c n) -> p t c n", t=NT, c=2)
        w_fc2 = logc_all[:, 0:HM // 128 * D].rearrange("p (c n) -> p c n", n=D)
        with nc.sbuf_tensor("hid1_parts", [128, 2, NC2, NP], F32R) as hid1_parts:
            hid_parts = [hid1_parts, hid2_parts]
        big2 = sb("big2", [128, 4 * NP + 640])
        idx = sb("idx", [TP, 2, ET], I32)
        idf = sb("idf", [TP, 4, ET])
        oh_dst_all = sb("oh_dst", [128, 4, N + 1], BF16)
        oh_dst = oh_dst_all[0:TP]
        small = oh_dst_all.rearrange("p a n -> p (a n)").bitcast(F32)
        oh_src = sb("oh_src", [TP, 4, HALF], BF16)
        vs = sb("vs", [TP, NT, 2 * D])
        stats = {k: (sb(f"st_{k}", [TP, NT, 6]), sb(f"mv_{k}", [TP, NT, 2]),
                     sb(f"ve_{k}", [TP, NT]), sb(f"rs_{k}", [TP, NT]))
                 for k in NORMS}

        cnt_new = big1[0:TP, 0:NT * HALF].rearrange("p (t n) -> p t n", t=NT)
        cnt_lo = big1[0:TP, NT * HALF:2 * NT * HALF].rearrange("p (t n) -> p t n", t=NT)
        cnt_hi = big2[0:TP, 0:NT * HALF].rearrange("p (t n) -> p t n", t=NT)
        cnt_upper = big2[0:TP, NT * HALF:2 * NT * HALF].bitcast(I32).rearrange("p (t n) -> p t n", t=NT)
        probs = [big1[0:TP, k * NP:(k + 1) * NP] for k in range(2, 5)]
        probs_T = [big2[0:TP, k * 640:k * 640 + N].rearrange("p (s n) -> p s n", s=NT) for k in range(2)]
        tile_x = [big1[:, k * D:(k + 1) * D] for k in range(TB)]
        tile_xT = [big1[:, (TB + k) * D:(TB + k + 1) * D].rearrange("p (c n) -> p c n", c=2) for k in range(2)]
        tile_y = [big1[:, (TB + 2 + k) * D:(TB + 3 + k) * D] for k in range(2)]
        tile_h = [big2[:, k * 512:(k + 1) * 512].rearrange("p (m n) -> p m n", m=4) for k in range(2)]
        gw_flat = gw[:].rearrange("p m c n -> p (m c n)")
        W = 2 * F0
        w1_moe = [b.rearrange("p (c n) -> p c n", c=2) for b in
                  (ring[:, 0, 0:W], ring[:, 1, 0:W], gw_flat[:, 0:W], logc_all[:, HM // 128 * D:HM // 128 * D + W],
                   spare[0][:, 0:W], spare[1][:, 0:W])]
        w2_moe = [b.rearrange("p (c n) -> p c n", c=4) for b in
                  (ring[:, 0, W:2 * W], ring[:, 1, W:2 * W], gw_flat[:, W:2 * W], big2[:, 1856:1856 + W],
                   spare[0][:, W:2 * W], spare[1][:, W:2 * W])]
        hid = [b[:, 0:4 * NP].rearrange("p (m n) -> p m n", m=4) for b in (big1, big2)]

        hid_whole = [q_T, k_T]

        kv_sb = sb("kv_sb", [128, 2, 132])
        ek = sb("ek", [TP, 2, D])
        eq = sb("eq", [128, 2, HALF])
        zden = sb("zden", [TP, 2, NT, 8])
        gmax = sb("gmax", [TP, STEPS])
        gneg = sb("gneg", [TP, STEPS])
        gden = sb("gden", [TP, STEPS])
        grec = sb("grec", [TP, STEPS])
        att = sb("att", [TP, NT, 64])
        bst = sb("bst", [128, 2, 2, 6])
        bmv = sb("bmv", [128, 2, 2])
        bve = sb("bve", [128, 2])
        brs = sb("brs", [128, 2])
        bsc = sb("bsc", [128, 3, 2])
        lg = sb("lg", [TP, NT, 16])
        top = sb("top", [TP, NT, 8])
        topi = sb("topi", [TP, NT, 8], U32)
        topf = sb("topf", [TP, NT, 2])
        tw = sb("tw", [TP, 4, NT])
        pick = big2[0:TP, 1536:1696].rearrange("p (k t e) -> p k t e", k=2, t=NT)
        picked = sb("picked", [TP, NT, 16], BF16)
        before = sb("before", [TP, TP], BF16)
        ones_b = sb("ones_b", [TP, 128], BF16)
        tiles = sb("tiles", [TP, 3, 32])
        tiles_i = sb("tiles_i", [TP, 16], I32)
        place = big2[0:TP, 1696:1856].rearrange("p (k t e) -> p k t e", k=2, t=NT)
        slot = sb("slot", [TP, 3, 2 * NT])
        slot_i = sb("slot_i", [TP, 3, 2 * NT], I32)
        row_hot = big2[0:TP, 0:NT * SLOT].bitcast(F16).rearrange("p (k n) -> p k n", k=2 * NT)
        tile_hot = big2[0:TP, NT * SLOT:NT * (SLOT + MT)].bitcast(F16).rearrange("p (k n) -> p k n", k=2 * NT)
        ids_i = sb("ids_i", [128, SLOT], I32)
        row_ids = sb("row_ids", [TP, SLOT])
        tile_ids = sb("tile_ids", [TP, MT])
        choice_ids = sb("choice_ids", [TP, 2 * NT])
        spare_ids = sb("spare_ids", [128, MT])
        own_tile = big2[0:1, 1024:1024 + (MT - E0) * 16].rearrange("p (j e) -> p j e", j=MT - E0)
        tile_e = sb("tile_e", [1, MT - E0])
        tile_expert = sb("tile_expert", [1, MT], I32)
        slot_m = sb("slot_m", [128, 2, MT])
        from_row = sb("from_row", [128, MT], I32)
        to_row = sb("to_row", [128, MT], I32)
        row_at = sb("row_at", [128, TB + 2], I32)
        b1_moe = sb("b1_moe", [128, TB, 4])
        gate = sb("gate", [TP, NT, 16])
        gate2 = sb("gate2", [TP, NT, 16])
        gate_T = eq[0:16].rearrange("p a n -> p (a n)")[:, 0:N]
        inv_deg = sb("inv_deg", [128, NP])
        at_sb, at_T = [small[:, k * 256:(k + 1) * 256].rearrange("p (c n) -> p c n", c=2) for k in range(2)]
        bn_v, bn_r, bn_s, bn_b, bn_t = [small[:, 512 + k * 4 * E1:512 + (k + 1) * 4 * E1] for k in range(5)]
        at_m = small[:, 704:720].rearrange("p (k n) -> p k n", k=4)

        def c(name, j=0, n=1):
            return cols[:, col[name][0] + j:col[name][0] + j + n]

        def wide(r):
            return r.unsqueeze(1).broadcast_to([TP, NT, D])

        moe_in = nc.dram_tensor("moe_in", (N, D), F32, kind="Internal").ap()
        moe_out = nc.dram_tensor("moe_out", (1 + 2 * N + MT * SLOT, D), F32, kind="Internal").ap()

        block = ctx.enter_context(nc.Block())

        @block.sync
        def _(sp):
            sp.dma_start(idx[:, 0, :], A["src"].rearrange("(p j) -> p j", p=TP)).then_inc(S("edges_loaded"), 16)
            sp.dma_start(idx[:, 1, :], A["dst"].rearrange("(p j) -> p j", p=TP)).then_inc(S("edges_loaded"), 16)
            sp.dma_start(x_R[:], A["x"].rearrange("(t p) f -> p t f", p=TP)).then_inc(S("x_loaded"), 16)
            sp.dma_start(w_mix, A["w_mix"].rearrange("(c p) n -> p c n", p=128)).then_inc(S("w_mix_loaded"), 16)
            sp.dma_start(rows[:], A["rows"].unsqueeze(0).broadcast_to([TP, len(ROWS), D])).then_inc(S("rows_loaded"), 16)
            sp.dma_start(cols[:], A["cols"]).then_inc(S("cols_loaded"), 16)

            def attention_weights(i, first):
                if not first:
                    sp.wait_ge(S("g_rows_read"), i * NT)
                sp.dma_start(gw[:], A["gw"][bass.ds(i, 1)].rearrange("a m (c p) n -> p (a m) c n", p=128))\
                    .then_inc(S("gw_loaded"), 16)
                sp.dma_start(gbias[:], A["gbias"][bass.ds(i, 1)].broadcast_to([TP, 2 * D]))\
                    .then_inc(S("gw_loaded"), 16)

            sp.dma_start(gcols[:], A["gcols"]).then_inc(S("gcols_loaded"), 16)
            attention_weights(0, True)
            sp.dma_start(w_g1[:], A["w_g1"].rearrange("(c p) n -> p c n", p=128)).then_inc(S("w_g1_loaded"), 16)
            sp.dma_start(gate_w[:], A["gate_w"].rearrange("(c p) n -> p c n", p=128)).then_inc(S("gates_loaded"), 16)
            sp.dma_start(moe_b2[:], A["moe_b2"]).then_inc(S("gates_loaded"), 16)
            sp.dma_start(moe_bo[:], A["moe_bo"]).then_inc(S("gates_loaded"), 16)
            sp.wait_ge(S("my_done"), NT)
            sp.dma_start(w_m1[:], A["w_m1"].rearrange("(c p) n -> p c n", p=128)).then_inc(S("w_m1_loaded"), 16)

            def expert_weights(j, u, e):
                sp.dma_start(w1_moe[u], A["moe_w1"][bass.ds(e, 1)].rearrange("a (c p) n -> p (a c) n", p=128))\
                    .then_inc(S(f"w_loaded{u}"), 16)
                sp.dma_start(w2_moe[u], A["moe_w2"][bass.ds(e, 1)].rearrange("a (c p) n -> p (a c) n", p=128))\
                    .then_inc(S(f"w_loaded{u}"), 16)
                sp.dma_start(b1_moe[:, u, :], A["moe_b1"][bass.ds(e, 1)].rearrange("a p m -> (a p) m"))\
                    .then_inc(S(f"w_loaded{u}"), 16)

            with sp.Fori(1, GL) as i:
                attention_weights(i, False)
            for j in range(2):
                expert_weights(j, j, j)
            sp.wait_ge(S("g_rows_read"), GL * NT)
            expert_weights(2, 2, 2)
            sp.wait_ge(S("g_max"), GL * STEPS)
            sp.dma_start(w_fc2, A["w_fc2"].rearrange("(c p) n -> p c n", p=128)).then_inc(S("w_fc2_loaded"), 16)
            expert_weights(3, 3, 3)
            expert_weights(4, 4, 4)
            expert_weights(5, 5, 5)
            sp.wait_ge(S("rows_ready"), READY.index("xm") + 1)
            sp.dma_start(moe_in.rearrange("(t p) f -> p t f", p=TP), n_R[:]).then_inc(S("moe_in_stored"), 16)
            sp.wait_ge(S("tile_expert_ready"), 1)

            def tile_weights(j, u):
                e = sp.value_load(tile_expert[0:1, bass.ds(j, 1)], min_val=0, max_val=E0 - 1)
                sp.wait_ge(S("moe_y_done"), j - (TB - 1))
                expert_weights(j, u, e)

            with sp.Fori(1, MT // TB) as g:
                for u in range(TB):
                    tile_weights(g * TB + u, u)
            tile_weights(MT - 1, 0)
            sp.wait_ge(S("moe_scattered0"), 16 * (MT - MT // 2))
            sp.wait_ge(S("moe_scattered1"), 16 * (MT // 2))
            for k in range(2):
                sp.dma_start(vs[:].rearrange("p t (a f) -> p (t a) f", a=2)[:, k * NT:(k + 1) * NT],
                             moe_out[1 + k * N:1 + (k + 1) * N].rearrange("(k p) f -> p k f", p=TP))\
                    .then_inc(S(f"choice{k}_loaded"), 16)

            def ffn_weights(e, u):
                sp.dma_start(w3_ffn[u][0], A["ffn_w"][bass.ds(e, 1), 0].rearrange("a (c p) n -> p (a c) n", p=128))\
                    .then_inc(S(f"ffn_loaded{u}"), 16)
                sp.dma_start(w3_ffn[u][1], A["ffn_w"][bass.ds(e, 1), 1].rearrange("a (c p) n -> p (a c) n", p=128))\
                    .then_inc(S(f"ffn_loaded{u}"), 16)
                sp.dma_start(w3_ffn[u][2], A["ffn_w"][bass.ds(e, 1), 2].rearrange("a (c p) n -> p (a c) n", p=128))\
                    .then_inc(S(f"ffn_loaded{u}"), 16)

            sp.wait_ge(S("moe_y_done"), MT)
            for e in range(2):
                ffn_weights(e, e)
            with sp.Fori(1, E1 // 2) as g:
                for u in range(2):
                    sp.wait_ge(S("w_lo"), (g * 2 + u - 1) * 3)
                    ffn_weights(g * 2 + u, u)
            for t in range(NT):
                sp.wait_ge(S("ffn_acc"), (E1 - 1) * NT + t + 1)
                sp.dma_start(out[t * TP:(t + 1) * TP], x_R[:, t, :]).then_inc(S("stored"), 16)
            sp.wait_ge(S("stored"), NT * 16)

        @block.gpsimd
        def _(pool):
            own = Steps(pool, S("pool_steps"))

            def rstd(name):
                st, mv, ve, rs = stats[name]
                for g, (a, b) in enumerate(GROUPS):
                    pool.wait_ge(S("norm_var"), 2 * NORMS.index(name) + g + 1)
                    pool.tensor_tensor(rs[:, a:b], ve[:, a:b], neg_half[0:TP, a:b], ALU.pow).then_inc(S("norm_rstd"), 1)

            pool.iota(node_ids[:], pattern=[[1, N]], base=0, channel_multiplier=0).then_inc(S("ids_ready"), 1)
            pool.memset(to_floor[:], -0.48828125).then_inc(S("ids_ready"), 1)
            own.step(pool.memset(minus_one[:], -1.0))
            own.step(pool.memset(neg_half[:], -0.5))
            own.step(pool.memset(ident[:], 0.0))
            own.step(pool.memset(head_mask[:], 1.0))
            own.link(pool.memset(head_cols[:], 1.0))
            pool.affine_select(out=ident[:], in_=ident[:], compare_op=ALU.not_equal, fill=1.0, base=0,
                               pattern=[[-1, 128]], channel_multiplier=1).then_inc(S("ident_ready"), 1)
            for t in (n_T, a_T):
                pool.memset(t[:, :, N:NP], 0.0).then_inc(S("pads_ready"), 1)
            rstd("ln0")

            def split_counts(k, lower, upper):
                pool.wait_ge(S("counts_out"), k + 1)
                own.link(pool.tensor_copy(upper, cnt_upper))
                own.link(pool.tensor_scalar(lower, upper, -float(FIELD), None, ALU.mult))

            pool.memset(vones[:, :, :, 128:129], 1.0).then_inc(S("constants_ready"), 1)
            own.step(pool.affine_select(out=head_mask[:], in_=head_mask[:], compare_op=ALU.is_ge, fill=0.0, base=0,
                                        pattern=[[-32, 4], [0, 32]], channel_multiplier=1))
            own.link(pool.affine_select(out=head_cols[:], in_=head_cols[:], compare_op=ALU.is_ge, fill=0.0, base=0,
                                        pattern=[[-32, 4]], channel_multiplier=1))
            pool.affine_select(out=head_mask[:], in_=head_mask[:], compare_op=ALU.is_ge, fill=0.0, base=31,
                               pattern=[[32, 4], [0, 32]], channel_multiplier=-1).then_inc(S("constants_ready"), 1)
            pool.affine_select(out=head_cols[:], in_=head_cols[:], compare_op=ALU.is_ge, fill=0.0, base=31,
                               pattern=[[32, 4]], channel_multiplier=-1).then_inc(S("constants_ready"), 1)
            split_counts(0, cnt_lo, cnt_hi)
            pool.tensor_tensor(cnt_lo, cnt_lo, cnt_new, ALU.add).then_inc(S("counts_added"), 1)
            pool.wait_ge(S("counts_added"), 1)
            lower, upper = count[:, :, 0:HALF], count[:, :, HALF:NP]
            split_counts(1, lower, upper)
            rstd("ln1")
            own.link(pool.tensor_tensor(lower, lower, cnt_new, ALU.add))
            own.step(pool.tensor_tensor(cnt_lo, cnt_lo, lower, ALU.add))
            pool.tensor_tensor(cnt_hi, cnt_hi, upper, ALU.add).then_inc(S("counts_added"), 1)
            pool.wait_ge(S("counts_added"), 2)
            for ids, pattern, base, down in ((expert_ids, [[1, 16]], 0, 0), (row_ids, [[1, SLOT]], 0, 0),
                                             (tile_ids, [[1, MT]], 0, 0), (choice_ids, [[TP, 2 * NT]], 1, 1),
                                             (spare_ids, [[SLOT, MT]], 1 + 2 * N, 1)):
                p, n = ids.shape
                own.link(pool.iota(ids_i[0:p, 0:n], pattern=pattern, base=base, channel_multiplier=down))
                own.link(pool.tensor_copy(ids[:], ids_i[0:p, 0:n]))
            own.step(pool.memset(ones_b[:], 1.0))
            own.step(pool.memset(tiles[:], 0.0))
            own.link(pool.memset(before[:], 0.0))
            pool.affine_select(out=before[:], in_=before[:], compare_op=ALU.is_ge, fill=1.0, base=0,
                               pattern=[[-1, TP]], channel_multiplier=1).then_inc(S("constants_ready"), 1)
            pool.memset(ones[:], 1.0).then_inc(S("constants_ready"), 1)
            pool.wait_ge(S("counts_out"), 3)
            pool.memset(at_sb[:], 0.0).then_inc(S("constants_ready"), 1)

            pool.wait_ge(S("bn_var"), 2)
            pool.tensor_tensor(bn_r[:], bn_v[:], neg_half[:, 0:4 * E1], ALU.pow).then_inc(S("bn_rstd"), 1)

            def attention(i, last):
                for n in range(STEPS):
                    pool.wait_ge(S("g_max"), i * STEPS + n + 1)
                    pool.tensor_tensor(gneg[:, n:n + 1], gmax[:, n:n + 1], minus_one[:], ALU.mult)\
                        .then_inc(S("g_neg"), 1)
                    if last and n == 6:
                        rstd("ln2")
                if not last:
                    for m in range(NC2):
                        pool.wait_ge(S("g_var"), i * 2 + m + 1)
                        pool.tensor_tensor(brs[:, m:m + 1], bve[:, m:m + 1], neg_half[:, 0:1], ALU.pow)\
                            .then_inc(S("g_rstd"), 1)

            with pool.Fori(0, GL - 1) as i:
                attention(i, False)
            attention(GL - 1, True)
            rstd("lnm")
            pool.wait_ge(S("rows_placed"), 2)
            pool.wait_ge(S("moe_in_stored"), 16)

            def gather(j, u):
                pool.tensor_copy(row_at[:, u:u + 1], from_row[:, bass.ds(j, 1)]).then_inc(S("gather_at"), 1)
                pool.wait_ge(S("gather_at"), j + 1)
                pool.nop(nofuse=True)
                pool.indirect_dma_start(tile_x[u], None, moe_in,
                                        bass.IndirectOffsetOnAxis(ap=row_at[:, u:u + 1].bitcast(U32), axis=0))\
                    .then_inc(S(f"moe_gathered{u}"), 16)

            def scatter(j, u):
                pool.wait_ge(S("moe_y_out"), j + 1)
                pool.nop(nofuse=True)
                pool.tensor_copy(row_at[:, TB + u:TB + 1 + u], to_row[:, bass.ds(j, 1)]).then_inc(S("scatter_at"), 1)
                pool.wait_ge(S("scatter_at"), j + 1)
                pool.nop(nofuse=True)
                pool.indirect_dma_start(moe_out, bass.IndirectOffsetOnAxis(ap=row_at[:, TB + u:TB + 1 + u].bitcast(U32), axis=0),
                                        tile_y[u], None).then_inc(S(f"moe_scattered{u}"), 16)

            for j in range(TB):
                gather(j, j)
            with pool.Fori(0, MT // TB - 1) as g:
                for u in range(TB):
                    scatter(g * TB + u, u % 2)
                    gather(g * TB + (u + TB), u)
            scatter(MT - 1 - TB, 0)
            gather(MT - 1, 0)
            for j in range(MT - TB, MT):
                scatter(j, j % 2)
            for t in (n_T, k_T, b_T, c_T):
                pool.memset(t[:, :, N:NP], 0.0).then_inc(S("pads_ready"), 1)
            for name in ("lny", "lnx", "lnh", "gn0", "gn1"):
                rstd(name)

            def weight_hi(e, u, k, loads):
                pool.wait_ge(S(f"ffn_loaded{u}"), loads)
                pool.nop(nofuse=True)
                pool.tensor_copy(w_parts[u][:, 0, k * 2 * D:(k + 1) * 2 * D], w3_ffn[u][k]).then_inc(S("w_hi"), 1)

            pool.wait_ge(S("agg_done"), 4)
            for k in range(3):
                weight_hi(0, 0, k, 48)
            rstd("lnf")
            pool.wait_ge(S("fc2_done"), NT)
            for k in range(3):
                weight_hi(1, 1, k, 48)
            with pool.Fori(1, E1 // 2) as g:
                for u in range(2):
                    e = g * 2 + u
                    for k in range(3):
                        if k < 2:
                            pool.wait_ge(S("ffn_h_done"), e * 4 + (2 * k - 6))
                        else:
                            pool.wait_ge(S("ffn_y_done"), e * 3 - 3)
                        weight_hi(e, u, k, g * 48 + 48)

        @block.scalar
        def _(act):
            def evac_T(name, dst, bank):
                act.wait_ge(S("rows_turned"), 10 * TURNS.index(name) + 10)
                act.activation(dst[:, :, 0:4 * TP], ps[:, bank:bank + 2, 0:4 * TP], ACT.Identity)\
                    .then_inc(S("T_by_act"), 1)

            evac_T("n0", n_T, 5)

            def counts(k):
                act.wait_ge(S("onehot_used"), CHUNKS[k][1])
                if k:
                    act.wait_ge(S("counts_added"), k)
                act.activation(cnt_new, ps[0:TP, 0:NT, 0:HALF], ACT.Copy)
                act.activation(cnt_upper, ps[0:TP, 0:NT, 0:HALF], ACT.Identity, scale=1.0 / FIELD, bias=to_floor[:])\
                    .then_inc(S("counts_out"), 1)

            act.wait_ge(S("ids_ready"), 2)
            counts(0)
            for j in range(4):
                act.wait_ge(S("mq_done"), j + 1)
                if j >= 2:
                    act.wait_ge(S("mq_phi"), j - 1)
                act.activation(eq[:, j % 2, :], ps[:, 5 + j % 3, 0:HALF], ACT.Exp).then_inc(S("mq_exp"), 1)
            for t in range(NT):
                act.wait_ge(S("mkv_done"), t + 1)
                if t >= 2:
                    act.wait_ge(S("mkv_phi"), t - 1)
                act.activation(ek[:, t % 2, :], ps[0:TP, 5 + (4 + t) % 3, 0:D], ACT.Exp)
                act.activation(vones[:, t, :, 0:128],
                               ps[0:TP, 5 + (4 + t) % 3, D:2 * D].rearrange("p (c n) -> p c n", c=2), ACT.Copy)\
                    .then_inc(S("mkv_exp"), 1)
            counts(1)
            evac_T("m1", a_T, 5)
            counts(2)
            act.wait_ge(S("cols_loaded"), 16)
            for j in range(4):
                m, h = divmod(j, 2)
                act.wait_ge(S("mh_done"), j + 1)
                act.activation(b_T[:, m, h * HALF:(h + 1) * HALF], ps[:, 5 + (18 + j) % 3, 0:HALF], ACT.Gelu,
                               bias=c("mix_b1", m)).then_inc(S("mh_gelu"), 1)
            act.wait_ge(S("count_floor"), 1)
            act.activation(logc, logc, ACT.Ln).then_inc(S("count_ln"), 1)

            def project(i):
                for m in range(NC2):
                    act.wait_ge(S("g_q_done"), i * 2 + m + 1)
                    for h, z in ((2 * m, slice(0, 64)), (2 * m + 1, slice(64, 128))):
                        act.activation(halves(q_parts[h][z]), pair(2 * m)[z], ACT.Identity,
                                       bias=gcols[z, bass.ds(i * 8 + m, 1)]).then_inc(S("g_q"), 1)
                for m in range(NC2):
                    act.wait_ge(S("g_k_done"), i * 2 + m + 1)
                    for h, z in ((2 * m, slice(0, 64)), (2 * m + 1, slice(64, 128))):
                        act.activation(halves(k_parts[h][z]), pair(4 + 2 * m)[z], ACT.Identity,
                                       bias=gcols[z, bass.ds(i * 8 + (2 + m), 1)]).then_inc(S("g_k"), 1)
                    for h, z, other in ((2 * m, slice(0, 64), slice(64, 128)), (2 * m + 1, slice(64, 128), slice(0, 64))):
                        act.wait_ge(S("g_k"), i * 4 + h + 1)
                        act.activation(k_parts[h][other], k_parts[h][z], ACT.Copy).then_inc(S("g_k_twice"), 1)

            def attention(i, last):
                for n in range(STEPS + 1):
                    if n < STEPS:
                        act.wait_ge(S("g_neg"), i * STEPS + n + 1)
                        act.activation(probs[n % 3], probs[n % 3], ACT.Exp, bias=gneg[:, n:n + 1],
                                       accum_out=gden[:, n:n + 1]).then_inc(S("g_exp"), 1)
                    if n:
                        m = n - 1
                        act.wait_ge(S("g_turned"), i * STEPS + m + 1)
                        if m >= 2:
                            act.wait_ge(S("g_pv"), i * STEPS + m - 1)
                        act.activation(probs_T[m % 2], quads(4), ACT.Copy).then_inc(S("g_probs_T"), 1)
                if not last:
                    for m in range(NC2):
                        act.wait_ge(S("gh_turned"), i * 10 + (5 * m + 5))
                        act.activation(a_T[:, m, 0:4 * TP], ps[:, 2 * m, 0:4 * TP], ACT.Identity).then_inc(S("gh_T"), 1)
                    for m in range(NC2):
                        act.wait_ge(S("g_affine"), i * 2 + m + 1)
                        act.activation(n_T[:, m, 0:N], a_T[:, m, 0:N], ACT.Relu, bias=bsc[:, 2, m:m + 1],
                                       scale=bsc[:, 0, m:m + 1]).then_inc(S("g_next"), 1)
                    project(i + 1)

            act.wait_ge(S("gcols_loaded"), 16)
            project(0)
            with act.Fori(0, GL - 1) as i:
                attention(i, False)
            attention(GL - 1, True)

            evac_T("xm", c_T, 0)
            act.wait_ge(S("top_diff"), 1)
            act.activation(tw[:, 1, :], tw[:, 0, :], ACT.Exp).then_inc(S("top_exp"), 1)

            act.wait_ge(S("gate_turned"), NT)
            act.activation(gate_T.rearrange("p (t n) -> p t n", t=NT), quads(2, 16), ACT.Copy).then_inc(S("gate_T_ready"), 1)

            def moe_h(j, u, first):
                act.wait_ge(S("moe_h_done"), j + 1)
                if not first:
                    act.wait_ge(S("moe_y_done"), j - 1)
                for m in range(4):
                    last = act.activation(tile_h[u % 2][:, m, :], ps[:, 2 + u % 2, m * SLOT:(m + 1) * SLOT], ACT.Relu,
                                          bias=b1_moe[:, u, m:m + 1])
                last.then_inc(S("moe_relu"), 1)

            for j in range(TB):
                moe_h(j, j, j < 2)
            with act.Fori(1, MT // TB) as g:
                for u in range(TB):
                    moe_h(g * TB + u, u, False)
            moe_h(MT - 1, 0, False)

            evac_T("x2", n_T, 0)
            for m in range(NC2):
                act.wait_ge(S("m1_q_done"), m + 1)
                act.activation(halves(q_T[:, m, :]), pair(4 + 2 * m), ACT.Identity, bias=c("m1_bq", m))\
                    .then_inc(S("m1_q"), 1)
            for k in range(4):
                act.wait_ge(S("m1_neg"), k + 1)
                p, q = 64 * (k % 2), k // 2
                act.activation(at_sb[p:p + 64, q, p:p + 64], ps[p:p + 64, 5, q * 128 + p:q * 128 + p + 64], ACT.Exp,
                               bias=at_m[p:p + 64, k, 1:2], scale=0.125, accum_out=at_m[p:p + 64, k, 2:3])\
                    .then_inc(S("m1_exp"), 1)
            evac_T("y1", b_T, 4)

            def fc1_gelu(m):
                act.wait_ge(S("fc1_done"), m + 1)
                act.activation(halves(hid[0][:, m, :] if m < 4 else hid[1][:, m - 4, :]), pair(4 + 2 * (m % 2)),
                               ACT.Gelu, bias=c("m1_bfc1", m)).then_inc(S("fc1_gelu"), 1)

            for m in range(4):
                fc1_gelu(m)
            act.wait_ge(S("gn_normed"), 1)
            act.activation(y_R[:], y_R[:], ACT.Silu).then_inc(S("g1_x"), 1)
            for m in range(4, HM // 128):
                fc1_gelu(m)
            evac_T("g1", k_T, 0)
            act.wait_ge(S("gn_normed"), 2)
            act.activation(y_R[:], y_R[:], ACT.Silu).then_inc(S("g1_x"), 1)
            evac_T("x3", c_T, 0)
            act.wait_ge(S("T_by_act"), TURNS.index("x3") + 1)
            act.wait_ge(S("T_by_dve"), TURNS.index("x3") + 1)
            act.activation(x_parts[:, 0], c_T[:], ACT.Copy).then_inc(S("x_hi"), 1)
            act.wait_ge(S("gate2_shift"), 1)
            act.activation(gate2[:, :, 0:E1], gate2[:, :, 0:E1], ACT.Exp).then_inc(S("gate2_exp"), 1)

            act.wait_ge(S("bn_affine"), 1)

            def ffn(e, u, first):
                for k in range(2):
                    for m in range(NC2):
                        act.wait_ge(S("ffn_h_done"), e * 4 + 2 * k + m + 1)
                        if not first:
                            act.wait_ge(S("ffn_lo"), e * 4 + (2 * k + m - 3))
                        j = e * 2 + (2 * E1 * k + m)
                        act.activation(halves(hid_whole[k][:, m, :]), pair(2 * m), ACT.Relu,
                                       bias=bn_b[:, bass.ds(j, 1)], scale=bn_s[:, bass.ds(j, 1)]).then_inc(S("ffn_out"), 1)
                        act.wait_ge(S("ffn_out"), e * 4 + (2 * k + m + 1))
                        act.activation(hid_parts[k][:, 0, m, :], hid_whole[k][:, m, :], ACT.Copy).then_inc(S("ffn_relu"), 1)

            ffn(0, 0, True)
            ffn(1, 1, False)
            with act.Fori(1, E1 // 2) as g:
                for u in range(2):
                    ffn(g * 2 + u, u, False)

        @block.vector
        def _(dve):
            own = Steps(dve, S("dve_steps"))
            tt, tsc, stt = dve.tensor_tensor, dve.tensor_scalar, dve.scalar_tensor_tensor

            def norm_pieces(name, X, Y, eps, gain=None, shift=None):
                st, mv, ve, rs = stats[name]

                def group(g):
                    a, b = GROUPS[g]
                    for t in range(a, b):
                        own.step(dve.bn_stats(st[:, t, :], X[:, t, :]))
                    own.settle()
                    for t in range(a, b):
                        own.step(dve.bn_aggr(mv[:, t, :], st[:, t, :]))
                    own.settle()
                    tsc(ve[:, a:b], mv[:, a:b, 1], eps, None, ALU.add).then_inc(S("norm_var"), 1)

                def centre():
                    for t in range(NT):
                        own.step(stt(out=Y[:, t, :], in0=X[:, t, :], scalar=mv[:, t, 0:1], in1=gain,
                                     op0=ALU.subtract, op1=ALU.mult))

                def apply():
                    if gain is not None:
                        own.settle()
                    for g, (a, b) in enumerate(GROUPS):
                        dve.wait_ge(S("norm_rstd"), 2 * NORMS.index(name) + g + 1)
                        for t in range(a, b):
                            if gain is None:
                                last = tsc(Y[:, t, :], X[:, t, :], mv[:, t, 0:1], rs[:, t:t + 1], ALU.subtract, ALU.mult)
                            else:
                                last = stt(out=Y[:, t, :], in0=Y[:, t, :], scalar=rs[:, t:t + 1], in1=shift,
                                           op0=ALU.mult, op1=ALU.add)
                            if t < NT - 1:
                                own.step(last)
                    return last

                return [lambda: group(0), lambda: group(1)] + ([centre] if gain is not None else []) + [apply]

            def norm(name, X, Y, eps, gain=None, shift=None):
                for piece in norm_pieces(name, X, Y, eps, gain, shift):
                    last = piece()
                return last

            def evac_T(name, dst, bank):
                dve.wait_ge(S("rows_turned"), 10 * TURNS.index(name) + 10)
                dve.tensor_copy(dst[:, :, 4 * TP:N], ps[:, bank, 0:2 * TP].rearrange("p (c n) -> p c n", c=2))\
                    .then_inc(S("T_by_dve"), 1)

            dve.wait_ge(S("edges_loaded"), 32)
            own.link(dve.tensor_copy(idf[:, 0:2, :], idx[:]))
            own.link(tsc(idf[:, 3, :], idf[:, 0, :], float(HALF), None, ALU.is_ge))
            own.step(stt(out=idf[:, 2, :], in0=idf[:, 3, :], scalar=-float(HALF), in1=idf[:, 0, :],
                         op0=ALU.mult, op1=ALU.add))
            own.link(tsc(idf[:, 3, :], idf[:, 3, :], float(FIELD - 1), 1.0, ALU.mult, ALU.add))
            dve.wait_ge(S("ids_ready"), 1)

            def one_hot(j, u, free):
                if free is not None:
                    dve.wait_ge(S("onehot_used"), free)
                tsc(oh_src[:, u, 0:HALF], node_ids[:, 0:HALF], idf[:, 2, bass.ds(j, 1)], idf[:, 3, bass.ds(j, 1)],
                    ALU.is_equal, ALU.mult)
                tsc(oh_dst[:, u, 0:N], node_ids[:], idf[:, 1, bass.ds(j, 1)], None, ALU.is_equal)\
                    .then_inc(S("onehot_ready"), 1)

            def four(g):
                for u in range(4):
                    one_hot(g * 4 + u, u, g * 4 + (u - 3))

            def edges(k, done):
                a, b = CHUNKS[k]
                with dve.Fori(a // 4 + done, b // 4) as g:
                    four(g)
                if b % 4:
                    one_hot(b - 1, 0, b - 4)

            for u in range(4):
                one_hot(u, u, None)
            dve.wait_ge(S("x_loaded"), 16)
            norm("ln0", x_R, n_R, 1e-5).then_inc(S("rows_ready"), 1)

            def add_last_counts():
                dve.wait_ge(S("counts_added"), 2)
                dve.wait_ge(S("counts_out"), 3)
                own.link(stt(out=cnt_new, in0=cnt_upper, scalar=-float(FIELD), in1=cnt_new, op0=ALU.mult, op1=ALU.add))
                own.step(tt(count[:, :, 0:HALF], cnt_lo, cnt_new, ALU.add))
                own.link(tt(count[:, :, HALF:NP], cnt_hi, cnt_upper, ALU.add))

            edges(0, 1)
            four(CHUNKS[1][0] // 4)
            evac_T("n0", n_T, 7)
            dve.wait_ge(S("pads_ready"), 2)
            for j in range(4):
                m, h = divmod(j, 2)
                dve.wait_ge(S("mq_exp"), j + 1)
                own.link(tsc(eq[:, j % 2, :], eq[:, j % 2, :], 1.0, None, ALU.min))
                stt(out=q_T[:, m, h * HALF:(h + 1) * HALF], in0=ps[:, 5 + j % 3, 0:HALF], scalar=0.0,
                    in1=eq[:, j % 2, :], op0=ALU.max, op1=ALU.add).then_inc(S("mq_phi"), 1)
            for t in range(NT):
                dve.wait_ge(S("mkv_exp"), t + 1)
                own.link(tsc(ek[:, t % 2, :], ek[:, t % 2, :], 1.0, None, ALU.min))
                stt(out=vs[:, t, 0:D], in0=ps[0:TP, 5 + (4 + t) % 3, 0:D], scalar=0.0,
                    in1=ek[:, t % 2, :], op0=ALU.max, op1=ALU.add).then_inc(S("mkv_phi"), 1)
            edges(1, 1)
            dve.wait_ge(S("constants_ready"), 3)
            dve.wait_ge(S("mKV_done"), 2)
            for q in range(2):
                own.step(tt(kv_sb[:, q, 0:128].rearrange("p (h n) -> p h n", h=4),
                            ps[:, 5, q * 129:q * 129 + 128].rearrange("p (h n) -> p h n", h=4), head_mask[:], ALU.mult))
                last = tsc(kv_sb[:, q, 128:132], head_cols[:], ps[:, 5, q * 129 + 128:q * 129 + 129], None, ALU.mult)
                if q == 0:
                    own.step(last)
            last.then_inc(S("mKV_ready"), 1)
            for t in range(NT):
                b = 5 + (1 + t) % 3
                dve.wait_ge(S("mt_done"), t + 1)
                src = ps[0:TP, b, 0:264].rearrange("p (c n) -> p c n", c=2)
                own.link(tsc(zden[:, 0, t, :].rearrange("p (c n) -> p c n", c=2), src[:, :, 128:132], 1e-6, None, ALU.add))
                own.link(dve.reciprocal(zden[:, 1, t, :], zden[:, 0, t, :]))
                for q in range(2):
                    last = tt(mix_R[:, t, q * 128:(q + 1) * 128].rearrange("p (h n) -> p h n", h=4),
                              ps[0:TP, b, q * 132:q * 132 + 128].rearrange("p (h n) -> p h n", h=4),
                              zden[:, 1, t, 4 * q:4 * q + 4].unsqueeze(2).broadcast_to([TP, 4, 32]), ALU.mult)
                    if q == 0:
                        own.step(last)
                last.then_inc(S("mt_out"), 1)
            own.settle()
            four(CHUNKS[2][0] // 4)
            dve.wait_ge(S("mt_out"), NT)
            own.link(tt(mix_R[:], mix_R[:], n_R[:], ALU.add))
            dve.wait_ge(S("rows_loaded"), 16)
            norm1 = norm_pieces("ln1", mix_R, h_R, 1e-5, row["mix_ln1_g"], row["mix_ln1_b"])
            norm1[0]()
            norm1[1]()
            four(CHUNKS[2][0] // 4 + 1)
            norm1[2]()
            norm1[3]().then_inc(S("rows_ready"), 1)
            dve.wait_ge(S("rows_ready"), READY.index("m1") + 1)
            edges(2, 2)
            evac_T("m1", a_T, 7)
            own.link(tt(h_R[:], h_R[:], wide(row["mix_b2"]), ALU.add))
            add_last_counts()
            own.link(tsc(logc, count[:], 1.0, None, ALU.max))
            tsc(big2[0:TP, 0:NT * NP].rearrange("p (t n) -> p t n", t=NT), count[:], 0.5, MASK,
                ALU.is_lt, ALU.mult).then_inc(S("count_floor"), 1)
            for t in range(NT):
                dve.wait_ge(S("my_done"), t + 1)
                tt(mix_R[:, t, :], ps[0:TP, 5 + (22 + t) % 3, 0:D], h_R[:, t, :], ALU.add).then_inc(S("my_out"), 1)
            dve.wait_ge(S("count_floor"), 1)
            dve.wait_ge(S("count_ln"), 1)
            stt(out=logc, in0=logc, scalar=8.0, in1=big2[0:TP, 0:NT * NP].rearrange("p (t n) -> p t n", t=NT),
                op0=ALU.mult, op1=ALU.add).then_inc(S("logc_ready"), 1)
            dve.wait_ge(S("logc_ready"), 1)
            dve.wait_ge(S("cols_loaded"), 16)
            for k in range(2):
                tsc(bn_v[:, k * 2 * E1:(k + 1) * 2 * E1], c("v1" if k == 0 else "v2", 0, 2 * E1), 1e-3, None, ALU.add)\
                    .then_inc(S("bn_var"), 1)

            def bn_affine():
                dve.wait_ge(S("bn_rstd"), 1)
                for k in range(2):
                    z = slice(k * 2 * E1, (k + 1) * 2 * E1)
                    own.step(tt(bn_s[:, z], bn_r[:, z], c("g1" if k == 0 else "g2", 0, 2 * E1), ALU.mult))
                    own.link(tt(bn_t[:, z], c("b1" if k == 0 else "b2", 0, 2 * E1), c("m1" if k == 0 else "m2", 0, 2 * E1),
                                ALU.subtract))
                    own.link(tt(bn_t[:, z], bn_t[:, z], bn_s[:, z], ALU.mult))
                    last = tt(bn_b[:, z], bn_t[:, z], c("be1" if k == 0 else "be2", 0, 2 * E1), ALU.add)
                    if k == 0:
                        own.step(last)
                last.then_inc(S("bn_affine"), 1)

            norm2 = norm_pieces("ln2", mix_R, mix_R, 1e-5, row["mix_ln2_g"], row["mix_ln2_b"])
            fillers = {5: norm2[0], 6: norm2[1], 9: norm2[2], 12: lambda: own.step(norm2[3]()), 14: bn_affine,
                       16: lambda: (own.settle(), own.link(tt(x_R[:], x_R[:], mix_R[:], ALU.add)))}

            LAYER_STEPS = 2 * GH + 10

            def project(i):
                for m in range(NC2):
                    for h, z, other in ((2 * m, slice(0, 64), slice(64, 128)), (2 * m + 1, slice(64, 128), slice(0, 64))):
                        dve.wait_ge(S("g_q"), i * 4 + h + 1)
                        stt(out=halves(q_parts[h][other]), in0=pair(2 * m)[z], scalar=gcols[z, bass.ds(i * 8 + m, 1)],
                            in1=halves(q_parts[h][z]).bitcast(F32), op0=ALU.add, op1=ALU.subtract).then_inc(S("g_q_lo"), 1)
                for m in range(NC2):
                    for h, z in ((2 * m, slice(0, 64)), (2 * m + 1, slice(64, 128))):
                        dve.wait_ge(S("g_k"), i * 4 + h + 1)
                        stt(out=halves(k_lo[m][z]), in0=pair(4 + 2 * m)[z], scalar=gcols[z, bass.ds(i * 8 + (2 + m), 1)],
                            in1=halves(k_parts[h][z]).bitcast(F32), op0=ALU.add, op1=ALU.subtract).then_inc(S("g_k_lo"), 1)
                for t in range(3):
                    rows_in(i, t)

            def rows_in(i, t):
                dve.wait_ge(S("g_rows_done"), i * NT + t + 1)
                tt(vs[:, t, :], ps[0:TP, ROWS_BANK[t], :], gbias[:], ALU.add).then_inc(S("g_rows_read"), 1)

            def attention(i, last_layer):
                lay = Steps(dve, S("g_dve_steps"), i * LAYER_STEPS)

                def head_out(h):
                    z = slice(h * NT, h * NT + NT)
                    dve.wait_ge(S("g_exp"), i * STEPS + h * NT + NT)
                    lay.link(dve.reciprocal(grec[:, z], gden[:, z]))
                    lay.link(stt(out=grec[:, z], in0=gmax[:, z], scalar=HAS_EDGE, in1=grec[:, z],
                                 op0=ALU.is_gt, op1=ALU.mult))
                    dve.wait_ge(S("g_pv"), i * STEPS + h * NT + NT)
                    tt(att[:], ps[0:TP, 6 + h % 2, 0:NT * 64].rearrange("p (t n) -> p t n", t=NT),
                       grec[:, z].unsqueeze(2).broadcast_to([TP, NT, 64]), ALU.mult).then_inc(S("g_head"), 1)
                    dve.wait_ge(S("g_head"), i * GH + h + 1)
                    tt(h_R[:, :, h * 64:(h + 1) * 64], att[:], vs[:, :, D + h * 64:D + (h + 1) * 64], ALU.add)\
                        .then_inc(S("g_out"), 1)
                    dve.wait_ge(S("g_out"), i * GH + h + 1)

                for n in range(STEPS):
                    dve.wait_ge(S("g_scores"), i * STEPS + n + 1)
                    if n >= 3:
                        dve.wait_ge(S("g_turned"), i * STEPS + n - 2)
                    dve.nop(nofuse=True)
                    dve.tensor_tensor_reduce(out=halves(probs[n % 3]), in0=pair(2 * (n % 2), TP),
                                             in1=halves(logc[:, n % NT, :]), scale=0.125, scalar=-3.0e38,
                                             op0=ALU.add, op1=ALU.max, accum_out=gmax[:, n:n + 1])\
                        .then_inc(S("g_max"), 1)
                    if n < 2:
                        rows_in(i, 3 + n)
                    if n == 1:
                        dve.wait_ge(S("g_rows_read"), i * NT + NT)
                    if n % NT == 3 and n > NT:
                        head_out(n // NT - 1)
                    if last_layer and n in fillers:
                        fillers[n]()
                if last_layer:
                    z = slice(0, (GH - 1) * 64)
                    own.step(tt(x_R[:, :, z], x_R[:, :, z], h_R[:, :, z], ALU.add))
                    head_out(GH - 1)
                    return

                def sums(m):
                    dve.wait_ge(S("gh_turned"), i * 10 + (5 * m + 5))
                    dve.tensor_copy(a_T[:, m, 4 * TP:N], ps[:, 2 * m + 1, 0:TP]).then_inc(S("gh_T2"), 1)
                    dve.wait_ge(S("gh_T"), i * 2 + m + 1)
                    dve.wait_ge(S("gh_T2"), i * 2 + m + 1)
                    dve.nop(nofuse=True)
                    lay.step(dve.bn_stats(bst[:, m, 0, :], a_T[:, m, 0:HALF]))
                    lay.step(dve.bn_stats(bst[:, m, 1, :], a_T[:, m, HALF:N]))

                def moments(m):
                    lay.settle()
                    dve.nop(nofuse=True)
                    lay.link(dve.bn_aggr(bmv[:, m, :], bst[:, m, :, :]))
                    tsc(bve[:, m:m + 1], bmv[:, m, 1:2], 1e-5, None, ALU.add).then_inc(S("g_var"), 1)

                def affine(m):
                    dve.wait_ge(S("g_rstd"), i * 2 + m + 1)
                    z = slice(m, m + 1)
                    lay.link(tt(bsc[:, 0, z], brs[:, z], gcols[:, bass.ds(i * 8 + (4 + m), 1)], ALU.mult))
                    lay.link(tt(bsc[:, 1, z], bmv[:, m, 0:1], bsc[:, 0, z], ALU.mult))
                    tt(bsc[:, 2, z], gcols[:, bass.ds(i * 8 + (6 + m), 1)], bsc[:, 1, z], ALU.subtract)\
                        .then_inc(S("g_affine"), 1)

                sums(0)
                moments(0)
                head_out(GH - 1)
                affine(0)
                sums(1)
                moments(1)
                affine(1)
                project(i + 1)
                return lay.n

            dve.wait_ge(S("gcols_loaded"), 16)
            project(0)

            with dve.Fori(0, GL - 1) as i:
                LS = attention(i, False)
            assert LS == LAYER_STEPS, LS
            attention(GL - 1, True)

            z = slice((GH - 1) * 64, D)
            own.link(tt(x_R[:, :, z], x_R[:, :, z], h_R[:, :, z], ALU.add))
            norm("lnm", x_R, n_R, 1e-5).then_inc(S("rows_ready"), 1)
            evac_T("xm", c_T, 2)
            dve.wait_ge(S("logits_done"), 1)
            own.link(tt(lg[:], ps[0:TP, 7, 0:NT * 16].rearrange("p (t n) -> p t n", t=NT),
                        row["gates"][:, 0:16].unsqueeze(1).broadcast_to([TP, NT, 16]), ALU.add))
            for t in range(NT):
                own.step(dve.max(top[:, t, :], lg[:, t, :]))
            own.settle()
            for t in range(NT):
                own.step(dve.max_index(topi[:, t, :], top[:, t, :], lg[:, t, :]))
            tt(tw[:, 0, :], top[:, :, 1], top[:, :, 0], ALU.subtract).then_inc(S("top_diff"), 1)
            own.settle()
            own.link(dve.tensor_copy(topf[:], topi[:, :, 0:2]))
            dve.wait_ge(S("constants_ready"), 4)
            for k in range(2):
                own.step(tt(pick[:, k], expert_ids[:].unsqueeze(1).broadcast_to([TP, NT, 16]),
                            topf[:, :, k].unsqueeze(2).broadcast_to([TP, NT, 16]), ALU.is_equal))
            own.settle()
            tt(picked[:], pick[:, 0], pick[:, 1], ALU.add).then_inc(S("picked_ready"), 1)
            dve.wait_ge(S("top_exp"), 1)
            own.link(tsc(tw[:, 2, :], tw[:, 1, :], 1.0, None, ALU.add))
            own.link(dve.reciprocal(tw[:, 2, :], tw[:, 2, :]))
            own.link(tt(tw[:, 3, :], tw[:, 1, :], tw[:, 2, :], ALU.mult))
            for k in range(2):
                own.step(tt(place[:, k], pick[:, k], tw[:, 2 + k, :].unsqueeze(2).broadcast_to([TP, NT, 16]), ALU.mult))
            own.settle()
            tt(gate[:], place[:, 0], place[:, 1], ALU.add).then_inc(S("gate_ready"), 1)
            dve.wait_ge(S("gate_ready"), 1)
            dve.wait_ge(S("ranked"), 1)
            own.link(tsc(tiles_i[:], ps[0:TP, 6, 128:144], -1.0, 0.0, ALU.add, ALU.max))
            own.link(tsc(tiles_i[:], tiles_i[:], 7, None, ALU.logical_shift_right))
            own.link(dve.tensor_copy(tiles[:, 0, 16:32], tiles_i[:]))
            own.link(dve.tensor_copy(tiles[:, 2, 16:32], tiles[:, 0, 16:32]))
            for k, shift in enumerate((1, 2, 4, 8)):
                src, dst = tiles[:, k % 2, :], tiles[:, (k + 1) % 2, :]
                own.link(tt(dst[:, 16:32], src[:, 16:32], src[:, 16 - shift:32 - shift], ALU.add))
            upto = tiles[:, 0, 16:32]
            own.link(tt(tiles[:, 2, 16:32], upto, tiles[:, 2, 16:32], ALU.subtract))
            own.step(dve.tensor_copy(tile_expert[:, 0:E0], tile_ids[0:1, 0:E0]))
            own.link(tt(own_tile, tile_ids[0:1, 0:MT - E0].unsqueeze(2).broadcast_to([1, MT - E0, 16]),
                        upto[0:1].unsqueeze(1).broadcast_to([1, MT - E0, 16]), ALU.is_ge))
            own.link(dve.tensor_reduce(tile_e[:], own_tile, AX, ALU.add))
            tsc(tile_expert[:, E0:MT], tile_e[:], float(E0 - 1), None, ALU.min).then_inc(S("tile_expert_ready"), 1)
            rank = ps[0:TP, 6, 0:NT * 16].rearrange("p (t n) -> p t n", t=NT)
            own.step(stt(out=tiles[:, 1, 16:32], in0=tiles[:, 2, 16:32], scalar=float(E0 - 1), in1=expert_ids[:],
                         op0=ALU.add, op1=ALU.subtract))
            own.step(stt(out=place[:, 0], in0=expert_ids[:].unsqueeze(1).broadcast_to([TP, NT, 16]),
                         scalar=float(SLOT), in1=rank, op0=ALU.mult, op1=ALU.add))
            own.link(tsc(place[:, 1], rank, float(SLOT), float(SLOT), ALU.is_ge, ALU.mult))
            own.link(tt(place[:, 1], place[:, 1], tiles[:, 1, 16:32].unsqueeze(1).broadcast_to([TP, NT, 16]), ALU.mult))
            own.link(tt(place[:, 0], place[:, 0], place[:, 1], ALU.add))
            own.link(tt(place[:, 1], place[:, 0], pick[:, 1], ALU.mult))
            own.link(tt(place[:, 0], place[:, 0], pick[:, 0], ALU.mult))
            own.link(dve.tensor_reduce(slot[:, 0, :].rearrange("p (k t) -> p k t", k=2), place, AX, ALU.add))
            own.link(dve.tensor_copy(slot_i[:, 0, :], slot[:, 0, :]))
            own.step(tsc(slot_i[:, 1, :], slot_i[:, 0, :], 7, None, ALU.logical_shift_right))
            own.link(tsc(slot_i[:, 2, :], slot_i[:, 0, :], SLOT - 1, None, ALU.bitwise_and))
            own.link(dve.tensor_copy(slot[:, 1:3, :], slot_i[:, 1:3, :]))
            for k in range(2 * NT):
                tsc(tile_hot[:, k, :], tile_ids[:], slot[:, 1, k:k + 1], choice_ids[:, k:k + 1], ALU.is_equal, ALU.mult)
                tsc(row_hot[:, k, :], row_ids[:], slot[:, 2, k:k + 1], None, ALU.is_equal).then_inc(S("hot_ready"), 1)
            dve.wait_ge(S("hot_ready"), 2 * NT)
            dve.wait_ge(S("inverted"), 1)
            src = ps[:, 7, 0:MT]
            own.step(tsc(slot_m[:, 0, :], src, float(N) + 0.5, -float(N), ALU.is_gt, ALU.mult))
            own.link(tsc(slot_m[:, 1, :], src, 0.5, None, ALU.is_lt))
            own.step(tt(slot_m[:, 0, :], src, slot_m[:, 0, :], ALU.add))
            own.link(tt(slot_m[:, 1, :], slot_m[:, 1, :], spare_ids[:], ALU.mult))
            own.step(tsc(slot_m[:, 0, :], slot_m[:, 0, :], -1.0, 0.0, ALU.add, ALU.max))
            own.settle()
            dve.tensor_copy(from_row[:], slot_m[:, 0, :]).then_inc(S("rows_placed"), 1)
            tt(to_row[:], src, slot_m[:, 1, :], ALU.add).then_inc(S("rows_placed"), 1)
            dve.wait_ge(S("deg_done"), 2)
            tsc(halves(inv_deg[:]), pair(4), 1.0, None, ALU.max).then_inc(S("deg_read"), 1)

            def bias_rows(n, acc):
                for t in range(NT):
                    dve.wait_ge(S("bias_done"), n * NT + min(t // 2 * 2 + 2, NT))
                    tt(acc[:, t, :], ps[0:TP, 7 - t // 2, (t % 2) * D:(t % 2 + 1) * D],
                       acc[:, t, :], ALU.add).then_inc(S("bias_in"), 1)
                dve.wait_ge(S("bias_in"), n * NT + NT)

            def moe_tile_T(j, u, first):
                dve.wait_ge(S("moe_turned"), j * 2 + 2)
                if not first:
                    dve.wait_ge(S("moe_h_done"), j - 1)
                dve.tensor_copy(tile_xT[u], ps[:, u, 0:D].rearrange("p (c n) -> p c n", c=2)).then_inc(S("moe_T"), 1)

            def moe_tile_y(j, u, k):
                dve.wait_ge(S("moe_y_done"), j + 1)
                if k is not None:
                    dve.wait_ge(S(f"moe_scattered{u}"), k * 16)
                dve.tensor_copy(tile_y[u], ps[:, 4 + u, 0:D]).then_inc(S("moe_y_out"), 1)

            moe_tile_T(0, 0, True)
            bias_rows(0, n_R)
            own.step(tt(x_R[:], x_R[:], wide(row["moe_beta"]), ALU.add))
            moe_tile_T(1, 1, True)
            moe_tile_T(2, 0, False)
            moe_tile_y(0, 0, None)
            moe_tile_T(3, 1, False)
            moe_tile_y(1, 1, None)
            with dve.Fori(2, MT // 2) as g:
                for u in range(2):
                    moe_tile_T(g * 2 + u, u, False)
                    moe_tile_y(g * 2 + (u - 2), u, g - 1)
            moe_tile_T(MT - 1, 0, False)
            moe_tile_y(MT - 3, 0, (MT - 3) // 2)
            moe_tile_y(MT - 2, 1, (MT - 3) // 2)
            moe_tile_y(MT - 1, 0, (MT - 1) // 2)
            dve.wait_ge(S("deg_read"), 1)
            own.step(dve.reciprocal(inv_deg[:], inv_deg[:]))
            for k in range(2):
                dve.wait_ge(S(f"choice{k}_loaded"), 16)
                for t in range(NT):
                    j = k * NT + t
                    own.step(stt(out=n_R[:, t, :], in0=vs[:, j // 2, (j % 2) * D:(j % 2 + 1) * D],
                                 scalar=tw[:, 2 + k, t:t + 1], in1=n_R[:, t, :], op0=ALU.mult, op1=ALU.add))
                own.settle()
            normy = norm_pieces("lny", n_R, y_R, 1e-5, row["moe_gamma"], row["moe_beta"])
            normx = norm_pieces("lnx", x_R, n_R, 1e-5)
            rs = stats["lny"][3]
            for piece in normy[0:3]:
                piece()
            own.settle()
            for g, (a, b) in enumerate(GROUPS):
                dve.wait_ge(S("norm_rstd"), 2 * NORMS.index("lny") + g + 1)
                for t in range(a, b):
                    own.step(stt(out=x_R[:, t, :], in0=y_R[:, t, :], scalar=rs[:, t:t + 1], in1=x_R[:, t, :],
                                 op0=ALU.mult, op1=ALU.add))
                own.settle()
                normx[g]()
            normx[2]().then_inc(S("rows_ready"), 1)
            evac_T("x2", n_T, 2)

            def aggregate(l, src_T, m):
                dve.wait_ge(S("agg_done"), 2 * l + m + 1)
                own.link(tt(halves(a_T[:, m, :]), pair(2 * m), halves(inv_deg[:]), ALU.mult))
                tt(a_T[:, m, :], a_T[:, m, :], src_T[:, m, :], ALU.add).then_inc(S("agg_out"), 1)

            def graph_row(l, t):
                dve.wait_ge(S("g1_h_done"), l * NT + t + 1)
                tt(y_R[:, t, :], ps[0:TP, t % 4, 0:D], row[f"g1_b{l}"], ALU.add).then_inc(S("g1_h"), 1)

            for t in range(NT):
                dve.wait_ge(S("m1_kv_done"), t + 1)
                tt(vs[:, t, :], ps[0:TP, t, :],
                   rows[:, ROWS.index("m1_bk"):ROWS.index("m1_bv") + 1, :].rearrange("p a n -> p (a n)"), ALU.add)\
                    .then_inc(S("m1_kv"), 1)
            dve.wait_ge(S("m1_at_done"), 2)
            for k in range(4):
                p, q = 64 * (k % 2), k // 2
                own.link(dve.reduce_max(at_m[p:p + 64, k, 0:1], ps[p:p + 64, 5, q * 128 + p:q * 128 + p + 64], AX))
            for k in range(4):
                p = 64 * (k % 2)
                tsc(at_m[p:p + 64, k, 1:2], at_m[p:p + 64, k, 0:1], -0.125, None, ALU.mult).then_inc(S("m1_neg"), 1)
            for k in range(4):
                p, q = 64 * (k % 2), k // 2
                dve.wait_ge(S("m1_exp"), k + 1)
                own.link(dve.reciprocal(at_m[p:p + 64, k, 2:3], at_m[p:p + 64, k, 2:3]))
                tsc(at_sb[p:p + 64, q, p:p + 64], at_sb[p:p + 64, q, p:p + 64], at_m[p:p + 64, k, 2:3], None, ALU.mult)\
                    .then_inc(S("m1_attn"), 1)
            dve.wait_ge(S("T_by_act"), TURNS.index("x2") + 1)
            dve.wait_ge(S("T_by_dve"), TURNS.index("x2") + 1)
            aggregate(0, n_T, 0)
            dve.wait_ge(S("at_turned"), 2)
            dve.tensor_copy(at_T[:], ps[:, 6, 0:256].rearrange("p (c n) -> p c n", c=2)).then_inc(S("at_T_ready"), 1)
            aggregate(0, n_T, 1)
            for t in range(NT):
                dve.wait_ge(S("m1_xf_done"), t + 1)
                tt(mix_R[:, t, :], ps[0:TP, 4 + t % 4, 0:D], n_R[:, t, :], ALU.add).then_inc(S("m1_xf"), 1)
            dve.wait_ge(S("m1_xf"), NT)
            first, second, centre, apply = norm_pieces("lnh", mix_R, h_R, 1e-5, row["m1_norm_g"], row["m1_norm_b"])
            first()
            second()
            for t in range(NT - 1):
                graph_row(0, t)
            centre()
            graph_row(0, NT - 1)
            apply().then_inc(S("rows_ready"), 1)
            dve.wait_ge(S("g1_h"), NT)
            first, second, centre, apply = norm_pieces("gn0", y_R, y_R, 1e-5, row["g1_g0"], row["g1_beta0"])
            first()
            evac_T("y1", b_T, 6)
            second()
            centre()
            apply().then_inc(S("gn_normed"), 1)
            evac_T("g1", k_T, 2)
            dve.wait_ge(S("T_by_act"), TURNS.index("g1") + 1)
            dve.wait_ge(S("T_by_dve"), TURNS.index("g1") + 1)
            aggregate(1, k_T, 0)
            own.link(tt(x_R[:], x_R[:], mix_R[:], ALU.add))
            aggregate(1, k_T, 1)
            own.settle()
            for t in range(NT):
                graph_row(1, t)
            dve.wait_ge(S("g1_h"), 2 * NT)
            norm("gn1", y_R, y_R, 1e-5, row["g1_g1"], row["g1_beta1"]).then_inc(S("gn_normed"), 1)
            own.link(tt(x_R[:], x_R[:], wide(row["m1_bfc2"]), ALU.add))

            def weight_lo(e, u, k):
                dve.wait_ge(S("w_hi"), e * 3 + k + 1)
                z = slice(k * 2 * D, (k + 1) * 2 * D)
                tt(w_parts[u][:, 1, z], w3_ffn[u][k], w_parts[u][:, 0, z].bitcast(F32), ALU.subtract)\
                    .then_inc(S("w_lo"), 1)

            dve.wait_ge(S("g1_x"), 2)
            own.link(tt(x_R[:], x_R[:], y_R[:], ALU.add))
            for k in range(3):
                weight_lo(0, 0, k)
            normf = norm_pieces("lnf", x_R, n_R, 1e-5)
            for t in range(NT):
                dve.wait_ge(S("fc2_done"), t + 1)
                tt(x_R[:, t, :], ps[0:TP, 4 + t if t < 4 else 3, 0:D], x_R[:, t, :], ALU.add).then_inc(S("fc2_out"), 1)
                if t + 1 == GROUPS[0][1]:
                    dve.wait_ge(S("fc2_out"), t + 1)
                    normf[0]()
            dve.wait_ge(S("fc2_out"), NT)
            normf[1]()
            normf[2]().then_inc(S("rows_ready"), 1)
            evac_T("x3", c_T, 2)

            dve.wait_ge(S("x_hi"), 1)
            tt(x_parts[:, 1], c_T[:], x_parts[:, 0].bitcast(F32), ALU.subtract).then_inc(S("x_lo"), 1)
            dve.wait_ge(S("logits_done"), 2)
            own.link(tt(gate2[:, :, 0:E1], ps[0:TP, 7, 0:NT * E1].rearrange("p (t n) -> p t n", t=NT),
                        row["gates"][:, 16:16 + E1].unsqueeze(1).broadcast_to([TP, NT, E1]), ALU.add))
            own.link(dve.tensor_reduce(tw[:, 0, :], gate2[:, :, 0:E1], AX, ALU.max))
            tt(gate2[:, :, 0:E1], gate2[:, :, 0:E1], tw[:, 0, :].unsqueeze(2).broadcast_to([TP, NT, E1]), ALU.subtract)\
                .then_inc(S("gate2_shift"), 1)
            dve.wait_ge(S("gate2_exp"), 1)
            own.link(dve.tensor_reduce(tw[:, 1, :], gate2[:, :, 0:E1], AX, ALU.add))
            own.link(dve.reciprocal(tw[:, 1, :], tw[:, 1, :]))
            tt(gate2[:, :, 0:E1], gate2[:, :, 0:E1], tw[:, 1, :].unsqueeze(2).broadcast_to([TP, NT, E1]), ALU.mult)\
                .then_inc(S("gate2_ready"), 1)

            def hidden_lo(e, k):
                for m in range(NC2):
                    dve.wait_ge(S("ffn_relu"), e * 4 + (2 * k + m + 1))
                    tt(hid_parts[k][:, 1, m, :], hid_whole[k][:, m, :], hid_parts[k][:, 0, m, :].bitcast(F32),
                       ALU.subtract).then_inc(S("ffn_lo"), 1)

            gate2_flat = gate2[:].rearrange("p t n -> p (t n)")

            def add_rows(e, first=False):
                for t in range(NT):
                    if t % 2 == 0:
                        dve.wait_ge(S("ffn_y_done"), e * 3 + (t // 2 + 1))
                    if not first:
                        dve.wait_ge(S("ffn_acc"), e * NT + (t - NT + 1))
                    stt(out=x_R[:, t, :], in0=ps[0:TP, 4 + t // 2, (t % 2) * D:(t % 2 + 1) * D],
                        scalar=gate2_flat[:, bass.ds(e + 16 * t, 1)], in1=x_R[:, t, :], op0=ALU.mult, op1=ALU.add)\
                        .then_inc(S("ffn_acc"), 1)

            def expert(e, u, first=False, last=False):
                hidden_lo(e, 0)
                if not last:
                    weight_lo(e + 1, 1 - u, 0)
                add_rows(e - 1, first)
                if not last:
                    weight_lo(e + 1, 1 - u, 1)
                hidden_lo(e, 1)
                if not last:
                    weight_lo(e + 1, 1 - u, 2)

            dve.wait_ge(S("gate_turned"), 2 * NT)
            dve.tensor_copy(gate_T[0:E1, :].rearrange("p (t n) -> p t n", t=NT), quads(4, E1)).then_inc(S("gate2_T_ready"), 1)
            hidden_lo(0, 0)
            bias_rows(1, x_R)
            for k in range(2):
                weight_lo(1, 1, k)
            hidden_lo(0, 1)
            weight_lo(1, 1, 2)
            expert(1, 1, first=True)
            with dve.Fori(1, E1 // 2 - 1) as g:
                for u in range(2):
                    expert(g * 2 + u, u)
            expert(E1 - 2, 0)
            expert(E1 - 1, 1, last=True)
            add_rows(E1 - 1)

        @block.tensor
        def _(pe):
            mm = pe.matmul

            def turn(name, src, bank):
                pe.wait_ge(S("rows_ready"), READY.index(name) + 1)
                for t in range(NT):
                    for q in range(NC2):
                        dst = ps[:, bank + q, t * TP:(t + 1) * TP] if t < 4 else ps[:, bank + 2, q * TP:(q + 1) * TP]
                        pe.transpose(dst, src[:, t, q * 128:(q + 1) * 128], ident[0:TP, 0:TP])\
                            .then_inc(S("rows_turned"), 1)

            def turned(name):
                pe.wait_ge(S("T_by_act"), TURNS.index(name) + 1)
                pe.wait_ge(S("T_by_dve"), TURNS.index(name) + 1)

            def to_T(b, w, src_T, m0, K=NC2):
                for h in range(2):
                    for k in range(K):
                        last = mm(ps[:, b + h, 0:HALF], w[:, k, m0:m0 + 128], src_T[:, k, h * HALF:(h + 1) * HALF],
                                  start=(k == 0), stop=(k == K - 1))
                return last

            def to_R(dst, src, t, w, K=NC2):
                for k in range(K):
                    last = mm(dst, src(k)[:, t * TP:(t + 1) * TP], w(k), start=(k == 0), stop=(k == K - 1))
                return last

            def count_tile(u, g, first, last):
                pe.wait_ge(S("onehot_ready"), g * 4 + (u + 1))
                for t in range(NT):
                    ins = mm(ps[0:TP, t, 0:HALF], oh_dst[:, u, t * TP:(t + 1) * TP], oh_src[:, u, 0:HALF],
                             start=first, stop=last, skip_group_check=not (first or last))
                ins.then_inc(S("onehot_used"), 1)
                return ins

            def edges(k):
                a, b = CHUNKS[k]
                if k:
                    pe.wait_ge(S("counts_out"), k)
                for u in range(4):
                    count_tile(u, a // 4, u == 0, False)
                if k == 0:
                    turn("n0", n_R, 5)
                rest = 1 if b % 4 else 0
                with pe.Fori(a // 4 + 1, b // 4 - (1 - rest)) as g:
                    for u in range(4):
                        count_tile(u, g, False, False)
                if rest:
                    count_tile(0, b // 4, False, True)
                else:
                    for u in range(4):
                        count_tile(u, b // 4 - 1, False, u == 3)

            pe.wait_ge(S("ident_ready"), 1)
            edges(0)
            pe.wait_ge(S("w_mix_loaded"), 16)
            turned("n0")
            pe.wait_ge(S("pads_ready"), 2)
            for j in range(4):
                m, h = divmod(j, 2)
                if j == 3:
                    pe.wait_ge(S("mq_phi"), 1)
                for k in range(NC2):
                    last = mm(ps[:, 5 + j % 3, 0:HALF], w_mix[:, k, m * 128:(m + 1) * 128],
                              n_T[:, k, h * HALF:(h + 1) * HALF], start=(k == 0), stop=(k == 1))
                last.then_inc(S("mq_done"), 1)
            for t in range(NT):
                pe.wait_ge(S("mq_phi"), min(t + 2, 4))
                if t >= 3:
                    pe.wait_ge(S("mkv_phi"), t - 2)
                to_R(ps[0:TP, 5 + (4 + t) % 3, :], lambda k: n_T[:, k, :], t, lambda k: w_mix[:, k, D:3 * D])\
                    .then_inc(S("mkv_done"), 1)
            edges(1)
            pe.wait_ge(S("mkv_phi"), NT)
            pe.wait_ge(S("constants_ready"), 1)
            for q in range(2):
                for t in range(NT):
                    last = mm(ps[:, 5, q * 129:(q + 1) * 129], vs[:, t, q * 128:(q + 1) * 128], vones[:, t, q, :],
                              start=(t == 0), stop=(t == NT - 1))
                last.then_inc(S("mKV_done"), 1)
            pe.wait_ge(S("mKV_ready"), 1)
            for t in range(NT):
                if t >= 3:
                    pe.wait_ge(S("mt_out"), t - 2)
                for q in range(2):
                    last = mm(ps[0:TP, 5 + (1 + t) % 3, q * 132:(q + 1) * 132], q_T[:, q, t * TP:(t + 1) * TP],
                              kv_sb[:, q, :], start=True, stop=True)
                last.then_inc(S("mt_done"), 1)
            edges(2)
            turn("m1", h_R, 5)
            turned("m1")
            for j in range(4):
                m, h = divmod(j, 2)
                if j == 3:
                    pe.wait_ge(S("mh_gelu"), 1)
                for k in range(NC2):
                    last = mm(ps[:, 5 + (18 + j) % 3, 0:HALF], w_mix[:, k, 3 * D + m * 128:3 * D + (m + 1) * 128],
                              a_T[:, k, h * HALF:(h + 1) * HALF], start=(k == 0), stop=(k == 1))
                last.then_inc(S("mh_done"), 1)
            pe.wait_ge(S("mh_gelu"), 4)
            for t in range(NT):
                if t >= 3:
                    pe.wait_ge(S("my_out"), t - 2)
                to_R(ps[0:TP, 5 + (22 + t) % 3, 0:D], lambda k: b_T[:, k, :], t, lambda k: w_mix[:, k, 4 * D:5 * D])\
                    .then_inc(S("my_done"), 1)
            pe.wait_ge(S("counts_out"), 3)

            def project(i, first):
                pe.wait_ge(S("gw_loaded"), i * 32 + 32)
                for k in range(NC2):
                    if not first:
                        pe.wait_ge(S("g_next"), i * 2 + (k - 1))
                    for m in range(NC2):
                        if m and not first and k == 0:
                            pe.wait_ge(S("gh_T"), i * 2)
                            pe.wait_ge(S("gh_T2"), i * 2)
                        for h in range(2):
                            last = mm(ps[:, 2 * m + h, 0:HALF], gw[:, 0, k, m * 128:(m + 1) * 128],
                                      n_T[:, k, h * HALF:(h + 1) * HALF], start=(k == 0), stop=(k == 1))
                        if k:
                            last.then_inc(S("g_q_done"), 1)
                if first:
                    pe.wait_ge(S("my_out"), NT)
                for m in range(NC2):
                    to_T(4 + 2 * m, gw[:, 1], n_T, m * 128).then_inc(S("g_k_done"), 1)
                pe.wait_ge(S("g_q_lo"), i * 4 + 4)
                for t in range(3):
                    if t == 2:
                        pe.wait_ge(S("g_k_lo"), i * 4 + 2)
                    rows_out(i, t)

            def rows_out(i, t):
                for k in range(NC2):
                    last = mm(ps[0:TP, ROWS_BANK[t], :], n_T[:, k, t * TP:(t + 1) * TP], gw[:, 2:4, k, :],
                              start=(k == 0), stop=(k == 1))
                last.then_inc(S("g_rows_done"), 1)

            def attention(i, last_layer):
                def scores(n):
                    h, t = divmod(n, NT)
                    if t == 0:
                        pe.wait_ge(S("g_k_twice"), i * 4 + h + 1)
                        pe.wait_ge(S("g_k_lo"), i * 4 + h + 1)
                    if n == 1:
                        pe.wait_ge(S("g_rows_read"), i * NT + 2)
                    if n >= 2:
                        pe.wait_ge(S("g_max"), i * STEPS + n - 1)
                    z = slice(64 * (h % 2), 64 * (h % 2) + 64)
                    rows_t = slice(t * TP, (t + 1) * TP)
                    for b in range(2):
                        cols_b = slice(b * HALF, (b + 1) * HALF)
                        dst = ps[0:TP, 2 * (n % 2) + b, 0:HALF]
                        mm(dst, q_parts[h][:, rows_t], k_parts[h][:, cols_b], start=True, stop=False)
                        last = mm(dst, q_parts[h][z, rows_t], k_lo[h // 2][z, cols_b], start=False, stop=True)
                    last.then_inc(S("g_scores"), 1)

                def turn_probs(n):
                    pe.wait_ge(S("g_exp"), i * STEPS + n + 1)
                    if n:
                        pe.wait_ge(S("g_probs_T"), i * STEPS + n)
                    else:
                        pe.wait_ge(S("g_rows_read"), i * NT + 4)
                    for s in range(NT):
                        last = pe.transpose(quads(4)[:, s, :], probs[n % 3][:, s * TP:(s + 1) * TP], ident[0:TP, 0:TP])
                    last.then_inc(S("g_turned"), 1)

                def weigh(n):
                    h, t = divmod(n, NT)
                    if t == 0 and h >= 2:
                        pe.wait_ge(S("g_head"), i * GH + h - 1)
                    if n == 0:
                        pe.wait_ge(S("g_rows_read"), i * NT + NT)
                    pe.wait_ge(S("g_probs_T"), i * STEPS + n + 1)
                    for s in range(NT):
                        last = mm(ps[0:TP, 6 + h % 2, t * 64:(t + 1) * 64], probs_T[n % 2][:, s, :],
                                  vs[:, s, h * 64:(h + 1) * 64], start=(s == 0), stop=(s == NT - 1))
                    last.then_inc(S("g_pv"), 1)

                scores(0)
                rows_out(i, 3)
                scores(1)
                pe.wait_ge(S("g_k_lo"), i * 4 + 4)
                rows_out(i, 4)
                def turn_heads(m):
                    pe.wait_ge(S("g_out"), i * GH + (2 * m + 2))
                    for t in range(NT):
                        dst = ps[:, 2 * m, t * TP:(t + 1) * TP] if t < 4 else ps[:, 2 * m + 1, 0:TP]
                        pe.transpose(dst, h_R[:, t, m * 128:(m + 1) * 128], ident[0:TP, 0:TP])\
                            .then_inc(S("gh_turned"), 1)

                for n in range(STEPS):
                    turn_probs(n)
                    if n + 2 < STEPS:
                        scores(n + 2)
                    if n:
                        weigh(n - 1)
                if not last_layer:
                    pe.wait_ge(S("g_max"), i * STEPS + STEPS - 1)
                    turn_heads(0)
                weigh(STEPS - 1)
                if last_layer:
                    return
                turn_heads(1)
                project(i + 1, False)

            project(0, True)
            with pe.Fori(0, GL - 1) as i:
                attention(i, False)
            attention(GL - 1, True)

            pe.wait_ge(S("g_probs_T"), GL * STEPS)
            pe.wait_ge(S("constants_ready"), 5)

            def degrees(h):
                for s in range(NT):
                    last = mm(ps[:, 4 + h, 0:HALF], ones[:], count[:, s, h * HALF:(h + 1) * HALF],
                              start=(s == 0), stop=(s == NT - 1))
                last.then_inc(S("deg_done"), 1)

            turn("xm", n_R, 0)
            turned("xm")
            pe.wait_ge(S("gates_loaded"), 48)
            for t in range(NT):
                last = to_R(ps[0:TP, 7, t * 16:(t + 1) * 16], lambda k: c_T[:, k, :], t, lambda k: gate_w[:, k, 0:16])
            last.then_inc(S("logits_done"), 1)

            def bias_rows(biases, n):
                for t in range(NT):
                    mm(ps[0:TP, 7 - t // 2, (t % 2) * D:(t % 2 + 1) * D],
                       gate_T[0:n, t * TP:(t + 1) * TP], biases[:], start=True, stop=True).then_inc(S("bias_done"), 1)

            pe.wait_ge(S("picked_ready"), 1)
            for t in range(NT):
                for s in range(t + 1):
                    mm(ps[0:TP, 6, t * 16:(t + 1) * 16], (before if s == t else ones_b)[:, 0:TP], picked[:, s, :],
                       start=(s == 0), stop=(s == t))
            for s in range(NT):
                last = mm(ps[0:TP, 6, 128:144], ones_b[:, 0:TP], picked[:, s, :], start=(s == 0), stop=(s == NT - 1))
            last.then_inc(S("ranked"), 1)
            degrees(0)
            degrees(1)
            pe.wait_ge(S("gate_ready"), 1)
            for t in range(NT):
                pe.transpose(quads(2, 16)[:, t, :], gate[:, t, :], ident[0:TP, 0:TP]).then_inc(S("gate_turned"), 1)
            for k in range(2 * NT):
                pe.wait_ge(S("hot_ready"), k + 1)
                last = mm(ps[:, 7, 0:MT], row_hot[:, k, :], tile_hot[:, k, :], start=(k == 0), stop=(k == 2 * NT - 1))
            last.then_inc(S("inverted"), 1)

            def moe_turn(j, u, k, first=False):
                pe.wait_ge(S(f"moe_gathered{u}"), k * 16)
                if not first:
                    pe.wait_ge(S("moe_T"), j - 1)
                for q in range(NC2):
                    pe.transpose(ps[:, u % 2, q * 128:(q + 1) * 128], tile_x[u][:, q * 128:(q + 1) * 128], ident[:])\
                        .then_inc(S("moe_turned"), 1)

            def moe_h(j, u, k, first=False):
                pe.wait_ge(S(f"w_loaded{u}"), k * 48)
                pe.wait_ge(S("moe_T"), j + 1)
                if not first:
                    pe.wait_ge(S("moe_relu"), j - 1)
                for m in range(4):
                    for q in range(NC2):
                        last = mm(ps[:, 2 + u % 2, m * SLOT:(m + 1) * SLOT], w1_moe[u][:, q, m * 128:(m + 1) * 128],
                                  tile_xT[u % 2][:, q, :], start=(q == 0), stop=(q == 1))
                last.then_inc(S("moe_h_done"), 1)

            def moe_y(j, u, first=False):
                pe.wait_ge(S("moe_relu"), j + 1)
                if not first:
                    pe.wait_ge(S("moe_y_out"), j - 1)
                for m in range(4):
                    last = mm(ps[:, 4 + u % 2, 0:D], tile_h[u % 2][:, m, :], w2_moe[u][:, m, :],
                              start=(m == 0), stop=(m == 3))
                last.then_inc(S("moe_y_done"), 1)

            moe_turn(0, 0, 1, True)
            pe.wait_ge(S("gate_T_ready"), 1)
            pe.wait_ge(S("deg_read"), 1)
            bias_rows(moe_b2, E0)
            moe_turn(1, 1, 1, True)
            moe_h(0, 0, 1, True)
            moe_turn(2, 2, 1)
            moe_h(1, 1, 1, True)
            pe.wait_ge(S("bias_in"), NT)
            moe_y(0, 0, True)
            for j in range(2, TB):
                moe_turn(j + 1, (j + 1) % TB, 1 + (j + 1) // TB)
                moe_h(j, j, 1)
                moe_y(j - 1, j - 1, j == 2)
            with pe.Fori(1, MT // TB) as g:
                for u in range(TB):
                    after = (u + 1) % TB
                    moe_turn(g * TB + (u + 1), after, g + (1 if after else 2))
                    moe_h(g * TB + u, u, g + 1)
                    moe_y(g * TB + (u - 1), (u - 1) % TB)
            moe_h(MT - 1, 0, MT // TB + 1)
            moe_y(MT - 2, TB - 1)
            moe_y(MT - 1, 0)

            turn("x2", n_R, 0)
            turned("x2")
            pe.wait_ge(S("w_m1_loaded"), 16)
            for m in range(NC2):
                to_T(4 + 2 * m, w_m1, n_T, m * 128).then_inc(S("m1_q_done"), 1)

            def aggregate(l, src_R, m):
                for h in range(2):
                    for s in range(NT):
                        last = mm(ps[:, 2 * m + h, 0:HALF], src_R[:, s, m * 128:(m + 1) * 128],
                                  count[:, s, h * HALF:(h + 1) * HALF], start=(s == 0), stop=(s == NT - 1))
                last.then_inc(S("agg_done"), 1)

            for t in range(NT):
                if t == 4:
                    pe.wait_ge(S("m1_q"), 1)
                to_R(ps[0:TP, t, :], lambda k: n_T[:, k, :], t, lambda k: w_m1[:, k, D:3 * D])\
                    .then_inc(S("m1_kv_done"), 1)

            def graph_rows(l):
                pe.wait_ge(S("agg_out"), 2 * l + 2)
                for t in range(NT):
                    if t == 4:
                        pe.wait_ge(S("g1_h"), l * NT + 1)
                    to_R(ps[0:TP, t % 4, 0:D], lambda k: a_T[:, k, :], t, lambda k: w_g1[:, k, l * D:(l + 1) * D])\
                        .then_inc(S("g1_h_done"), 1)

            pe.wait_ge(S("m1_kv"), NT)
            for q in range(2):
                for t in range(NT):
                    last = mm(ps[:, 5, q * 128:(q + 1) * 128], vs[:, t, q * 128:(q + 1) * 128],
                              vs[:, t, D + q * 128:D + (q + 1) * 128], start=(t == 0), stop=(t == NT - 1))
                last.then_inc(S("m1_at_done"), 1)
            aggregate(0, n_R, 0)
            pe.wait_ge(S("m1_q"), 2)
            pe.wait_ge(S("m1_attn"), 4)
            for q in range(2):
                pe.transpose(ps[:, 6, q * 128:(q + 1) * 128], at_sb[:, q, :], ident[:]).then_inc(S("at_turned"), 1)
            aggregate(0, n_R, 1)
            pe.wait_ge(S("at_T_ready"), 1)
            for t in range(NT):
                if t == 4:
                    pe.wait_ge(S("m1_xf"), 1)
                for q in range(2):
                    last = mm(ps[0:TP, 4 + t % 4, q * 128:(q + 1) * 128], q_T[:, q, t * TP:(t + 1) * TP],
                              at_T[:, q, :], start=True, stop=True)
                last.then_inc(S("m1_xf_done"), 1)
            pe.wait_ge(S("w_g1_loaded"), 16)
            graph_rows(0)
            turn("y1", h_R, 4)
            turned("y1")
            for m in range(HM // 128):
                if m >= 2:
                    pe.wait_ge(S("fc1_gelu"), m - 1)
                to_T(4 + 2 * (m % 2), w_m1, b_T, 3 * D + m * 128).then_inc(S("fc1_done"), 1)
            pe.wait_ge(S("g1_x"), 1)
            for t in range(NT):
                for q in range(NC2):
                    dst = ps[:, q, t * TP:(t + 1) * TP] if t < 4 else ps[:, 2, q * TP:(q + 1) * TP]
                    pe.transpose(dst, y_R[:, t, q * 128:(q + 1) * 128], ident[0:TP, 0:TP]).then_inc(S("rows_turned"), 1)
            turned("g1")
            for m in range(NC2):
                aggregate(1, y_R, m)
            graph_rows(1)
            pe.wait_ge(S("w_fc2_loaded"), 16)
            pe.wait_ge(S("fc1_gelu"), HM // 128)
            for t in range(NT):
                if t == 4:
                    pe.wait_ge(S("g1_h"), 2 * NT - 1)
                to_R(ps[0:TP, 4 + t if t < 4 else 3, 0:D], lambda k: (hid[0][:, k, :] if k < 4 else hid[1][:, k - 4, :]), t,
                     lambda k: w_fc2[:, k, :], HM // 128).then_inc(S("fc2_done"), 1)

            turn("x3", n_R, 0)
            turned("x3")
            for t in range(NT):
                last = to_R(ps[0:TP, 7, t * E1:(t + 1) * E1], lambda k: c_T[:, k, :], t, lambda k: gate_w[:, k, 16:16 + E1])
            last.then_inc(S("logits_done"), 1)

            PARTS = [(0, 0), (1, 0), (0, 1)]

            def ffn_h(e, u, k, first, chunks=range(NC2)):
                pe.wait_ge(S("w_lo"), e * 3 + (k + 1))
                for m in chunks:
                    if k == 1:
                        if m == 0:
                            pe.wait_ge(S("ffn_lo"), e * 4 + 2)
                    elif not first:
                        pe.wait_ge(S("ffn_out"), e * 4 + m - 1)
                    src = x_parts if k == 0 else hid_parts[0]
                    for h in range(2):
                        for n, (a, b, q) in enumerate([(a, b, q) for q in range(NC2) for a, b in PARTS]):
                            at = k * 2 * D + q * D + m * 128
                            last = mm(ps[:, 2 * m + h, 0:HALF], w_parts[u][:, a, at:at + 128],
                                      src[:, b, q, h * HALF:(h + 1) * HALF], start=(n == 0), stop=(n == 5))
                    last.then_inc(S("ffn_h_done"), 1)

            def ffn_y(e, u, first):
                pe.wait_ge(S("w_lo"), e * 3 + 3)
                pe.wait_ge(S("ffn_lo"), e * 4 + 4)
                for t in range(NT):
                    if t % 2 == 0 and not first:
                        pe.wait_ge(S("ffn_acc"), e * NT + min(t + 2, NT) - NT)
                    for n, (a, b, q) in enumerate([(a, b, q) for q in range(NC2) for a, b in PARTS]):
                        at = 4 * D + q * D
                        last = mm(ps[0:TP, 4 + t // 2, (t % 2) * D:(t % 2 + 1) * D],
                                  hid_parts[1][:, a, q, t * TP:(t + 1) * TP], w_parts[u][:, b, at:at + D],
                                  start=(n == 0), stop=(n == 5))
                    if t % 2 or t == NT - 1:
                        last.then_inc(S("ffn_y_done"), 1)

            pe.wait_ge(S("x_lo"), 1)
            ffn_h(0, 0, 0, True, (0,))
            pe.wait_ge(S("gate2_ready"), 1)
            for t in range(NT):
                pe.transpose(quads(4, E1)[:, t, :], gate2[:, t, 0:E1], ident[0:TP, 0:TP]).then_inc(S("gate_turned"), 1)
            ffn_h(0, 0, 0, True, (1,))
            pe.wait_ge(S("gate2_T_ready"), 1)
            bias_rows(moe_bo, E1)
            ffn_h(0, 0, 1, True)
            ffn_h(1, 1, 0, False)
            pe.wait_ge(S("bias_in"), 2 * NT)
            ffn_y(0, 0, True)
            ffn_h(1, 1, 1, False)
            with pe.Fori(1, E1 // 2) as g:
                ffn_h(g * 2, 0, 0, False)
                ffn_y(g * 2 - 1, 1, False)
                ffn_h(g * 2, 0, 1, False)
                ffn_h(g * 2 + 1, 1, 0, False)
                ffn_y(g * 2, 0, False)
                ffn_h(g * 2 + 1, 1, 1, False)
            ffn_y(E1 - 1, 1, False)


def kernel(**inputs):
    import numpy as np
    import concourse.bacc as bacc
    from concourse import mybir as mb
    from concourse.bass_utils import run_bass_kernel_spmd

    a = {k: np.asarray(v) for k, v in inputs.items()}

    def columns(v):
        return np.reshape(v, (-1, 128)).T

    gates = np.zeros((D,), np.float32)
    gates[0:E0] = a["L0_ffn_gate_b"]
    gates[E0:E0 + E1] = a["L1_ffn_br"]
    b_qkv = a["L1_mix_b_qkv"]
    by_name = {
        "mix_ln1_g": a["L0_mix_ln1_g"], "mix_ln1_b": a["L0_mix_ln1_b"], "mix_b2": a["L0_mix_b2"],
        "mix_ln2_g": a["L0_mix_ln2_g"], "mix_ln2_b": a["L0_mix_ln2_b"],
        "moe_gamma": a["L0_ffn_gamma"], "moe_beta": a["L0_ffn_beta"],
        "g1_b0": a["L1_gnn_b0"], "g1_g0": a["L1_gnn_g0"], "g1_beta0": a["L1_gnn_beta0"],
        "g1_b1": a["L1_gnn_b1"], "g1_g1": a["L1_gnn_g1"], "g1_beta1": a["L1_gnn_beta1"],
        "m1_bk": b_qkv[D:2 * D], "m1_bv": b_qkv[2 * D:3 * D],
        "m1_norm_g": a["L1_mix_norm_g"], "m1_norm_b": a["L1_mix_norm_b"], "m1_bfc2": a["L1_mix_b_fc2"],
        "gates": gates,
        "mix_b1": a["L0_mix_b1"], "m1_bq": b_qkv[0:D], "m1_bfc1": a["L1_mix_b_fc1"],
        **{k: a[f"L1_ffn_{k}"] for k in ("b1", "g1", "be1", "m1", "v1", "b2", "g2", "be2", "m2", "v2")},
    }
    nothing = np.zeros((1, D), np.float32)
    bn_g = np.concatenate([a["L0_gnn_bn_gamma"], nothing])
    bn_b = np.concatenate([a["L0_gnn_bn_beta"], nothing])
    arrays = {
        "x": a["x"], "src": a["src"], "dst": a["dst"],
        "rows": np.stack([by_name[k] for k in ROWS]),
        "cols": np.concatenate([columns(by_name[k]) for k, _ in COLS], 1),
        "gw": np.stack([a["L0_gnn_Wq"], a["L0_gnn_Wk"], a["L0_gnn_Wv"], a["L0_gnn_Ws"]], 1),
        "gbias": np.concatenate([a["L0_gnn_bv"], a["L0_gnn_bs"]], 1),
        "gcols": np.concatenate([columns(v[i]) for i in range(GL)
                                 for v in (a["L0_gnn_bq"], a["L0_gnn_bk"], bn_g, bn_b)], 1),
        "w_mix": np.concatenate([a["L0_mix_Wqkv"].T, a["L0_mix_W1"].T, a["L0_mix_W2"].T], 1),
        "w_g1": np.concatenate([a["L1_gnn_W0"].T, a["L1_gnn_W1"].T], 1),
        "w_m1": np.concatenate([a["L1_mix_w_qkv"], a["L1_mix_w_fc1"]], 1),
        "w_fc2": a["L1_mix_w_fc2"],
        "gate_w": np.concatenate([a["L0_ffn_gate_w"], a["L1_ffn_Wr"]], 1),
        "moe_b1": np.transpose(np.reshape(a["L0_ffn_b1"], (E0, F0 // 128, 128)), (0, 2, 1)),
        "moe_w1": a["L0_ffn_w1"], "moe_w2": a["L0_ffn_w2"], "moe_b2": a["L0_ffn_b2"],
        "ffn_w": np.stack([a["L1_ffn_W1"], a["L1_ffn_W2"], a["L1_ffn_Wo"]], 1), "moe_bo": a["L1_ffn_bo"],
    }
    arrays = {f"in_{k}": np.ascontiguousarray(v) for k, v in arrays.items()}
    nc = bacc.Bacc("TRN2", target_bir_lowering=False, num_devices=1)
    A = {k[3:]: nc.dram_tensor(k, v.shape, mb.dt.from_np(v.dtype), kind="ExternalInput").ap() for k, v in arrays.items()}
    out = nc.dram_tensor("out_x", (N, D), mb.dt.float32, kind="ExternalOutput").ap()
    program(nc, A, out)
    r = run_bass_kernel_spmd(nc, [arrays], core_ids=[0])
    return r.results[0]["out_x"]
```
